# Optimizing a Trainium2 kernel written in Bass

```python
import numpy as np
import jax
import jax.numpy as jnp

def _softmax(x, axis=-1):
    return jax.nn.softmax(x, axis=axis)

def _gelu(x):
    return jax.nn.gelu(x, approximate=True)

def _silu(x):
    return jax.nn.silu(x)

def _sigmoid(x):
    return jax.nn.sigmoid(x)

def _layernorm(x, axis=-1, eps=1e-05):
    m = jnp.mean(x, axis=axis, keepdims=True)
    v = jnp.var(x, axis=axis, keepdims=True)
    return (x - m) / jnp.sqrt(v + eps)

def _scatter_add(tgt, idx, src, axis=0):
    return tgt.at[idx].add(src)

def _segment_sum(src, seg, n):
    return jax.ops.segment_sum(src, seg, n)
kernel_name = 'mk_hybrid_d2_jaxref_r4_50afb2'

def setup_inputs(seed: int=0):
    np.random.seed(seed)
    _w = jnp.asarray

    def _L0_attn_a_setup():
        import jax, jax.numpy as jnp
        import numpy as np
        HIDDEN = 256
        HEADS = 16
        key = jax.random.key(seed)
        ks = jax.random.split(key, 7)
        s = 1.0 / np.sqrt(HIDDEN)
        return {'x': jax.random.normal(ks[0], (4, 1024, HIDDEN), dtype=jnp.float32), 'Wq': jax.random.uniform(ks[1], (HIDDEN, HIDDEN), jnp.float32, -s, s), 'bq': jax.random.uniform(ks[2], (HIDDEN,), jnp.float32, -s, s), 'Wk': jax.random.uniform(ks[3], (HIDDEN, HIDDEN), jnp.float32, -s, s), 'bk': jax.random.uniform(ks[4], (HIDDEN,), jnp.float32, -s, s), 'Wv': jax.random.uniform(ks[5], (HIDDEN, HIDDEN), jnp.float32, -s, s), 'bv': jax.random.uniform(ks[6], (HIDDEN,), jnp.float32, -s, s)}
    _L0_attn_a_in = _L0_attn_a_setup()

    def _L0_attn_b_setup():
        import jax, jax.numpy as jnp
        import numpy as np
        HID = 256
        NH = 16
        NKV = 4
        HD = 64
        C = 64
        RATIO = 0.125
        KS = 7

        def _block_causal_attention(x, qw, kw, vw, ow, k):
            B, nc, _, D = x.shape
            T = nc * k
            xf = x.reshape(B, T, D)
            q = (xf @ qw.T).reshape(B, T, NH, HD).transpose(0, 2, 1, 3)
            kk = (xf @ kw.T).reshape(B, T, NKV, HD).transpose(0, 2, 1, 3)
            v = (xf @ vw.T).reshape(B, T, NKV, HD).transpose(0, 2, 1, 3)
            rep = NH // NKV
            kk = jnp.repeat(kk, rep, axis=1)
            v = jnp.repeat(v, rep, axis=1)
            chunk_ids = jnp.arange(T) // k
            mask = chunk_ids[:, None] >= chunk_ids[None, :]
            scores = jnp.einsum('bhqd,bhkd->bhqk', q, kk) / np.float32(np.sqrt(HD))
            scores = jnp.where(mask[None, None], scores, jnp.finfo(scores.dtype).min)
            p = jax.nn.softmax(scores, axis=-1)
            o = jnp.einsum('bhqk,bhkd->bhqd', p, v)
            o = o.transpose(0, 2, 1, 3).reshape(B, T, NH * HD)
            return (o @ ow.T).reshape(B, nc, k, D)

        def _causal_conv(x, dw, pw):
            B, nc, L, D = x.shape
            xc = x.reshape(B * nc, L, D).transpose(0, 2, 1)
            xp = jnp.pad(xc, ((0, 0), (0, 0), (KS - 1, 0)))
            y = jax.lax.conv_general_dilated(xp, dw, window_strides=(1,), padding='VALID', dimension_numbers=('NCH', 'OIH', 'NCH'), feature_group_count=D)
            y = jax.nn.gelu(y, approximate=False)
            y = jnp.einsum('ncl,oc->nol', y, pw)
            return y.transpose(0, 2, 1).reshape(B, nc, L, D)

        def _forward(hidden_states, q_w, k_w, v_w, o_w, dw_r, pw_r, dw_i, pw_i, gate_w, alpha_raw):
            B, N, D = hidden_states.shape
            pad_len = -N % C
            x = jnp.pad(hidden_states, ((0, 0), (0, pad_len), (0, 0))) if pad_len else hidden_states
            nc = x.shape[1] // C
            chunks = x.reshape(B, nc, C, D)
            Xh = jnp.fft.rfft(chunks.astype(jnp.float32), axis=2)
            M = Xh.shape[2]
            k = max(1, int(M * RATIO))
            X_low, X_high = (Xh[:, :, :k, :], Xh[:, :, k:, :])
            A_r = _block_causal_attention(X_low.real, q_w, k_w, v_w, o_w, k)
            A_i = _block_causal_attention(X_low.imag, q_w, k_w, v_w, o_w, k)
            A_low = jax.lax.complex(A_r, A_i)
            H_r = _causal_conv(X_high.real, dw_r, pw_r)
            H_i = _causal_conv(X_high.imag, dw_i, pw_i)
            g = jax.nn.sigmoid(chunks.mean(axis=2) @ gate_w.T)[:, :, None, :]
            A_high = jax.lax.complex(H_r * g, H_i * g) + X_high
            alpha = jax.nn.sigmoid(alpha_raw)
            A_low_fused = alpha * A_low + (1.0 - alpha) * X_low
            Y_hat = jnp.concatenate([A_low_fused, A_high], axis=2)
            Y = jnp.fft.irfft(Y_hat, n=C, axis=2)
            return Y.reshape(B, -1, D)[:, :N, :].astype(hidden_states.dtype)
        key = jax.random.key(seed)
        ks = jax.random.split(key, 11)
        B, N = (4, 1024)
        s = 0.02
        return {'hidden_states': jax.random.normal(ks[0], (B, N, HID), jnp.float32), 'q_w': jax.random.normal(ks[1], (NH * HD, HID), jnp.float32) * s, 'k_w': jax.random.normal(ks[2], (NKV * HD, HID), jnp.float32) * s, 'v_w': jax.random.normal(ks[3], (NKV * HD, HID), jnp.float32) * s, 'o_w': jax.random.normal(ks[4], (HID, NH * HD), jnp.float32) * s, 'dw_r': jax.random.normal(ks[5], (HID, 1, KS), jnp.float32) * 0.3, 'pw_r': jax.random.normal(ks[6], (HID, HID), jnp.float32) * s, 'dw_i': jax.random.normal(ks[7], (HID, 1, KS), jnp.float32) * 0.3, 'pw_i': jax.random.normal(ks[8], (HID, HID), jnp.float32) * s, 'gate_w': jax.random.normal(ks[9], (HID, HID), jnp.float32) * s, 'alpha_raw': jnp.zeros((1,), jnp.float32)}
    _L0_attn_b_in = _L0_attn_b_setup()

    def _L0_ffn_setup():
        import jax, jax.numpy as jnp
        import numpy as np
        B, S, H, E, K, F = (4, 512, 256, 8, 128, 1024)
        key = jax.random.key(seed)
        k0, k1, k2, k3 = jax.random.split(key, 4)
        sc = lambda d: 1.0 / np.sqrt(d).astype(np.float32)
        return {'x': jax.random.normal(k0, (B, S, H), jnp.float32), 'Wg': jax.random.normal(k1, (E, H), jnp.float32) * sc(H), 'W1': jax.random.normal(k2, (E, H, F), jnp.float32) * sc(H), 'b1': jnp.zeros((E, F), jnp.float32), 'W2': jax.random.normal(k3, (E, F, H), jnp.float32) * sc(F), 'b2': jnp.zeros((E, H), jnp.float32)}
    _L0_ffn_in = _L0_ffn_setup()

    def _L1_attn_a_setup():
        import jax, jax.numpy as jnp
        import numpy as np
        B, T, D = (4, 256, 256)
        H, DK, DV = (16, 32, 32)
        GAMMA = 0.99

        def _xavier(key, shape, gain=0.1):
            fan_in, fan_out = shape
            lim = gain * jnp.sqrt(6.0 / (fan_in + fan_out))
            return jax.random.uniform(key, shape, jnp.float32, -lim, lim)

        def _hla_forward(x, Wq, Wk, Wv, Wo):
            Bs, Ts, _ = x.shape
            q = (x @ Wq).reshape(Bs, Ts, H, DK).transpose(1, 0, 2, 3)
            k = (x @ Wk).reshape(Bs, Ts, H, DK).transpose(1, 0, 2, 3)
            v = (x @ Wv).reshape(Bs, Ts, H, DV).transpose(1, 0, 2, 3)
            S_K0 = jnp.zeros((Bs, H, DK, DK), x.dtype)
            C_QV0 = jnp.zeros((Bs, H, DK, DV), x.dtype)
            G0 = jnp.zeros((Bs, H, DK, DV), x.dtype)

            def step(carry, qkv):
                S_K, C_QV, G = carry
                q_t, k_t, v_t = qkv
                C_prev = GAMMA * C_QV
                k_C = jnp.einsum('bhk,bhkv->bhv', k_t, C_prev)
                G = GAMMA * G + k_t[..., :, None] * k_C[..., None, :]
                S_K = GAMMA * S_K + k_t[..., :, None] * k_t[..., None, :]
                C_QV = C_prev + q_t[..., :, None] * v_t[..., None, :]
                S_C = jnp.einsum('bhij,bhjv->bhiv', S_K, C_QV)
                o_t = jnp.einsum('bhk,bhkv->bhv', q_t, S_C - G)
                return ((S_K, C_QV, G), o_t)
            _, outs = jax.lax.scan(step, (S_K0, C_QV0, G0), (q, k, v))
            out = outs.transpose(1, 0, 2, 3).reshape(Bs, Ts, H * DV)
            return out @ Wo
        key = jax.random.key(seed)
        kx, kq, kk, kv, ko = jax.random.split(key, 5)
        return {'x': jax.random.normal(kx, (B, T, D), jnp.float32), 'Wq': _xavier(kq, (D, H * DK)), 'Wk': _xavier(kk, (D, H * DK)), 'Wv': _xavier(kv, (D, H * DV)), 'Wo': _xavier(ko, (H * DV, D))}
    _L1_attn_a_in = _L1_attn_a_setup()

    def _L1_attn_b_setup():
        import jax, jax.numpy as jnp
        import numpy as np
        H = 16
        WIN = 128
        key = jax.random.key(seed)
        ks = jax.random.split(key, 4)
        B, S, D = (1, 1024, 256)
        s = 1.0 / np.sqrt(D)
        x = jax.random.normal(ks[0], (B, S, D), jnp.float32)
        Wqkv = jax.random.normal(ks[1], (3 * D, D), jnp.float32) * s
        bqkv = jnp.zeros((3 * D,), jnp.float32)
        Wout = jax.random.normal(ks[2], (D, D), jnp.float32) * s
        bout = jnp.zeros((D,), jnp.float32)
        return {'x': x, 'Wqkv': Wqkv, 'bqkv': bqkv, 'Wout': Wout, 'bout': bout}
    _L1_attn_b_in = _L1_attn_b_setup()

    def _L1_ffn_setup():
        import jax, jax.numpy as jnp
        import numpy as np
        D_MODEL = 256
        key = jax.random.key(seed)
        k_x, k_w, k_a1, k_a2 = jax.random.split(key, 4)
        x = jax.random.normal(k_x, (4, 512, D_MODEL), dtype=jnp.float32)
        weight = jax.random.normal(k_w, (D_MODEL, D_MODEL), dtype=jnp.float32) * 0.02
        aux_weight1 = jax.random.normal(k_a1, (D_MODEL, D_MODEL), dtype=jnp.float32) * 0.02
        aux_weight2 = jax.random.normal(k_a2, (D_MODEL, D_MODEL), dtype=jnp.float32) * 0.02
        bias = jnp.zeros((D_MODEL,), dtype=jnp.float32)
        return {'x': x, 'weight': weight, 'aux_weight1': aux_weight1, 'aux_weight2': aux_weight2, 'bias': bias}
    _L1_ffn_in = _L1_ffn_setup()
    _d = {'L0_attn_a_x': _L0_attn_a_in['x'], 'L0_attn_a_Wq': _L0_attn_a_in['Wq'], 'L0_attn_a_bq': _L0_attn_a_in['bq'], 'L0_attn_a_Wk': _L0_attn_a_in['Wk'], 'L0_attn_a_bk': _L0_attn_a_in['bk'], 'L0_attn_a_Wv': _L0_attn_a_in['Wv'], 'L0_attn_a_bv': _L0_attn_a_in['bv'], 'L0_attn_b_q_w': _L0_attn_b_in['q_w'], 'L0_attn_b_k_w': _L0_attn_b_in['k_w'], 'L0_attn_b_v_w': _L0_attn_b_in['v_w'], 'L0_attn_b_o_w': _L0_attn_b_in['o_w'], 'L0_attn_b_dw_r': _L0_attn_b_in['dw_r'], 'L0_attn_b_pw_r': _L0_attn_b_in['pw_r'], 'L0_attn_b_dw_i': _L0_attn_b_in['dw_i'], 'L0_attn_b_pw_i': _L0_attn_b_in['pw_i'], 'L0_attn_b_gate_w': _L0_attn_b_in['gate_w'], 'L0_attn_b_alpha_raw': _L0_attn_b_in['alpha_raw'], 'L0_ffn_Wg': _L0_ffn_in['Wg'], 'L0_ffn_W1': _L0_ffn_in['W1'], 'L0_ffn_b1': _L0_ffn_in['b1'], 'L0_ffn_W2': _L0_ffn_in['W2'], 'L0_ffn_b2': _L0_ffn_in['b2'], 'L1_attn_a_Wq': _L1_attn_a_in['Wq'], 'L1_attn_a_Wk': _L1_attn_a_in['Wk'], 'L1_attn_a_Wv': _L1_attn_a_in['Wv'], 'L1_attn_a_Wo': _L1_attn_a_in['Wo'], 'L1_attn_b_Wqkv': _L1_attn_b_in['Wqkv'], 'L1_attn_b_bqkv': _L1_attn_b_in['bqkv'], 'L1_attn_b_Wout': _L1_attn_b_in['Wout'], 'L1_attn_b_bout': _L1_attn_b_in['bout'], 'L1_ffn_weight': _L1_ffn_in['weight'], 'L1_ffn_aux_weight1': _L1_ffn_in['aux_weight1'], 'L1_ffn_aux_weight2': _L1_ffn_in['aux_weight2'], 'L1_ffn_bias': _L1_ffn_in['bias']}
    _x0 = _d['L0_attn_a_x']
    _d['L0_attn_a_x'] = jax.random.normal(jax.random.fold_in(jax.random.key(seed), 1), (8, 1024, 256), dtype=_x0.dtype)
    del _x0
    return _d

def reference(L0_attn_a_x, L0_attn_a_Wq, L0_attn_a_bq, L0_attn_a_Wk, L0_attn_a_bk, L0_attn_a_Wv, L0_attn_a_bv, L0_attn_b_q_w, L0_attn_b_k_w, L0_attn_b_v_w, L0_attn_b_o_w, L0_attn_b_dw_r, L0_attn_b_pw_r, L0_attn_b_dw_i, L0_attn_b_pw_i, L0_attn_b_gate_w, L0_attn_b_alpha_raw, L0_ffn_Wg, L0_ffn_W1, L0_ffn_b1, L0_ffn_W2, L0_ffn_b2, L1_attn_a_Wq, L1_attn_a_Wk, L1_attn_a_Wv, L1_attn_a_Wo, L1_attn_b_Wqkv, L1_attn_b_bqkv, L1_attn_b_Wout, L1_attn_b_bout, L1_ffn_weight, L1_ffn_aux_weight1, L1_ffn_aux_weight2, L1_ffn_bias):

    def _L0_attn_a_ref(x, Wq, bq, Wk, bk, Wv, bv):
        import jax, jax.numpy as jnp
        import numpy as np
        HIDDEN = 256
        HEADS = 16
        batch, len_, hidden = x.shape
        xh = x.reshape(batch, HEADS, len_ // HEADS, hidden)
        q = jnp.einsum('bhcd,ed->bhce', xh, Wq) + bq
        k = jnp.einsum('bhcd,ed->bhce', xh, Wk) + bk
        v = jnp.einsum('bhcd,ed->bhce', xh, Wv) + bv
        score = jax.nn.softmax(jnp.einsum('bhce,bhke->bhck', q, k), axis=-1)
        out = jnp.einsum('bhck,bhke->bhce', score, v)
        return out.reshape(batch, len_, hidden)

    def _L0_attn_b_ref(hidden_states, q_w, k_w, v_w, o_w, dw_r, pw_r, dw_i, pw_i, gate_w, alpha_raw):
        import jax, jax.numpy as jnp
        import numpy as np
        HID = 256
        NH = 16
        NKV = 4
        HD = 64
        C = 64
        RATIO = 0.125
        KS = 7

        def _block_causal_attention(x, qw, kw, vw, ow, k):
            B, nc, _, D = x.shape
            T = nc * k
            xf = x.reshape(B, T, D)
            q = (xf @ qw.T).reshape(B, T, NH, HD).transpose(0, 2, 1, 3)
            kk = (xf @ kw.T).reshape(B, T, NKV, HD).transpose(0, 2, 1, 3)
            v = (xf @ vw.T).reshape(B, T, NKV, HD).transpose(0, 2, 1, 3)
            rep = NH // NKV
            kk = jnp.repeat(kk, rep, axis=1)
            v = jnp.repeat(v, rep, axis=1)
            chunk_ids = jnp.arange(T) // k
            mask = chunk_ids[:, None] >= chunk_ids[None, :]
            scores = jnp.einsum('bhqd,bhkd->bhqk', q, kk) / np.float32(np.sqrt(HD))
            scores = jnp.where(mask[None, None], scores, jnp.finfo(scores.dtype).min)
            p = jax.nn.softmax(scores, axis=-1)
            o = jnp.einsum('bhqk,bhkd->bhqd', p, v)
            o = o.transpose(0, 2, 1, 3).reshape(B, T, NH * HD)
            return (o @ ow.T).reshape(B, nc, k, D)

        def _causal_conv(x, dw, pw):
            B, nc, L, D = x.shape
            xc = x.reshape(B * nc, L, D).transpose(0, 2, 1)
            xp = jnp.pad(xc, ((0, 0), (0, 0), (KS - 1, 0)))
            y = jax.lax.conv_general_dilated(xp, dw, window_strides=(1,), padding='VALID', dimension_numbers=('NCH', 'OIH', 'NCH'), feature_group_count=D)
            y = jax.nn.gelu(y, approximate=False)
            y = jnp.einsum('ncl,oc->nol', y, pw)
            return y.transpose(0, 2, 1).reshape(B, nc, L, D)

        def _forward(hidden_states, q_w, k_w, v_w, o_w, dw_r, pw_r, dw_i, pw_i, gate_w, alpha_raw):
            B, N, D = hidden_states.shape
            pad_len = -N % C
            x = jnp.pad(hidden_states, ((0, 0), (0, pad_len), (0, 0))) if pad_len else hidden_states
            nc = x.shape[1] // C
            chunks = x.reshape(B, nc, C, D)
            Xh = jnp.fft.rfft(chunks.astype(jnp.float32), axis=2)
            M = Xh.shape[2]
            k = max(1, int(M * RATIO))
            X_low, X_high = (Xh[:, :, :k, :], Xh[:, :, k:, :])
            A_r = _block_causal_attention(X_low.real, q_w, k_w, v_w, o_w, k)
            A_i = _block_causal_attention(X_low.imag, q_w, k_w, v_w, o_w, k)
            A_low = jax.lax.complex(A_r, A_i)
            H_r = _causal_conv(X_high.real, dw_r, pw_r)
            H_i = _causal_conv(X_high.imag, dw_i, pw_i)
            g = jax.nn.sigmoid(chunks.mean(axis=2) @ gate_w.T)[:, :, None, :]
            A_high = jax.lax.complex(H_r * g, H_i * g) + X_high
            alpha = jax.nn.sigmoid(alpha_raw)
            A_low_fused = alpha * A_low + (1.0 - alpha) * X_low
            Y_hat = jnp.concatenate([A_low_fused, A_high], axis=2)
            Y = jnp.fft.irfft(Y_hat, n=C, axis=2)
            return Y.reshape(B, -1, D)[:, :N, :].astype(hidden_states.dtype)
        return _forward(hidden_states, q_w, k_w, v_w, o_w, dw_r, pw_r, dw_i, pw_i, gate_w, alpha_raw)

    def _L0_ffn_ref(x, Wg, W1, b1, W2, b2):
        import jax, jax.numpy as jnp
        import numpy as np
        B, S, H, E, K, F = (4, 512, 256, 8, 128, 1024)
        b, s, h = x.shape
        logits = jnp.einsum('bsh,eh->bse', x, Wg)
        Sm = jnp.swapaxes(jax.nn.softmax(logits, axis=-1), 1, 2)
        G, I = jax.lax.top_k(Sm, K)
        ex = jnp.take_along_axis(x[:, None, :, :], I[..., None], axis=2)
        h1 = jax.nn.gelu(jnp.einsum('bekh,ehf->bekf', ex, W1) + b1[None, :, None, :])
        out = jnp.einsum('bekf,efh->bekh', h1, W2) + b2[None, :, None, :]
        out = G[..., None] * out
        new_x = jnp.zeros_like(x).at[jnp.arange(b)[:, None, None], I].add(out)
        return new_x

    def _L1_attn_a_ref(x, Wq, Wk, Wv, Wo):
        import jax, jax.numpy as jnp
        import numpy as np
        B, T, D = (4, 256, 256)
        H, DK, DV = (16, 32, 32)
        GAMMA = 0.99

        def _xavier(key, shape, gain=0.1):
            fan_in, fan_out = shape
            lim = gain * jnp.sqrt(6.0 / (fan_in + fan_out))
            return jax.random.uniform(key, shape, jnp.float32, -lim, lim)

        def _hla_forward(x, Wq, Wk, Wv, Wo):
            Bs, Ts, _ = x.shape
            q = (x @ Wq).reshape(Bs, Ts, H, DK).transpose(1, 0, 2, 3)
            k = (x @ Wk).reshape(Bs, Ts, H, DK).transpose(1, 0, 2, 3)
            v = (x @ Wv).reshape(Bs, Ts, H, DV).transpose(1, 0, 2, 3)
            S_K0 = jnp.zeros((Bs, H, DK, DK), x.dtype)
            C_QV0 = jnp.zeros((Bs, H, DK, DV), x.dtype)
            G0 = jnp.zeros((Bs, H, DK, DV), x.dtype)

            def step(carry, qkv):
                S_K, C_QV, G = carry
                q_t, k_t, v_t = qkv
                C_prev = GAMMA * C_QV
                k_C = jnp.einsum('bhk,bhkv->bhv', k_t, C_prev)
                G = GAMMA * G + k_t[..., :, None] * k_C[..., None, :]
                S_K = GAMMA * S_K + k_t[..., :, None] * k_t[..., None, :]
                C_QV = C_prev + q_t[..., :, None] * v_t[..., None, :]
                S_C = jnp.einsum('bhij,bhjv->bhiv', S_K, C_QV)
                o_t = jnp.einsum('bhk,bhkv->bhv', q_t, S_C - G)
                return ((S_K, C_QV, G), o_t)
            _, outs = jax.lax.scan(step, (S_K0, C_QV0, G0), (q, k, v))
            out = outs.transpose(1, 0, 2, 3).reshape(Bs, Ts, H * DV)
            return out @ Wo
        return _hla_forward(x, Wq, Wk, Wv, Wo)

    def _L1_attn_b_ref(x, Wqkv, bqkv, Wout, bout):
        import jax, jax.numpy as jnp
        import numpy as np
        H = 16
        WIN = 128
        B, S, D = x.shape
        d = D // H
        pads = WIN // 2
        C = WIN
        N = S // C
        L = C + WIN - 1
        qkv = (x @ Wqkv.T + bqkv).reshape(B, S, 3, H, d).transpose(2, 0, 3, 1, 4)
        q, k, v = (qkv[0], qkv[1], qkv[2])
        kp = jnp.pad(k, ((0, 0), (0, 0), (pads, pads), (0, 0)))
        vp = jnp.pad(v, ((0, 0), (0, 0), (pads, pads), (0, 0)))
        idx = jnp.arange(N)[:, None] * C + jnp.arange(L)[None, :]
        kb = kp[:, :, idx, :]
        vb = vp[:, :, idx, :]
        qc = q.reshape(B, H, N, C, d)
        scores = jnp.einsum('bhncd,bhnld->bhncl', qc, kb) / np.sqrt(d).astype(np.float32)
        c = jnp.arange(C)[:, None]
        j = jnp.arange(L)[None, :]
        band = (j >= c) & (j < c + WIN)
        scores = jnp.where(band, scores, -jnp.inf)
        attn = jax.nn.softmax(scores, axis=-1)
        o = jnp.einsum('bhncl,bhnld->bhncd', attn, vb).reshape(B, H, S, d)
        o = o.transpose(0, 2, 1, 3).reshape(B, S, D)
        return o @ Wout.T + bout

    def _L1_ffn_ref(x, weight, aux_weight1, aux_weight2, bias):
        import jax, jax.numpy as jnp
        import numpy as np
        D_MODEL = 256
        h = jnp.einsum('btc,cd->btd', x, weight)
        h = jnp.einsum('btc,cd->btd', h, aux_weight1)
        h = jnp.einsum('btc,cd->btd', h, aux_weight2)
        return jnp.tanh(h + bias)
    x = L0_attn_a_x
    x = x + _L0_attn_a_ref(_layernorm(x, axis=-1), L0_attn_a_Wq, L0_attn_a_bq, L0_attn_a_Wk, L0_attn_a_bk, L0_attn_a_Wv, L0_attn_a_bv)
    x = x + _L0_ffn_ref(_layernorm(x, axis=-1), L0_ffn_Wg, L0_ffn_W1, L0_ffn_b1, L0_ffn_W2, L0_ffn_b2)
    x = x + _L0_attn_b_ref(_layernorm(x, axis=-1), L0_attn_b_q_w, L0_attn_b_k_w, L0_attn_b_v_w, L0_attn_b_o_w, L0_attn_b_dw_r, L0_attn_b_pw_r, L0_attn_b_dw_i, L0_attn_b_pw_i, L0_attn_b_gate_w, L0_attn_b_alpha_raw)
    x = x + _L0_ffn_ref(_layernorm(x, axis=-1), L0_ffn_Wg, L0_ffn_W1, L0_ffn_b1, L0_ffn_W2, L0_ffn_b2)
    x = x + _L1_attn_a_ref(_layernorm(x, axis=-1), L1_attn_a_Wq, L1_attn_a_Wk, L1_attn_a_Wv, L1_attn_a_Wo)
    x = x + _L1_ffn_ref(_layernorm(x, axis=-1), L1_ffn_weight, L1_ffn_aux_weight1, L1_ffn_aux_weight2, L1_ffn_bias)
    x = x + _L1_attn_b_ref(_layernorm(x, axis=-1), L1_attn_b_Wqkv, L1_attn_b_bqkv, L1_attn_b_Wout, L1_attn_b_bout)
    x = x + _L1_ffn_ref(_layernorm(x, axis=-1), L1_ffn_weight, L1_ffn_aux_weight1, L1_ffn_aux_weight2, L1_ffn_bias)
    return x

_drawn_inputs = setup_inputs


def setup_inputs(seed=0):
    import zlib

    import numpy as np

    out = dict(_drawn_inputs(seed))
    spreads = {'L0_ffn_b1': (0.0, 0.1),
     'L0_ffn_b2': (0.0, 0.1),
     'L1_attn_b_bqkv': (0.0, 0.8),
     'L1_attn_b_bout': (0.0, 0.8),
     'L1_ffn_bias': (0.0, 0.8)}
    factors = {'L0_attn_a_bk': 64.0,
     'L0_attn_b_q_w': 3.386,
     'L0_attn_b_k_w': 3.331,
     'L0_attn_b_v_w': 3.08,
     'L0_attn_b_o_w': 3.116,
     'L0_attn_b_gate_w': 32.371,
     'L1_attn_a_Wq': 8.0,
     'L1_attn_a_Wk': 8.0,
     'L1_attn_a_Wv': 8.0,
     'L1_attn_a_Wo': 8.0,
     'L1_attn_b_Wqkv': 8.0,
     'L1_attn_b_Wout': 8.0,
     'L1_ffn_weight': 8.0,
     'L1_ffn_aux_weight1': 8.0,
     'L1_ffn_aux_weight2': 8.0}
    for name, (base, spread) in spreads.items():
        noise = np.random.default_rng([zlib.crc32(name.encode()), seed]).standard_normal(out[name].shape)
        drawn = base * np.exp(spread * noise) if base else spread * noise
        out[name] = jnp.asarray(drawn.astype(out[name].dtype))
    for name, factor in factors.items():
        out[name] = (out[name] * factor).astype(out[name].dtype)
    return out
```

```python
from contextlib import ExitStack

import numpy as np

import concourse.bass as bass
from concourse import mybir

P = 128
F32 = mybir.dt.float32
BF16 = mybir.dt.bfloat16
F16 = mybir.dt.float16
U32 = mybir.dt.uint32
I32 = mybir.dt.int32
ALU = mybir.AluOpType
ACT = mybir.ActivationFunctionType
AX_X = mybir.AxisListType.X

BATCH, SEQ, HID = 8, 1024, 256
HC = HID // P
TB = SEQ // P
NT = BATCH * TB
EPS = 1e-5


def past(index, least):
    return not isinstance(index, int) or index >= least


def skewed(eng, count, phases, unroll=2):
    latest = max(delay for delay, _ in phases)

    def step(at, slot):
        for delay, run in phases:
            index = at - delay
            if isinstance(at, int) and not 0 <= index < count:
                continue
            run(index, (slot - delay) % unroll)

    first = latest + unroll
    first += -first % unroll
    blocks = (count - first) // unroll
    if blocks < 2:
        first, blocks = 0, 0
    for at in range(first):
        step(at, at % unroll)
    if blocks:
        with eng.Fori(first, first + (blocks - 1) * unroll + 1, unroll) as at:
            for u in range(unroll):
                step(at + u, u)
    for at in range(first + blocks * unroll, count + latest):
        step(at, at % unroll)


class Chain:

    def __init__(self, eng, sem):
        self.eng, self.sem, self.n = eng, sem, 0

    def then(self, ins):
        ins.then_inc(self.sem, 1)
        self.n += 1
        self.eng.wait_ge(self.sem, self.n)


def layernorm_scales(nc, dve, act_side, R, step, var_ready, std_ready):
    raw, mean, var, rstd, shift, diff = R.raw, R.mean, R.var, R.rstd, R.shift, R.diff
    c = Chain(dve, step)
    c.then(nc.vector.tensor_tensor(mean[:], raw[:, :, 1], raw[:, :, 4], ALU.add))
    c.then(nc.vector.tensor_tensor(diff[:], raw[:, :, 1], raw[:, :, 4], ALU.subtract))
    c.then(nc.vector.tensor_tensor(var[:], raw[:, :, 2], raw[:, :, 5], ALU.add))
    c.then(nc.vector.tensor_tensor(diff[:], diff[:], diff[:], ALU.mult))
    c.then(nc.vector.tensor_scalar(diff[:], diff[:], 0.25, EPS, ALU.mult, ALU.add))
    c.then(nc.vector.scalar_tensor_tensor(out=var[:], in0=var[:], scalar=1.0 / HID, in1=diff[:],
                                          op0=ALU.mult, op1=ALU.add))
    nc.vector.tensor_scalar(mean[:], mean[:], -0.5, None, ALU.mult).then_inc(var_ready, 1)
    dve.wait_ge(std_ready, 1)
    c.then(nc.vector.reciprocal(rstd[:], var[:]))
    c.then(nc.vector.tensor_tensor(shift[:], mean[:], rstd[:], ALU.mult))


def std_of_var(nc, act, R, var_ready, std_ready):
    act.wait_ge(var_ready, 1)
    nc.scalar.activation(R.var[:], R.var[:], ACT.Sqrt).then_inc(std_ready, 1)


class Stage:

    def __init__(self, nc, tag):
        self.nc, self.tag, self.ctx, self.sems = nc, tag, ExitStack(), []

    def __enter__(self):
        return self

    def sb(self, name, shape, dt=F32):
        return self.ctx.enter_context(self.nc.sbuf_tensor(f"{self.tag}_{name}", shape, dt))

    def ps(self, name, shape=(P, 512), dt=F32):
        return self.ctx.enter_context(self.nc.psum_tensor(f"{self.tag}_{name}", list(shape), dt))

    def sem(self, name):
        self.sems.append(self.ctx.enter_context(self.nc.semaphore(f"{self.tag}_{name}")))
        return self.sems[-1]

    def __exit__(self, *error):
        if not error[0] and self.sems:
            with self.nc.Block() as block:
                @block.gpsimd
                def _(pool):
                    for s in self.sems:
                        pool.sem_clear(s)
        return self.ctx.__exit__(*error)


def reload_x(nc, R, tag, source):
    with Stage(nc, tag) as st:
        loaded = [st.sem(f"loaded{b}") for b in range(BATCH)]
        with nc.Block() as block:
            @block.sync
            def _(sp):
                for b in range(BATCH):
                    sp.dma_start(R.X[:, b * TB:(b + 1) * TB, :],
                                 source[b * SEQ:(b + 1) * SEQ, :].rearrange("(j p) d -> p j d", p=P)).then_inc(loaded[b], 16)

            @block.vector
            def _(dve):
                for b in range(BATCH):
                    dve.wait_ge(loaded[b], 16)
                    for j in range(TB):
                        nc.vector.bn_stats(R.raw[:, b * TB + j, :], R.X[:, b * TB + j, :])


def store_x(nc, R, out, sem):
    stored = sem("store_x_stored")
    with nc.Block() as block:
        @block.sync
        def _(sp):
            for b in range(BATCH):
                sp.dma_start(out[b].rearrange("(j p) d -> p j d", p=P),
                             R.X[:, b * TB:(b + 1) * TB, :]).then_inc(stored, 16)
            sp.wait_ge(stored, 16 * BATCH)


def row_of(tensor, i):
    return tensor[:, bass.ds(i, 1), :].rearrange("p a b -> p (a b)")


def tanh_ffn(nc, R, tag, sem_, weight, aux1, aux2, bias):
    def sem(name):
        return sem_(f"{tag}_{name}")

    with ExitStack() as ctx:
        def sb(name, shape, dt=F32):
            return ctx.enter_context(nc.sbuf_tensor(f"{tag}_{name}", shape, dt))

        def ps(name, shape, dt=F32):
            return ctx.enter_context(nc.psum_tensor(f"{tag}_{name}", shape, dt))

        w = sb("w", [P, 3, HC, HID])
        wT = sb("wT", [P, HC, HID])
        w01T = sb("w01T", [P, HC, HID])
        wc = sb("wc", [P, HC, HID])
        bias_all = sb("bias_all", [P, HID])
        xn = sb("xn", [P, 2, HID])
        xnT = sb("xnT", [P, 2, HC, P])
        pre = sb("pre", [P, 2, HID])
        th = sb("th", [P, 2, HID])
        psT = [ps(f"psT{i}", [P, 512]) for i in range(2)]
        psY = [ps(f"psY{i}", [P, 512]) for i in range(2)]
        psW = ps("psW", [P, HC, HID])

        loaded, wstep, wcopied = sem("loaded"), sem("wstep"), sem("wcopied")
        step, var_ready, std_ready = sem("step"), sem("var_ready"), sem("std_ready")
        scales_ready = sem("scales_ready")
        xn_ready, psT_ready, xnT_ready, psY_ready = sem("xn_ready"), sem("psT_ready"), sem("xnT_ready"), sem("psY_ready")
        pre_ready, th_ready, x_ready, stats_done = sem("pre_ready"), sem("th_ready"), sem("x_ready"), sem("stats_done")

        with nc.Block() as block:
            @block.sync
            def _(sp):
                for n, src in enumerate((weight, aux1, aux2)):
                    sp.dma_start(w[:, n], src.rearrange("(c p) d -> p c d", p=P)).then_inc(loaded, 16)
                sp.dma_start(bias_all[:], bias.rearrange("(a d) -> a d", a=1).broadcast_to([P, HID])).then_inc(loaded, 16)

            @block.tensor
            def _(pe):
                pe.wait_ge(loaded, 64)
                for c in range(HC):
                    for h in range(HC):
                        last = nc.tensor.transpose(psW[:, h, c * P:(c + 1) * P], w[:, 0, c, h * P:(h + 1) * P], R.ident[:])
                last.then_inc(wstep, 1)
                for m, (lhs, rhs) in enumerate(((1, wT), (2, w01T))):
                    pe.wait_ge(wcopied, m + 1)
                    for o in range(HC):
                        for c in range(HC):
                            if m == 0:
                                a, b = w[:, 1, c, o * P:(o + 1) * P], wT[:, c, :]
                            else:
                                a, b = w01T[:, c, o * P:(o + 1) * P], w[:, 2, c, :]
                            last = nc.tensor.matmul(psW[:, o, :], a, b, start=(c == 0), stop=(c == HC - 1))
                    last.then_inc(wstep, 1)
                pe.wait_ge(wcopied, 3)

                def transposes(i, s):
                    pe.wait_ge(xn_ready, i + 1)
                    if past(i, 2):
                        pe.wait_ge(xnT_ready, i - 1)
                    for c in range(HC):
                        last = nc.tensor.transpose(psT[s][:, c * P:(c + 1) * P], xn[:, s, c * P:(c + 1) * P], R.ident[:])
                    last.then_inc(psT_ready, 1)

                def products(i, s):
                    pe.wait_ge(xnT_ready, i + 1)
                    if past(i, 2):
                        pe.wait_ge(pre_ready, i - 1)
                    for c in range(HC):
                        last = nc.tensor.matmul(psY[s][:, 0:HID], xnT[:, s, c, :], wc[:, c, :], start=(c == 0), stop=(c == HC - 1))
                    last.then_inc(psY_ready, 1)

                skewed(pe, NT, [(0, transposes), (1, products)])

            @block.scalar
            def _(act):
                std_of_var(nc, act, R, var_ready, std_ready)
                for m, dst in enumerate((wT, w01T, wc)):
                    act.wait_ge(wstep, m + 1)
                    nc.scalar.copy(dst[:], psW[:]).then_inc(wcopied, 1)

                def copy_xnT(i, s):
                    act.wait_ge(psT_ready, i + 1)
                    if past(i, 2):
                        act.wait_ge(psY_ready, i - 1)
                    nc.scalar.copy(xnT[:, s].rearrange("p c t -> p (c t)"), psT[s][:, 0:HID]).then_inc(xnT_ready, 1)

                def tanh(i, s):
                    act.wait_ge(pre_ready, i + 1)
                    if past(i, 2):
                        act.wait_ge(x_ready, i - 1)
                    nc.scalar.activation(th[:, s], pre[:, s], ACT.Tanh).then_inc(th_ready, 1)

                skewed(act, NT, [(0, copy_xnT), (2, tanh)])

            @block.vector
            def _(dve):
                layernorm_scales(nc, dve, None, R, step, var_ready, std_ready)

                def normalize(i, s):
                    if past(i, 2):
                        dve.wait_ge(psT_ready, i - 1)
                    nc.vector.tensor_scalar(xn[:, s], row_of(R.X, i), R.rstd[:, bass.ds(i, 1)], R.shift[:, bass.ds(i, 1)],
                                            ALU.mult, ALU.add).then_inc(xn_ready, 1)

                def add_bias(i, s):
                    dve.wait_ge(psY_ready, i + 1)
                    if past(i, 2):
                        dve.wait_ge(th_ready, i - 1)
                    nc.vector.tensor_tensor(pre[:, s], psY[s][:, 0:HID], bias_all[:], ALU.add).then_inc(pre_ready, 1)

                def stats(i, s):
                    dve.wait_ge(x_ready, i + 1)
                    nc.vector.bn_stats(row_of(R.raw, i), row_of(R.X, i))

                skewed(dve, NT, [(0, normalize), (2, add_bias), (4, stats)])

            @block.gpsimd
            def _(pool):
                def residual(i, s):
                    pool.wait_ge(th_ready, i + 1)
                    nc.gpsimd.tensor_tensor(row_of(R.X, i), row_of(R.X, i), th[:, s], ALU.add).then_inc(x_ready, 1)

                skewed(pool, NT, [(0, residual)])


def top_k_experts(nc, R, tag, A, C, before):
    E, F, K = 8, 1024, 128
    NF = F // P
    ROUNDS = K // 8
    PAIRS = E * BATCH // 2
    PE_ = BATCH // 2
    with Stage(nc, tag) as st:
        sb, ps, sem = st.sb, st.ps, st.sem
        w1, w2 = sb("w1", [P, 2, HC, F]), sb("w2", [P, 2, NF, HID])
        b1_rows, b1 = sb("b1_rows", [E * NF, P]), sb("b1", [P, E * NF])
        b2_all = sb("b2_all", [P, E, HID])
        wgT = sb("wgT", [P, HC, E])
        gate, index = sb("gate", [P, E, BATCH]), sb("index", [P, E, BATCH], U32)
        zero = sb("zero", [P, 1], U32)
        ban = [ps(f"bank{i}") for i in range(8)]
        gathered_from, summed = R.xn_dram, R.sum_dram

        with Stage(nc, tag + "r") as rt:
            xn, xnT = rt.sb("xn", [P, 4, HID]), rt.sb("xnT", [P, 2, HID])
            L, Lx, Lsum = rt.sb("L", [P, NT, E]), rt.sb("Lx", [P, NT, E]), rt.sb("Lsum", [P, NT])
            SC = rt.sb("SC", [BATCH * E, SEQ])
            top, where = rt.sb("top", [BATCH * E, K]), rt.sb("where", [BATCH * E, K], U32)
            wheref, rowbase = rt.sb("wheref", [BATCH * E, K]), rt.sb("rowbase", [BATCH * E, 1])
            loaded, x_out, xn_out = rt.sem("loaded"), rt.sem("x_out"), rt.sem("xn_out")
            step, var_ready, std_ready = rt.sem("step"), rt.sem("var_ready"), rt.sem("std_ready")
            xn_ready, xT_done, xT_ready, L_done, L_ready = (rt.sem("xn_ready"), rt.sem("xT_done"), rt.sem("xT_ready"),
                                                           rt.sem("L_done"), rt.sem("L_ready"))
            shifted, exped, soft, turned, sc_ready = (rt.sem("shifted"), rt.sem("exped"), rt.sem("soft"), rt.sem("turned"),
                                                     rt.sem("sc_ready"))
            found, ends_turned, b1_turned, b1_ready = rt.sem("found"), rt.sem("ends_turned"), rt.sem("b1_turned"), rt.sem("b1_ready")
            xn_to = gathered_from.rearrange("(i p) d -> i p d", p=P)
            slot_out = [rt.sem(f"xn_out{n}") for n in range(4)]
            with nc.Block() as block:
                @block.sync
                def _(sp):
                    for c in range(HC):
                        sp.dma_start(wgT[:, c], A["L0_ffn_Wg"][:, c * P:(c + 1) * P].rearrange("e p -> p e"),
                                     allow_slow_non_contiguous=True).then_inc(loaded, 16)
                    sp.dma_start(b1_rows[:], A["L0_ffn_b1"].rearrange("e (f p) -> (e f) p", p=P)).then_inc(loaded, 16)
                    sp.dma_start(b2_all[:], A["L0_ffn_b2"].rearrange("(a e) d -> a e d", a=1).broadcast_to([P, E, HID])
                                 ).then_inc(loaded, 16)
                    sp.dma_start(rowbase[:], C["row_base"]).then_inc(loaded, 16)
                    for b in range(BATCH):
                        sp.dma_start(summed[b * SEQ:(b + 1) * SEQ, :].rearrange("(j p) d -> p j d", p=P),
                                     R.X[:, b * TB:(b + 1) * TB, :]).then_inc(x_out, 16)

                    def store_xn(i, s):
                        sp.wait_ge(xn_ready, i + 1)
                        sp.dma_start(xn_to[bass.ds(i, 1)].rearrange("a p d -> (a p) d"), xn[:, s]).then_inc(slot_out[s], 16)

                    skewed(sp, NT, [(0, store_xn)], unroll=4)
                    sp.wait_ge(x_out, 16 * BATCH)
                    for n in range(4):
                        sp.wait_ge(slot_out[n], 16 * NT // 4)

                @block.tensor
                def _(pe):
                    pe.wait_ge(loaded, 80)
                    nc.tensor.transpose(ban[7][:, 0:E * NF], b1_rows[:], R.ident[0:E * NF, 0:E * NF]).then_inc(b1_turned, 1)

                    def turn_x(i, s):
                        pe.wait_ge(xn_ready, i + 1)
                        if past(i, 2):
                            pe.wait_ge(xT_ready, i - 1)
                        for c in range(HC):
                            last = nc.tensor.transpose(ban[s % 2][:, c * P:(c + 1) * P], xn[:, s, c * P:(c + 1) * P], R.ident[:])
                        last.then_inc(xT_done, 1)

                    def logits(i, s):
                        pe.wait_ge(xT_ready, i + 1)
                        if past(i, 2):
                            pe.wait_ge(L_ready, i - 1)
                        for c in range(HC):
                            last = nc.tensor.matmul(ban[2 + s % 2][:, 0:E], xnT[:, s % 2, c * P:(c + 1) * P], wgT[:, c, :],
                                                    start=(c == 0), stop=(c == HC - 1))
                        last.then_inc(L_done, 1)

                    skewed(pe, NT, [(0, turn_x), (1, logits)], unroll=4)
                    pe.wait_ge(soft, 1)
                    for j in range(TB):
                        if j >= 2:
                            pe.wait_ge(sc_ready, j - 1)
                        nc.tensor.transpose(ban[4 + j % 2][0:BATCH * E, 0:P], L[:, j * BATCH:(j + 1) * BATCH, :].rearrange("p b e -> p (b e)"), R.ident[:]).then_inc(turned, 1)
                    pe.wait_ge(found, 1)
                    nc.tensor.transpose(ban[6][:, 0:BATCH * E], top[:], R.ident[0:BATCH * E, 0:BATCH * E]).then_inc(ends_turned, 1)
                    pe.wait_ge(b1_ready, 1)
                    nc.tensor.transpose(ban[7][:, 0:BATCH * E], wheref[:], R.ident[0:BATCH * E, 0:BATCH * E]).then_inc(ends_turned, 1)

                @block.scalar
                def _(act):
                    std_of_var(nc, act, R, var_ready, std_ready)
                    act.wait_ge(b1_turned, 1)
                    nc.scalar.copy(b1[:], ban[7][:, 0:E * NF]).then_inc(b1_ready, 1)

                    def copy_xT(i, s):
                        act.wait_ge(xT_done, i + 1)
                        if past(i, 2):
                            act.wait_ge(L_done, i - 1)
                        nc.scalar.copy(xnT[:, s % 2], ban[s % 2][:, 0:HID]).then_inc(xT_ready, 1)

                    skewed(act, NT, [(0, copy_xT)], unroll=4)
                    act.wait_ge(shifted, 1)
                    nc.scalar.activation(Lx[:], Lx[:], ACT.Exp).then_inc(exped, 1)
                    for j in range(TB):
                        act.wait_ge(turned, j + 1)
                        nc.scalar.copy(SC[:, j * P:(j + 1) * P], ban[4 + j % 2][0:BATCH * E, 0:P]).then_inc(sc_ready, 1)

                @block.vector
                def _(dve):
                    layernorm_scales(nc, dve, None, R, step, var_ready, std_ready)

                    def normalize(i, s):
                        if past(i, 4):
                            dve.wait_ge(xT_done, i - 3)
                            dve.wait_ge(slot_out[s], (i - s) * 4)
                        nc.vector.tensor_scalar(xn[:, s], row_of(R.X, i), R.rstd[:, bass.ds(i, 1)], R.shift[:, bass.ds(i, 1)],
                                                ALU.mult, ALU.add).then_inc(xn_ready, 1)

                    def copy_L(i, s):
                        dve.wait_ge(L_done, i + 1)
                        nc.vector.tensor_copy(row_of(L, i), ban[2 + s % 2][:, 0:E]).then_inc(L_ready, 1)

                    skewed(dve, NT, [(0, normalize), (2, copy_L)], unroll=4)
                    dve.wait_ge(L_ready, NT)
                    c = Chain(dve, rt.sem("softmax_step"))
                    c.then(nc.vector.tensor_reduce(Lsum[:], L[:], AX_X, ALU.max))
                    nc.vector.tensor_tensor(Lx[:], L[:], Lsum[:, :, None].broadcast_to([P, NT, E]), ALU.subtract).then_inc(shifted, 1)
                    dve.wait_ge(exped, 1)
                    c.then(nc.vector.tensor_reduce(Lsum[:], Lx[:], AX_X, ALU.add))
                    c.then(nc.vector.reciprocal(Lsum[:], Lsum[:]))
                    nc.vector.tensor_tensor(L[:].rearrange("p (j b) e -> p b j e", j=TB),
                                            Lx[:].rearrange("p (b j) e -> p b j e", j=TB),
                                            Lsum[:].rearrange("p (b j) -> p b j", j=TB)[:, :, :, None].broadcast_to([P, BATCH, TB, E]),
                                            ALU.mult).then_inc(soft, 1)
                    dve.wait_ge(sc_ready, TB)
                    for r in range(ROUNDS):
                        best = top[:, 8 * r:8 * r + 8]
                        c.then(nc.vector.max(out=best, in_=SC[:]))
                        c.then(nc.vector.max_index(out=where[:, 8 * r:8 * r + 8], in_max=best, in_values=SC[:]))
                        if r < ROUNDS - 1:
                            c.then(nc.vector.match_replace(out=SC[:], in_to_replace=best, in_values=SC[:], imm_value=-1.0))
                    c.then(nc.vector.tensor_copy(wheref[:], where[:]))
                    dve.wait_ge(loaded, 80)
                    nc.vector.tensor_scalar(wheref[:], wheref[:], rowbase[:, 0:1], None, ALU.add).then_inc(found, 1)
                    dve.wait_ge(ends_turned, 1)
                    nc.vector.tensor_copy(gate[:].rearrange("p e b -> p b e"), ban[6][:, 0:BATCH * E].rearrange("p (b e) -> p b e", e=E))
                    dve.wait_ge(ends_turned, 2)
                    nc.vector.tensor_copy(index[:].rearrange("p e b -> p b e"), ban[7][:, 0:BATCH * E].rearrange("p (b e) -> p b e", e=E))
                    nc.vector.memset(zero[:], 0)

        gate_g = gate[:].rearrange("p e b -> p (e b)")
        index_g = index[:].rearrange("p e b -> p (e b)")

        with Stage(nc, tag + "e") as ex:
            rows = ex.sb("rows", [P, 4, 2], U32)
            ex_in, exT = ex.sb("ex_in", [P, 2, 2, HID]), ex.sb("exT", [P, 2, HC, 2, P])
            hT = ex.sb("hT", [P, 2, NF, 2 * P])
            pre, y = ex.sb("pre", [P, 2, 2, HID]), ex.sb("y", [P, 2, 2, HID])
            turn = ex.sb("turn", [P, 2], U32)
            bias = ex.sb("bias", [P, 2, NF])
            bias_ready = ex.sem("bias_ready")
            bx, bh, by = ban[0], ban[1:6], ban[6:8]
            w_loaded = [ex.sem(f"w_loaded{n}") for n in range(2)]
            fetched_before, scattered_before = before * PAIRS // 4 * 32, before * E * 16
            fetched, scattered = R.fetched, R.scattered
            rows_ready, x_turned, xT_ready, up_done, h_ready = (ex.sem("rows_ready"), ex.sem("x_turned"), ex.sem("xT_ready"),
                                                               ex.sem("up_done"), ex.sem("h_ready"))
            down_done, pre_ready, y_ready, turns = (ex.sem("down_done"), ex.sem("pre_ready"), ex.sem("y_ready"),
                                                     [ex.sem("turns0"), ex.sem("turns1")])
            U = 2 * PE_

            with nc.Block() as block:
                @block.sync
                def _(sp):
                    def weights(e, par, waits):
                        if waits:
                            sp.wait_ge(down_done, PE_ * (e - 1))
                        sp.dma_start(w1[:, par], A["L0_ffn_W1"][bass.ds(e, 1)].rearrange("a (c p) f -> p (a c) f", p=P)
                                     ).then_inc(w_loaded[par], 16)
                        sp.dma_start(w2[:, par], A["L0_ffn_W2"][bass.ds(e, 1)].rearrange("a (c p) d -> p (a c) d", p=P)
                                     ).then_inc(w_loaded[par], 16)

                    for e in range(2):
                        weights(e, e, False)
                    with sp.Fori(2, E - 1, 2) as e:
                        for par in range(2):
                            weights(e + par, par, True)

                @block.gpsimd
                def _(pool):
                    def fetch(t, s):
                        pair = rows[:, s % 4, :]
                        if past(t, 2):
                            pool.wait_ge(x_turned, t - 1)
                        if past(t, 4):
                            for u in range(2):
                                b = 2 * (s % PE_) + u
                                pool.wait_ge(scattered[b], 4 * (t - s % PE_) + scattered_before)
                        nc.gpsimd.tensor_tensor(pair, index_g[:, bass.ds(2 * t, 2)], zero[:].broadcast_to([P, 2]), ALU.add
                                                ).then_inc(rows_ready, 1)
                        pool.wait_ge(rows_ready, t + 1)
                        if past(t, 1):
                            pool.wait_ge(turns[0], t)
                        nc.gpsimd.tensor_tensor(turn[:, 0:1], zero[:], zero[:], ALU.add).then_inc(turns[0], 1)
                        for u in range(2):
                            nc.gpsimd.indirect_dma_start(out=ex_in[:, s % 2, u, :], out_offset=None, in_=gathered_from,
                                                         in_offset=bass.IndirectOffsetOnAxis(ap=rows[:, s % 4, u:u + 1], axis=0)
                                                         ).then_inc(fetched[s % 4], 16)

                    def scatter(t, s):
                        pool.wait_ge(y_ready, 2 * t + 2)
                        if past(t, 1):
                            pool.wait_ge(turns[1], t)
                        nc.gpsimd.tensor_tensor(turn[:, 1:2], zero[:], zero[:], ALU.add).then_inc(turns[1], 1)
                        for u in range(2):
                            b = 2 * (s % PE_) + u
                            nc.gpsimd.indirect_dma_start(out=summed, out_offset=bass.IndirectOffsetOnAxis(ap=rows[:, s % 4, u:u + 1], axis=0),
                                                         in_=y[:, s % 2, u, :], in_offset=None, compute_op=ALU.add
                                                         ).then_inc(scattered[b], 16)

                    skewed(pool, PAIRS, [(0, fetch), (3, scatter)], unroll=U)
                    for b in range(BATCH):
                        pool.wait_ge(scattered[b], 16 * E + scattered_before)

                @block.tensor
                def _(pe):
                    def turn_x(t, s):
                        pe.wait_ge(fetched[s % 4], 8 * (t - s % 4) + 32 + fetched_before)
                        if past(t, 1):
                            pe.wait_ge(xT_ready, t)
                        for c in range(HC):
                            for u in range(2):
                                last = nc.tensor.transpose(bx[:, (2 * c + u) * P:(2 * c + u + 1) * P],
                                                           ex_in[:, s % 2, u, c * P:(c + 1) * P], R.ident[:])
                        last.then_inc(x_turned, 1)

                    def up(t, s):
                        par = s // PE_
                        pe.wait_ge(xT_ready, t + 1)
                        if s % PE_ == 0:
                            pe.wait_ge(w_loaded[par], 4 * (t - s) + 32)
                        for f in range(NF):
                            n = NF * (s % 5) + f
                            bank = bh[(NF * s + f) % 5]
                            if not isinstance(t, int) or NF * t + f >= 5:
                                pe.wait_ge(h_ready, NF * t + f - 4)
                            for c in range(HC):
                                last = nc.tensor.matmul(bank[:, 0:2 * P], w1[:, par, c, f * P:(f + 1) * P],
                                                        exT[:, s % 2, c].rearrange("p u t -> p (u t)"),
                                                        start=(c == 0), stop=(c == HC - 1))
                            last.then_inc(up_done, 1)

                    def down(t, s):
                        par = s // PE_
                        pe.wait_ge(h_ready, NF * t + NF)
                        for u in range(2):
                            if past(t, 1):
                                pe.wait_ge(pre_ready, 2 * t - 1 + u)
                            for f in range(NF):
                                last = nc.tensor.matmul(by[u][:, 0:HID], hT[:, s % 2, f, u * P:(u + 1) * P], w2[:, par, f, :],
                                                        start=(f == 0), stop=(f == NF - 1))
                        last.then_inc(down_done, 1)

                    skewed(pe, PAIRS, [(0, turn_x), (2, down), (1, up)], unroll=U)

                @block.scalar
                def _(act):
                    def gelu(t, s):
                        par = s // PE_
                        if s % PE_ == 0:
                            act.wait_ge(bias_ready, (t - s % PE_) // PE_ + 1 if isinstance(t, int) else (t - s) // 4 + s // PE_ + 1)
                        for f in range(NF):
                            act.wait_ge(up_done, NF * t + f + 1)
                            if f == 0 and past(t, 2):
                                act.wait_ge(down_done, t - 1)
                            nc.scalar.activation(hT[:, s % 2, f], bh[(NF * s + f) % 5][:, 0:2 * P], ACT.Gelu_apprx_tanh,
                                                 bias=bias[:, par, f:f + 1]).then_inc(h_ready, 1)

                    skewed(act, PAIRS, [(1, gelu)], unroll=U)

                @block.vector
                def _(dve):
                    def copy_xT(t, s):
                        if s % PE_ == 0:
                            if past(t, U):
                                dve.wait_ge(h_ready, NF * (t - PE_))
                            nc.vector.tensor_scalar(bias[:, s // PE_], b1[:, bass.ds(t * (NF // PE_), NF)], 0.0, None, ALU.add
                                                    ).then_inc(bias_ready, 1)
                        dve.wait_ge(x_turned, t + 1)
                        if past(t, 2):
                            dve.wait_ge(up_done, NF * (t - 1))
                        nc.vector.tensor_copy(exT[:, s % 2].rearrange("p c u t -> p (c u t)"), bx[:]).then_inc(xT_ready, 1)

                    def add_b2(t, s):
                        for u in range(2):
                            if u == 0:
                                dve.wait_ge(down_done, t + 1)
                            if past(t, 2):
                                dve.wait_ge(y_ready, 2 * t - 3 + u)
                            expert = (t - s % PE_) // PE_ if isinstance(t, int) else None
                            b2 = b2_all[:, expert, :] if expert is not None else \
                                b2_flat[:, bass.ds((t - s % PE_) * (HID // PE_), HID)]
                            nc.vector.tensor_tensor(pre[:, s % 2, u], by[u][:, 0:HID], b2, ALU.add).then_inc(pre_ready, 1)

                    def weigh(t, s):
                        for u in range(2):
                            dve.wait_ge(pre_ready, 2 * t + u + 1)
                            if past(t, 2):
                                b = 2 * ((s - 2) % PE_) + u
                                dve.wait_ge(scattered[b], 4 * (t - 2 - (s - 2) % PE_) + 16 + scattered_before)
                            nc.vector.tensor_scalar(y[:, s % 2, u], pre[:, s % 2, u], gate_g[:, bass.ds(2 * t + u, 1)], None, ALU.mult
                                                    ).then_inc(y_ready, 1)

                    b2_flat = b2_all[:].rearrange("p e d -> p (e d)")
                    skewed(dve, PAIRS, [(0, copy_xT), (2, add_b2), (2, weigh)], unroll=U)

        reload_x(nc, R, tag + "l", summed)


def turned_copies(nc, R, tag, jobs, banks):
    blocks = []
    with Stage(nc, tag) as st:
        loaded, turned, copied = st.sem("loaded"), st.sem("turned"), st.sem("copied")
        for n, (src, dst) in enumerate(jobs):
            rows, cols = src.shape
            staged = st.sb(f"staged{n}", [P, rows // P, cols])
            flat = dst.rearrange("p c r -> p (c r)")
            places = [(c, r) for c in range(cols // P) for r in range(rows // P)]
            for k in range(0, len(places), 4):
                blocks.append(([staged[:, r, c * P:(c + 1) * P] for c, r in places[k:k + 4]], flat[:, k * P:(k + 4) * P]))
            jobs[n] = (src, staged)
        with nc.Block() as block:
            @block.sync
            def _(sp):
                for src, staged in jobs:
                    sp.dma_start(staged[:], src.rearrange("(r p) c -> p r c", p=P)).then_inc(loaded, 16)

            @block.tensor
            def _(pe):
                pe.wait_ge(loaded, 16 * len(jobs))
                for n, (parts, _) in enumerate(blocks):
                    if n >= 2:
                        pe.wait_ge(copied, n - 1)
                    for k, part in enumerate(parts):
                        last = nc.tensor.transpose(banks[n % 2][:, k * P:(k + 1) * P], part, R.ident[:])
                    last.then_inc(turned, 1)

            @block.scalar
            def _(act):
                for n, (_, to) in enumerate(blocks):
                    act.wait_ge(turned, n + 1)
                    nc.scalar.copy(to, banks[n % 2][:]).then_inc(copied, 1)


def spectral_attention(nc, R, A, C):
    CH = 64
    NF = CH // 2 + 1
    LOW = 4
    HIGH = NF - LOW
    NCH = BATCH * SEQ // CH
    CB = SEQ // CH
    TAPS = 7
    HEADS, KV, HD = 16, 4, 64
    PRS = HEADS // 2
    with Stage(nc, "sp") as st:
        sb, ps, sem = st.sb, st.ps, st.sem
        qwT, kwT, vwT = sb("qwT", [P, HC, HEADS * HD]), sb("kwT", [P, HC, HID]), sb("vwT", [P, HC, HID])
        gwT, owT = sb("gwT", [P, HC, HID]), sb("owT", [P, PRS, HID])
        pwT = [sb("pwT_r", [P, HC, HID]), sb("pwT_i", [P, HC, HID])]
        bank = [ps(f"bank{i}") for i in range(8)]
        turned_copies(nc, R, "spw", [(A["L0_attn_b_q_w"], qwT[:]), (A["L0_attn_b_k_w"], kwT[:]), (A["L0_attn_b_v_w"], vwT[:]),
                                     (A["L0_attn_b_gate_w"], gwT[:]), (A["L0_attn_b_o_w"], owT[:]),
                                     (A["L0_attn_b_pw_r"], pwT[0][:]), (A["L0_attn_b_pw_i"], pwT[1][:])], bank)
        XF = sb("XF", [P, HC, NCH, 2, NF])
        lowA = sb("lowA", [P, BATCH, HID])
        alpha = sb("alpha", [P, 1])
        dw = sb("dw", [P, HC, 2, TAPS])
        XF_tile = XF[:].rearrange("p c (t h) r f -> p c t (h r f)", h=2)
        W = 2 * 2 * NF

        with Stage(nc, "spf") as f:
            dft = f.sb("dft", [P, W])
            xn = f.sb("xn", [P, 2, HID])
            g = f.sb("g", [P, HID])
            loaded, xn_ready, f_done, f_ready, z_done, e_ready, g_ready, stored = (
                f.sem("loaded"), f.sem("xn_ready"), f.sem("f_done"), f.sem("f_ready"), f.sem("z_done"), f.sem("e_ready"),
                f.sem("g_ready"), f.sem("stored"))
            step, var_ready, std_ready = f.sem("step"), f.sem("var_ready"), f.sem("std_ready")
            with nc.Block() as block:
                @block.sync
                def _(sp):
                    sp.dma_start(dft[:], C["dft"]).then_inc(loaded, 16)
                    sp.dma_start(alpha[:], A["L0_attn_b_alpha_raw"].rearrange("(a b) -> a b", a=1).broadcast_to([P, 1])).then_inc(loaded, 16)
                    for r, name in enumerate(("dw_r", "dw_i")):
                        sp.dma_start(dw[:, :, r, :], A[f"L0_attn_b_{name}"].rearrange("(c p) a k -> p c (a k)", p=P)).then_inc(loaded, 16)
                    sp.wait_ge(g_ready, 1)
                    sp.dma_start(R.gate_dram, g[:]).then_inc(stored, 16)
                    sp.wait_ge(stored, 16)

                @block.tensor
                def _(pe):
                    pe.wait_ge(loaded, 64)

                    def transform(i, s):
                        pe.wait_ge(xn_ready, i + 1)
                        if past(i, 2):
                            pe.wait_ge(f_ready, i - 1)
                        for c in range(HC):
                            last = nc.tensor.matmul(bank[s][:, c * W:(c + 1) * W], xn[:, s, c * P:(c + 1) * P], dft[:],
                                                    start=True, stop=True)
                        last.then_inc(f_done, 1)

                    skewed(pe, NT, [(0, transform)])
                    pe.wait_ge(f_ready, NT)
                    for c in range(HC):
                        last = nc.tensor.matmul(bank[2][:, 0:HID], XF[:, c, :, 0, 0], gwT[:, c, :], start=(c == 0), stop=(c == HC - 1))
                    last.then_inc(z_done, 1)

                @block.scalar
                def _(act):
                    std_of_var(nc, act, R, var_ready, std_ready)
                    act.wait_ge(loaded, 64)
                    nc.scalar.activation(alpha[:], alpha[:], ACT.Exp, scale=-1.0).then_inc(e_ready, 1)
                    act.wait_ge(z_done, 1)
                    nc.scalar.activation(g[:], bank[2][:, 0:HID], ACT.Exp, scale=-1.0 / CH).then_inc(e_ready, 1)

                @block.vector
                def _(dve):
                    layernorm_scales(nc, dve, None, R, step, var_ready, std_ready)

                    def normalize(i, s):
                        if past(i, 2):
                            dve.wait_ge(f_done, i - 1)
                        nc.vector.tensor_scalar(xn[:, s], row_of(R.X, i), R.rstd[:, bass.ds(i, 1)], R.shift[:, bass.ds(i, 1)],
                                                ALU.mult, ALU.add).then_inc(xn_ready, 1)

                    def copy_f(i, s):
                        dve.wait_ge(f_done, i + 1)
                        nc.vector.tensor_scalar(XF_tile[:, :, bass.ds(i, 1), :].rearrange("p c a w -> p (c a) w"),
                                                bank[s][:, 0:HC * W].rearrange("p (c w) -> p c w", c=HC), 0.0, None, ALU.add
                                                ).then_inc(f_ready, 1)

                    skewed(dve, NT, [(0, normalize), (1, copy_f)])
                    c = Chain(dve, f.sem("gate_step"))
                    dve.wait_ge(e_ready, 1)
                    c.then(nc.vector.tensor_scalar(alpha[:], alpha[:], 1.0, None, ALU.add))
                    c.then(nc.vector.reciprocal(alpha[:], alpha[:]))
                    dve.wait_ge(e_ready, 2)
                    c.then(nc.vector.tensor_scalar(g[:], g[:], 1.0, None, ALU.add))
                    nc.vector.reciprocal(g[:], g[:]).then_inc(g_ready, 1)

        T = CB * LOW
        with Stage(nc, "spa") as a:
            kwd = a.sb("kwd", [P, HC, KV, 2, HD])
            XL = a.sb("XL", [P, 2, HC, 2, T])
            Qd = a.sb("Qd", [P, 2, PRS, 2, T])
            kT = a.sb("kT", [P, KV, 2, T])
            v = a.sb("v", [P, HID])
            mask = a.sb("mask", [P, T])
            S, prob, tops, sums = (a.sb("S", [P, 2 * PRS, T]), a.sb("prob", [P, 2 * PRS, T]), a.sb("tops", [P, 2 * PRS]),
                                   a.sb("sums", [P, 2 * PRS]))
            pT, oT = a.sb("pT", [P, PRS, P]), a.sb("oT", [P, PRS, P])
            names = "loaded kwd_ready zeroed XL_ready q_done k_done v_done q_ready kv_ready S_done S_read shifted exped prob_ready pT_done pT_ready o_done o_ready A_done A_ready soft".split()
            (loaded, kwd_ready, zeroed, XL_ready, q_done, k_done, v_done, q_ready, kv_ready, S_done, S_read, shifted, exped,
             prob_ready, pT_done, pT_ready, o_done, o_ready, A_done, A_ready, soft) = (a.sem(n) for n in names)
            XF_row = XF[:].rearrange("p c (b n) r f -> p c b n r f", b=BATCH)
            with nc.Block() as block:
                @block.sync
                def _(sp):
                    sp.dma_start(mask[:], C["chunk_mask"]).then_inc(loaded, 16)

                @block.tensor
                def _(pe):
                    pe.wait_ge(kwd_ready, 2)

                    def project(b, s):
                        pe.wait_ge(XL_ready, b + 1)
                        if past(b, 1):
                            pe.wait_ge(q_ready, 4 * b)
                            pe.wait_ge(kv_ready, 2 * b)
                        for m in range(PRS):
                            for c in range(HC):
                                last = nc.tensor.matmul(bank[m // 4][:, m % 4 * P:(m % 4 + 1) * P], qwT[:, c, m * P:(m + 1) * P],
                                                        XL[:, s, c].rearrange("p r t -> p (r t)"), start=(c == 0), stop=(c == HC - 1))
                            if m % 4 == 3:
                                last.then_inc(q_done, 1)
                        for m in range(KV):
                            for c in range(HC):
                                last = nc.tensor.matmul(bank[2][:, m * P:(m + 1) * P], kwd[:, c, m].rearrange("p u d -> p (u d)"),
                                                        XL[:, s, c].rearrange("p r t -> p (r t)"), start=(c == 0), stop=(c == HC - 1))
                        last.then_inc(k_done, 1)
                        if past(b, 1):
                            pe.wait_ge(A_ready, b)
                        for c in range(HC):
                            last = nc.tensor.matmul(bank[3][:, 0:HID], XL[:, s, c].rearrange("p r t -> p (r t)"), vwT[:, c, :],
                                                    start=(c == 0), stop=(c == HC - 1))
                        last.then_inc(v_done, 1)

                    def scores(b, s):
                        pe.wait_ge(q_ready, 4 * b + 4)
                        pe.wait_ge(kv_ready, 2 * b + 2)
                        if past(b, 1):
                            pe.wait_ge(S_read, 2 * b)
                        for m in range(PRS):
                            for r in range(2):
                                last = nc.tensor.matmul(bank[4 + m // 4][:, (m % 4 * 2 + r) * T:(m % 4 * 2 + r + 1) * T],
                                                        Qd[:, r, m].rearrange("p h q -> p (h q)"), kT[:, m // 2, r], start=True, stop=True)
                            if m % 4 == 3:
                                last.then_inc(S_done, 1)

                    def weigh(b, s):
                        pe.wait_ge(prob_ready, b + 1)
                        if past(b, 1):
                            pe.wait_ge(o_ready, 2 * b)
                        for m in range(PRS):
                            last = nc.tensor.transpose(bank[6 + m // 4][:, m % 4 * P:(m % 4 + 1) * P],
                                                       prob[:, 2 * m:2 * m + 2].rearrange("p r k -> p (r k)"), R.ident[:])
                            if m % 4 == 3:
                                last.then_inc(pT_done, 1)
                        pe.wait_ge(pT_ready, 2 * b + 2)
                        for r in range(2):
                            for m in range(PRS):
                                for h in range(2):
                                    last = nc.tensor.matmul(bank[6 + r][h * HD:(h + 1) * HD, m * T:(m + 1) * T],
                                                            v[r * T:(r + 1) * T, (m // 2) * HD:(m // 2 + 1) * HD],
                                                            pT[r * T:(r + 1) * T, m, h * T:(h + 1) * T], start=True, stop=True)
                            last.then_inc(o_done, 1)
                        pe.wait_ge(o_ready, 2 * b + 2)
                        for m in range(PRS):
                            last = nc.tensor.matmul(bank[3][:, 0:HID], oT[:, m, :], owT[:, m, :], start=(m == 0), stop=(m == PRS - 1))
                        last.then_inc(A_done, 1)

                    for b in range(BATCH):
                        project(b, b % 2)
                        scores(b, b % 2)
                        weigh(b, b % 2)

                @block.scalar
                def _(act):
                    for u in range(2):
                        nc.scalar.copy(kwd[:, :, :, u, :], kwT[:].rearrange("p c (k d) -> p c k d", d=HD)).then_inc(kwd_ready, 1)
                    for b in range(BATCH):
                        for n in range(2):
                            act.wait_ge(q_done, 2 * b + n + 1)
                            if b == 0 and n == 0:
                                act.wait_ge(zeroed, 1)
                            if b >= 1 and n == 0:
                                act.wait_ge(S_done, 2 * b)
                            for h in range(2):
                                half = slice(h * HD, (h + 1) * HD)
                                nc.scalar.copy(Qd[half, :, 4 * n:4 * n + 4, h, :].rearrange("p r m q -> p m r q"),
                                               bank[n][half, :].rearrange("p (m r q) -> p m r q", m=4, r=2)).then_inc(q_ready, 1)
                        act.wait_ge(k_done, b + 1)
                        nc.scalar.copy(kT[:].rearrange("p k r t -> p (k r t)"), bank[2][:]).then_inc(kv_ready, 1)
                        act.wait_ge(v_done, b + 1)
                        if b:
                            act.wait_ge(o_done, 2 * b)
                        nc.scalar.copy(v[:], bank[3][:, 0:HID]).then_inc(kv_ready, 1)
                        act.wait_ge(shifted, b + 1)
                        nc.scalar.activation(prob[:], S[:], ACT.Exp).then_inc(exped, 1)
                        for n in range(2):
                            act.wait_ge(pT_done, 2 * b + n + 1)
                            nc.scalar.copy(pT[:, 4 * n:4 * n + 4].rearrange("p m t -> p (m t)"), bank[6 + n][:]).then_inc(pT_ready, 1)
                        for n in range(2):
                            act.wait_ge(o_done, 2 * b + n + 1)
                            if b and n == 0:
                                act.wait_ge(A_done, b)
                            nc.scalar.copy(oT[:, :, n * T:(n + 1) * T], bank[6 + n][:].rearrange("p (m t) -> p m t", t=T)).then_inc(o_ready, 1)
                        act.wait_ge(A_done, b + 1)
                        nc.scalar.copy(lowA[:, b], bank[3][:, 0:HID]).then_inc(A_ready, 1)

                @block.vector
                def _(dve):
                    nc.vector.memset(Qd[:], 0.0).then_inc(zeroed, 1)
                    c = Chain(dve, soft)
                    for b in range(BATCH):
                        if b >= 2:
                            dve.wait_ge(v_done, b - 1)
                        for half in range(HC):
                            ins = nc.vector.tensor_copy(XL[:, b % 2, half].rearrange("p r (n f) -> p r n f", f=LOW),
                                                        XF_row[:, half, b, :, :, 0:LOW].rearrange("p n r f -> p r n f"))
                        ins.then_inc(XL_ready, 1)
                        if b >= 1:
                            dve.wait_ge(pT_done, 2 * b)
                        if b == 0:
                            dve.wait_ge(loaded, 16)
                        for n in range(2):
                            dve.wait_ge(S_done, 2 * b + n + 1)
                            c.then(nc.vector.scalar_tensor_tensor(
                                out=S[:, 8 * n:8 * n + 8], in0=bank[4 + n][:].rearrange("p (m t) -> p m t", t=T), scalar=HD ** -0.5,
                                in1=mask[:, None, :].broadcast_to([P, PRS, T]), op0=ALU.mult, op1=ALU.add))
                            nc.vector.memset(R.turnstile[:], 0.0).then_inc(S_read, 1)
                        c.then(nc.vector.tensor_reduce(tops[:], S[:], AX_X, ALU.max))
                        nc.vector.tensor_tensor(S[:], S[:], tops[:, :, None].broadcast_to([P, 2 * PRS, T]), ALU.subtract).then_inc(shifted, 1)
                        dve.wait_ge(exped, b + 1)
                        c.then(nc.vector.tensor_reduce(sums[:], prob[:], AX_X, ALU.add))
                        c.then(nc.vector.reciprocal(sums[:], sums[:]))
                        nc.vector.tensor_tensor(prob[:], prob[:], sums[:, :, None].broadcast_to([P, 2 * PRS, T]), ALU.mult
                                                ).then_inc(prob_ready, 1)

        G = 4
        GC = 2 * G
        STEPS = NT // G
        with Stage(nc, "spc") as k:
            inv_high, inv_low, low_pass = k.sb("inv_high", [P, P]), k.sb("inv_low", [P, TB, P]), k.sb("low_pass", [P, P])
            acc = k.sb("acc", [P, HC, 2, GC, HIGH])
            gel = k.sb("gel", [P, 2, HC, 2, GC, HIGH])
            H = k.sb("H", [P, 2, HID])
            xn = k.sb("xn", [P, 4, HID])
            gx = k.sb("gx", [P, 4, HID])
            high, low = k.sb("high", [P, 2, HID]), k.sb("low", [P, 2, HID])
            names = "loaded zeroed acc_ready gel_ready xn_ready H_done H_ready Y_done terms_ready high_in x_ready taps".split()
            loaded, zeroed, acc_ready, gel_ready, xn_ready, H_done, H_ready, Y_done, terms_ready, high_in, x_ready, taps = (
                k.sem(n) for n in names)
            gx_in = [k.sem(f"gx_in{n}") for n in range(4)]
            XF_step = XF[:].rearrange("p c (k n) r f -> p c k n r f", n=GC)
            NTAP = HC * TAPS * 2
            with nc.Block() as block:
                @block.sync
                def _(sp):
                    for to, name in ((inv_high[:], "inv_high"), (inv_low[:], "inv_low"), (low_pass[:], "low_pass")):
                        sp.dma_start(to, C[name]).then_inc(loaded, 16)

                    def gates(i, s):
                        if past(i, 4):
                            sp.wait_ge(terms_ready, 2 * (i - 3))
                        for h in range(2):
                            sp.dma_start(gx[h * CH:(h + 1) * CH, s], R.gate_dram[bass.ds(2 * i + h, 1)].broadcast_to([CH, HID])
                                         ).then_inc(gx_in[s], 16)

                    skewed(sp, NT, [(0, gates)], unroll=4)

                @block.tensor
                def _(pe):
                    pe.wait_ge(loaded, 48)

                    def tile_H(t, j, s):
                        n = G * t + j
                        if not isinstance(t, int) or n >= 2:
                            pe.wait_ge(H_ready, 2 * (n - 1))
                        for r in range(2):
                            for c in range(HC):
                                last = nc.tensor.matmul(bank[n_slot(j)][r * CH:r * CH + 2 * HIGH, 0:HID],
                                                        gel[:, s, c, r, 2 * j:2 * j + 2].rearrange("p n f -> p (n f)"), pwT[r][:, c, :],
                                                        start=(c == 0), stop=(c == HC - 1))
                        last.then_inc(H_done, 1)

                    def tile_Y(t, j, place, row):
                        n = G * t + j
                        pe.wait_ge(H_ready, 2 * (n + 1))
                        pe.wait_ge(xn_ready, n + 1)
                        if not isinstance(t, int) or n >= 2:
                            pe.wait_ge(terms_ready, 2 * (n - 1))
                        nc.tensor.matmul(bank[2 + j % 2][:, 0:HID], inv_high[:], H[:, j % 2], start=True, stop=True)
                        nc.tensor.matmul(bank[4 + j % 2][:, 0:HID], low_pass[:], xn[:, j % 4], start=True, stop=False)
                        nc.tensor.matmul(bank[4 + j % 2][:, 0:HID], inv_low[:, place, :], row, start=False, stop=True).then_inc(Y_done, 1)

                    def n_slot(j):
                        return j % 2

                    lowA_flat = lowA[:].rearrange("p b d -> p (b d)")

                    def tiles(t, s):
                        pe.wait_ge(gel_ready, 4 * (t + 1))
                        row = lowA[:, t // 2, :] if isinstance(t, int) else lowA_flat[:, bass.ds((t - s) * (HID // 2), HID)]
                        for j in range(G + 1):
                            if j < G:
                                tile_H(t, j, s)
                            if j > 0:
                                tile_Y(t, j - 1, G * s + j - 1, row)

                    skewed(pe, STEPS, [(1, tiles)])

                @block.scalar
                def _(act):
                    def gelus(t, s):
                        for c in range(HC):
                            for r in range(2):
                                act.wait_ge(acc_ready, 4 * t + 2 * c + r + 1)
                                if past(t, 2) and c == 0 and r == 0:
                                    act.wait_ge(H_done, G * (t - 1))
                                nc.scalar.activation(gel[:, s, c, r], acc[:, c, r], ACT.Gelu).then_inc(gel_ready, 1)

                    def copies(t, s):
                        for j in range(G):
                            n = G * t + j
                            act.wait_ge(H_done, n + 1)
                            if not isinstance(t, int) or n >= 2:
                                act.wait_ge(Y_done, n - 1)
                            for r in range(2):
                                rows = slice(r * CH, r * CH + 2 * HIGH)
                                nc.scalar.copy(H[rows, j % 2], bank[j % 2][rows, 0:HID]).then_inc(H_ready, 1)

                    act.wait_ge(zeroed, 1)
                    skewed(act, STEPS, [(0, gelus), (1, copies)])

                @block.vector
                def _(dve):
                    nc.vector.memset(H[:], 0.0).then_inc(zeroed, 1)

                    def tile_norm(n, j):
                        if past(n, 4):
                            dve.wait_ge(terms_ready, 2 * (n - 3))
                        nc.vector.tensor_scalar(xn[:, j % 4], row_of(R.X, n), R.rstd[:, bass.ds(n, 1)], R.shift[:, bass.ds(n, 1)],
                                                ALU.mult, ALU.add).then_inc(xn_ready, 1)

                    def tile_terms(n, j):
                        dve.wait_ge(Y_done, n + 1)
                        dve.wait_ge(gx_in[j], (n - j) * 8 + 32)
                        if past(n, 2):
                            dve.wait_ge(x_ready, 2 * (n - 1))
                        nc.vector.tensor_tensor(high[:, j % 2], bank[2 + j % 2][:, 0:HID], gx[:, j], ALU.mult).then_inc(terms_ready, 1)
                        nc.vector.scalar_tensor_tensor(out=low[:, j % 2], in0=bank[4 + j % 2][:, 0:HID], scalar=alpha[:, 0:1],
                                                       in1=xn[:, j], op0=ALU.mult, op1=ALU.add).then_inc(terms_ready, 1)

                    def tile_stats(n):
                        dve.wait_ge(x_ready, 2 * (n + 1))
                        nc.vector.bn_stats(row_of(R.raw, n), row_of(R.X, n))

                    def taps_of(t, c, r, tap, order):
                        back = TAPS - 1 - tap
                        at = NTAP * t + order
                        src = XF_step[:, c, bass.ds(t, 1), :, r, LOW:NF - back].rearrange("p a n f -> p (a n) f")
                        if tap == TAPS - 1:
                            if past(t, 1):
                                dve.wait_ge(gel_ready, 4 * (t - 1) + 2 * c + r + 1)
                            ins = nc.vector.tensor_scalar(acc[:, c, r], src, dw[:, c, r, tap:tap + 1], None, ALU.mult)
                        else:
                            dve.wait_ge(taps, at - 1)
                            part = acc[:, c, r, :, back:HIGH]
                            ins = nc.vector.scalar_tensor_tensor(out=part, in0=src, scalar=dw[:, c, r, tap:tap + 1], in1=part,
                                                                 op0=ALU.mult, op1=ALU.add)
                        ins.then_inc(taps, 1)
                        if tap == 0:
                            dve.wait_ge(taps, at + 1)
                            nc.vector.memset(R.turnstile[:], 0.0).then_inc(acc_ready, 1)

                    def convolve(t, s):
                        order = 0
                        for c in range(HC):
                            for tap in range(TAPS - 1, -1, -1):
                                for r in range(2):
                                    taps_of(t, c, r, tap, order)
                                    order += 1

                    def tiles(t, s):
                        for j in range(G + 1):
                            if j < G:
                                tile_norm(G * t + j, j)
                            if j > 0:
                                tile_terms(G * t + j - 1, j - 1)

                    def finish(t, s):
                        for j in range(G):
                            tile_stats(G * t + j)

                    skewed(dve, STEPS, [(0, convolve), (1, tiles), (2, finish)])

                @block.gpsimd
                def _(pool):
                    def residual(n, j):
                        pool.wait_ge(terms_ready, 2 * n + 2)
                        nc.gpsimd.tensor_tensor(high[:, j % 2], high[:, j % 2], low[:, j % 2], ALU.add).then_inc(high_in, 1)
                        pool.wait_ge(high_in, n + 1)
                        nc.gpsimd.tensor_tensor(row_of(R.X, n), row_of(R.X, n), high[:, j % 2], ALU.add).then_inc(x_ready, 2)

                    skewed(pool, NT, [(0, residual)], unroll=4)


def second_order_attention(nc, R, A, C):
    H, DK = 16, 32
    HG = 4
    UT = H // HG
    NU = NT * UT
    with Stage(nc, "so") as st:
        sb, ps, sem = st.sb, st.ps, st.sem
        w = sb("w", [P, 3, HC, H * DK])
        wo = sb("wo", [P, UT, HID])
        upper, lower = sb("upper", [P, P]), sb("lower", [P, P])
        decay_t = sb("decay_t", [P, P])
        to_end, decay = sb("to_end", [P, NT]), sb("decay", [P, NT])
        head = sb("head", [P, HG])
        xn, xnT = sb("xn", [P, HID]), sb("xnT", [P, HID])
        QT, KT = sb("QT", [P, 2, UT, P]), sb("KT", [P, 2, UT, P])
        QTg, KTg = sb("QTg", [P, 2, UT, P]), sb("KTg", [P, 2, UT, P])
        QTs = sb("QTs", [P, 2, UT, HG, P])
        V, K = sb("V", [P, 2, UT, P]), sb("K", [P, 2, UT, P])
        Ke, Qe = sb("Ke", [P, 2, UT, P]), sb("Qe", [P, 2, UT, P])
        M, AT, BT = sb("M", [P, 2, HG, P]), sb("AT", [P, 4, HG, P]), sb("BT", [P, 2, HG, P])
        PT, Us, Ug = sb("PT", [P, 2, HG, P]), sb("Us", [P, 2, HG, P]), sb("Ug", [P, 4, P])
        WT, W, OT = sb("WT", [P, 2, P]), sb("W", [P, 2, P]), sb("OT", [P, 2, UT, P])
        state = sb("state", [P, UT, 3, P])
        b0, b1, bM, bB, bP, bU, bW, bS = (ps(f"bank{i}") for i in range(8))
        names = """loaded zeroed step var_ready std_ready xn_ready xT_done xT_ready QT_done KT_done QT_ready KT_ready V_done K_done
                   V_ready K_ready Q_done Qe_ready Ke_ready Qs_ready Qg_ready Kg_ready M_done M_ready AT_ready B_done BT_ready
                   U_done U_ready P_done PT_ready WT_done WT_ready W_done W_ready O_done O_ready S_done S_ready out_done
                   x_ready U_read""".split()
        s_ = {n: sem(n) for n in names}

        with nc.Block() as block:
            @block.sync
            def _(sp):
                for n, name in enumerate("qkv"):
                    sp.dma_start(w[:, n], A[f"L1_attn_a_W{name}"].rearrange("(c p) d -> p c d", p=P)).then_inc(s_["loaded"], 16)
                sp.dma_start(wo[:], A["L1_attn_a_Wo"].rearrange("(u p) d -> p u d", p=P)).then_inc(s_["loaded"], 16)
                for to, name in ((upper, "upper"), (lower, "lower"), (decay_t, "decay_t"), (to_end, "to_end"), (decay, "decay"), (head, "head")):
                    sp.dma_start(to[:], C[name]).then_inc(s_["loaded"], 16)

            @block.tensor
            def _(pe):
                def T(n, s):
                    return n - s % UT

                def tile_part(n, s):
                    u, par, t4 = s % UT, s // UT, T(n, s)
                    if u == 0:
                        pe.wait_ge(s_["xn_ready"], t4 + 4)
                        if past(n, 4):
                            pe.wait_ge(s_["K_ready"], t4)
                        for c in range(HC):
                            last = pe_t(b0[:, c * P:(c + 1) * P], xn[:, c * P:(c + 1) * P])
                        last.then_inc(s_["xT_done"], 4)
                    elif u == 1:
                        pe.wait_ge(s_["xT_ready"], t4 + 4)
                        if past(n, 4):
                            pe.wait_ge(s_["Qe_ready"], t4)
                        for k in range(UT):
                            for c in range(HC):
                                last = nc.tensor.matmul(b1[:, k * P:(k + 1) * P], w[:, 0, c, k * P:(k + 1) * P], xnT[:, c * P:(c + 1) * P],
                                                        start=(c == 0), stop=(c == HC - 1))
                        last.then_inc(s_["QT_done"], 4)
                        if past(n, 12):
                            pe.wait_ge(s_["x_ready"], t4 - 8)
                        for k in range(UT):
                            for c in range(HC):
                                last = nc.tensor.matmul(b0[:, k * P:(k + 1) * P], w[:, 1, c, k * P:(k + 1) * P], xnT[:, c * P:(c + 1) * P],
                                                        start=(c == 0), stop=(c == HC - 1))
                        last.then_inc(s_["KT_done"], 4)
                    elif u == 2:
                        pe.wait_ge(s_["QT_ready"], t4 + 4)
                        for c in range(HC):
                            last = nc.tensor.matmul(b1[:], xnT[:, c * P:(c + 1) * P], w[:, 2, c, :], start=(c == 0), stop=(c == HC - 1))
                        last.then_inc(s_["V_done"], 4)
                        pe.wait_ge(s_["KT_ready"], t4 + 4)
                        for k in range(UT):
                            last = pe_t(b0[:, k * P:(k + 1) * P], KT[:, par, k])
                        last.then_inc(s_["K_done"], 4)
                    else:
                        pe.wait_ge(s_["V_ready"], t4 + 4)
                        for k in range(UT):
                            last = pe_t(b1[:, k * P:(k + 1) * P], QT[:, par, k])
                        last.then_inc(s_["Q_done"], 4)

                def pe_t(out, in_):
                    return nc.tensor.transpose(out, in_, R.ident[:])

                def keys_queries(n, s):
                    u, par = s % UT, s // UT
                    if u == 0:
                        pe.wait_ge(s_["Qs_ready"], n + 4)
                    if past(n, 1):
                        pe.wait_ge(s_["M_ready"], n)
                    nc.tensor.matmul(bM[:], KT[:, par, u], QTs[:, par, u].rearrange("p h t -> p (h t)"), start=True, stop=True
                                     ).then_inc(s_["M_done"], 1)

                def turn_and_U(n, s):
                    u, par = s % UT, s // UT
                    pe.wait_ge(s_["M_ready"], n + 1)
                    if past(n, 1):
                        pe.wait_ge(s_["BT_ready"], n)
                    for h in range(HG):
                        last = pe_t(bB[:, h * P:(h + 1) * P], M[:, s % 2, h])
                    last.then_inc(s_["B_done"], 1)
                    if u == 0:
                        pe.wait_ge(s_["Qg_ready"], n + 4)
                    pe.wait_ge(s_["AT_ready"], n + 1)
                    if past(n, 4):
                        pe.wait_ge(s_["S_ready"], 4 * (n - 3))
                    if past(n, 3):
                        pe.wait_ge(s_["O_ready"], n - 2)
                    if past(n, 1):
                        pe.wait_ge(s_["U_ready"], n)
                    for h in range(HG):
                        nc.tensor.matmul(bU[h * DK:(h + 1) * DK, 0:P], K[:, par, u, h * DK:(h + 1) * DK], AT[:, s % 4, h],
                                         start=True, stop=False, tile_position=(0, h * DK))
                    nc.tensor.matmul(bU[:, 0:P], state[:, u, 0], QTg[:, par, u], start=False, stop=True).then_inc(s_["U_done"], 1)

                def products_of_U(n, s):
                    u, par = s % UT, s // UT
                    pe.wait_ge(s_["U_ready"], n + 1)
                    if past(n, 1):
                        pe.wait_ge(s_["PT_ready"], n)
                    nc.tensor.matmul(bP[:], QT[:, par, u], Us[:, s % 2].rearrange("p h t -> p (h t)"), start=True, stop=True
                                     ).then_inc(s_["P_done"], 1)
                    pe.wait_ge(s_["BT_ready"], n + 1)
                    if u == 0:
                        pe.wait_ge(s_["Kg_ready"], n + 4)
                    if past(n, 1):
                        pe.wait_ge(s_["W_ready"], n)
                    for h in range(HG):
                        nc.tensor.matmul(bW[h * DK:(h + 1) * DK, 0:P], V[:, par, u, h * DK:(h + 1) * DK], BT[:, s % 2, h],
                                         start=True, stop=False, tile_position=(0, h * DK))
                    nc.tensor.matmul(bW[:, 0:P], state[:, u, 2], KTg[:, par, u], start=False, stop=True).then_inc(s_["WT_done"], 1)

                def turn_W(n, s):
                    pe.wait_ge(s_["WT_ready"], n + 1)
                    pe_t(bW[:, P:2 * P], WT[:, s % 2]).then_inc(s_["W_done"], 1)

                def outputs(n, s):
                    u, par = s % UT, s // UT
                    pe.wait_ge(s_["PT_ready"], n + 1)
                    pe.wait_ge(s_["W_ready"], n + 1)
                    pe.wait_ge(s_["U_ready"], min(n + 3, NU) if isinstance(n, int) else n + 3)
                    for h in range(HG):
                        out = bU[h * DK:(h + 1) * DK, P:2 * P]
                        nc.tensor.matmul(out, V[:, par, u, h * DK:(h + 1) * DK], PT[:, s % 2, h],
                                         start=True, stop=False, tile_position=(0, h * DK))
                        nc.tensor.matmul(out, W[:, s % 2, h * DK:(h + 1) * DK], AT[:, s % 4, h],
                                         start=False, stop=False, tile_position=(0, h * DK))
                    nc.tensor.matmul(bU[:, P:2 * P], state[:, u, 2], Ug[:, s % 4], start=False, stop=False)
                    nc.tensor.matmul(bU[:, P:2 * P], state[:, u, 1], QTg[:, par, u], start=False, stop=True).then_inc(s_["O_done"], 1)
                    pe.wait_ge(s_["Ke_ready"], T(n, s) + 4)
                    pe.wait_ge(s_["Qe_ready"], T(n, s) + 4)
                    if past(n, 1):
                        pe.wait_ge(s_["S_ready"], 4 * n)
                    nc.tensor.matmul(bS[:, 0:P], Ke[:, par, u], K[:, par, u], start=True, stop=True)
                    nc.tensor.matmul(bS[:, P:2 * P], Ke[:, par, u], W[:, s % 2], start=True, stop=True)
                    nc.tensor.matmul(bS[:, 2 * P:3 * P], Qe[:, par, u], V[:, par, u], start=True, stop=True).then_inc(s_["S_done"], 1)

                def mix(n, s):
                    if s % UT != UT - 1:
                        return
                    pe.wait_ge(s_["O_ready"], n + 1)
                    if not isinstance(n, int) or n + 9 < NU:
                        pe.wait_ge(s_["xT_ready"], n + 13)
                    else:
                        pe.wait_ge(s_["K_ready"], NU)
                        pe.wait_ge(s_["x_ready"], n - 3)
                    for u in range(UT):
                        last = nc.tensor.matmul(b0[:, 0:HID], OT[:, s // UT, u], wo[:, u], start=(u == 0), stop=(u == UT - 1))
                    last.then_inc(s_["out_done"], 4)

                pe.wait_ge(s_["loaded"], 160)
                pe.wait_ge(s_["zeroed"], 2)
                skewed(pe, NU, [(7, turn_W), (6, products_of_U), (5, turn_and_U), (4, keys_queries), (0, tile_part), (7, outputs), (9, mix)],
                       unroll=2 * UT)

            @block.scalar
            def _(act):
                std_of_var(nc, act, R, s_["var_ready"], s_["std_ready"])

                def flat(ap):
                    return ap.rearrange("p u t -> p (u t)")

                def copy_out(n, s):
                    act.wait_ge(s_["O_done"], n + 1)
                    if past(n, 8):
                        act.wait_ge(s_["out_done"], n - s % UT - 4)
                    nc.scalar.copy(OT[:, s // UT, s % UT], bU[:, P:2 * P]).then_inc(s_["O_ready"], 1)

                def negate_W(n, s):
                    act.wait_ge(s_["W_done"], n + 1)
                    if past(n, 2):
                        act.wait_ge(s_["S_done"], n - 1)
                    nc.scalar.mul(W[:, s % 2], bW[:, P:2 * P], -1.0).then_inc(s_["W_ready"], 1)

                def copy_WT(n, s):
                    act.wait_ge(s_["WT_done"], n + 1)
                    nc.scalar.copy(WT[:, s % 2], bW[:, 0:P]).then_inc(s_["WT_ready"], 1)

                def copy_M(n, s):
                    act.wait_ge(s_["M_done"], n + 1)
                    if past(n, 2):
                        act.wait_ge(s_["B_done"], n - 1)
                        act.wait_ge(s_["AT_ready"], n - 1)
                    nc.scalar.copy(flat(M[:, s % 2]), bM[:]).then_inc(s_["M_ready"], 1)

                def tile_part(n, s):
                    u, par, t4 = s % UT, s // UT, n - s % UT
                    if u == 0:
                        act.wait_ge(s_["xT_done"], t4 + 4)
                        if past(n, 4):
                            act.wait_ge(s_["V_done"], t4)
                        nc.scalar.copy(xnT[:], b0[:, 0:HID]).then_inc(s_["xT_ready"], 4)
                    elif u == 1:
                        act.wait_ge(s_["QT_done"], t4 + 4)
                        if past(n, 8):
                            act.wait_ge(s_["Qg_ready"], t4 - 4)
                            act.wait_ge(s_["Kg_ready"], t4 - 4)
                            act.wait_ge(s_["Qs_ready"], t4 - 4)
                        nc.scalar.copy(flat(QT[:, par]), b1[:]).then_inc(s_["QT_ready"], 4)
                        act.wait_ge(s_["KT_done"], t4 + 4)
                        nc.scalar.copy(flat(KT[:, par]), b0[:]).then_inc(s_["KT_ready"], 4)
                    elif u == 2:
                        if past(n, 8):
                            act.wait_ge(s_["S_done"], t4 - 4)
                            act.wait_ge(s_["Ke_ready"], t4 - 4)
                        act.wait_ge(s_["V_done"], t4 + 4)
                        nc.scalar.copy(flat(V[:, par]), b1[:]).then_inc(s_["V_ready"], 4)
                        act.wait_ge(s_["K_done"], t4 + 4)
                        nc.scalar.copy(flat(K[:, par]), b0[:]).then_inc(s_["K_ready"], 4)

                skewed(act, NU, [(8, copy_out), (7, negate_W), (4, copy_M), (6, copy_WT), (0, tile_part)], unroll=2 * UT)

            @block.vector
            def _(dve):
                nc.vector.memset(QTs[:], 0.0).then_inc(s_["zeroed"], 1)
                nc.vector.memset(state[:], 0.0).then_inc(s_["zeroed"], 1)
                layernorm_scales(nc, dve, None, R, s_["step"], s_["var_ready"], s_["std_ready"])
                dve.wait_ge(s_["loaded"], 160)

                def spread4(ap):
                    return ap[:, None, :].broadcast_to([P, HG, P])

                def normalize(n, s):
                    if s % UT:
                        return
                    tile = n // UT
                    if past(n, 4):
                        dve.wait_ge(s_["xT_done"], n)
                    nc.vector.tensor_scalar(xn[:], row_of(R.X, tile), R.rstd[:, bass.ds(tile, 1)], R.shift[:, bass.ds(tile, 1)],
                                            ALU.mult, ALU.add).then_inc(s_["xn_ready"], 4)

                def update(n, s):
                    tile = (n - s % UT) // UT
                    dve.wait_ge(s_["S_done"], n + 1)
                    for h in range(HG):
                        rows, cols = slice(h * DK, (h + 1) * DK), slice(h * DK, (h + 1) * DK)
                        old = state[rows, s % UT, :, cols]
                        new = bS[rows, 0:3 * P].rearrange("p (m t) -> p m t", m=3)[:, :, cols]
                        nc.vector.scalar_tensor_tensor(out=old, in0=old, scalar=decay[rows, bass.ds(tile, 1)], in1=new,
                                                       op0=ALU.mult, op1=ALU.add).then_inc(s_["S_ready"], 1)

                def mask_P(n, s):
                    dve.wait_ge(s_["P_done"], n + 1)
                    if past(n, 2):
                        dve.wait_ge(s_["O_done"], n - 1)
                    nc.vector.tensor_tensor(PT[:, s % 2], bP[:].rearrange("p (h t) -> p h t", h=HG), spread4(upper[:]), ALU.mult
                                            ).then_inc(s_["PT_ready"], 1)

                def mask_B(n, s):
                    dve.wait_ge(s_["B_done"], n + 1)
                    if past(n, 2):
                        dve.wait_ge(s_["WT_done"], n - 1)
                    nc.vector.tensor_tensor(BT[:, s % 2], bB[:].rearrange("p (h t) -> p h t", h=HG), spread4(lower[:]), ALU.mult
                                            ).then_inc(s_["BT_ready"], 1)

                def spread_U(n, s):
                    dve.wait_ge(s_["U_done"], n + 1)
                    if past(n, 2):
                        dve.wait_ge(s_["P_done"], n - 1)
                    if past(n, 4):
                        dve.wait_ge(s_["O_done"], n - 3)
                    nc.vector.tensor_tensor(Us[:, s % 2], spread4(bU[:, 0:P]), head[:, :, None].broadcast_to([P, HG, P]), ALU.mult
                                            ).then_inc(s_["U_read"], 1)
                    dve.wait_ge(s_["U_read"], n + 1)
                    nc.vector.tensor_tensor(Ug[:, s % 4], bU[:, 0:P], decay_t[:], ALU.mult).then_inc(s_["U_ready"], 1)

                def tile_part(n, s):
                    u, par, t4 = s % UT, s // UT, n - s % UT
                    if u == 1:
                        dve.wait_ge(s_["QT_ready"], t4 + 4)
                        if past(n, 8):
                            dve.wait_ge(s_["M_done"], t4 - 4)
                        for h in range(HG):
                            rows = slice(h * DK, (h + 1) * DK)
                            nc.vector.tensor_copy(QTs[rows, par, :, h, :], QT[rows, par]).then_inc(s_["Qs_ready"], 1)
                    elif u == 2:
                        dve.wait_ge(s_["K_ready"], t4 + 4)
                        if past(n, 8):
                            dve.wait_ge(s_["S_done"], t4 - 4)
                        nc.vector.tensor_scalar(Ke[:, par], K[:, par], to_end[:, bass.ds(t4 // UT, 1)], None, ALU.mult).then_inc(s_["Ke_ready"], 4)
                    elif u == 3:
                        dve.wait_ge(s_["Q_done"], t4 + 4)
                        if past(n, 8):
                            dve.wait_ge(s_["S_done"], t4 - 4)
                        nc.vector.tensor_scalar(Qe[:, par].rearrange("p u t -> p (u t)"), b1[:], to_end[:, bass.ds(t4 // UT, 1)], None,
                                                ALU.mult).then_inc(s_["Qe_ready"], 4)

                def residual(n, s):
                    if s % UT != UT - 1:
                        return
                    tile = (n - s % UT) // UT
                    dve.wait_ge(s_["out_done"], n + 1)
                    nc.vector.tensor_tensor(row_of(R.X, tile), row_of(R.X, tile), b0[:, 0:HID], ALU.add).then_inc(s_["x_ready"], 4)

                def stats(n, s):
                    if s % UT != UT - 1:
                        return
                    tile = (n - s % UT) // UT
                    dve.wait_ge(s_["x_ready"], n + 1)
                    nc.vector.bn_stats(row_of(R.raw, tile), row_of(R.X, tile))

                skewed(dve, NU, [(0, normalize), (8, update), (6, mask_P), (5, mask_B), (5, spread_U), (1, tile_part), (9, residual), (10, stats)],
                       unroll=2 * UT)

            @block.gpsimd
            def _(pool):
                pool.wait_ge(s_["loaded"], 160)

                def mask_M(n, s):
                    pool.wait_ge(s_["M_ready"], n + 1)
                    if past(n, 4):
                        pool.wait_ge(s_["O_done"], n - 3)
                    nc.gpsimd.tensor_tensor(AT[:, s % 4], M[:, s % 2], upper[:, None, :].broadcast_to([P, HG, P]), ALU.mult
                                            ).then_inc(s_["AT_ready"], 1)

                def tile_part(n, s):
                    if s % UT != 1:
                        return
                    par, t4 = s // UT, n - 1
                    pool.wait_ge(s_["QT_ready"], t4 + 4)
                    if past(n, 8):
                        pool.wait_ge(s_["O_done"], t4 - 4)
                    for to, of, done in ((QTg, QT, "Qg_ready"), (KTg, KT, "Kg_ready")):
                        if of is KT:
                            pool.wait_ge(s_["KT_ready"], t4 + 4)
                        nc.gpsimd.tensor_tensor(to[:, par], of[:, par], decay_t[:, None, :].broadcast_to([P, UT, P]), ALU.mult
                                                ).then_inc(s_[done], 4)

                skewed(pool, NU, [(4, mask_M), (1, tile_part)], unroll=2 * UT)


def window_attention(nc, R, A, C):
    H, D, WIN = 16, 16, 128
    SPAN = 2 * WIN
    PADDED = SEQ + WIN
    PAIRS = H // 2
    NU = NT * PAIRS
    qT_dram = nc.dram_tensor("qT_dram", (BATCH * TB, HID, P), F32).ap()
    kT_dram = nc.dram_tensor("kT_dram", (BATCH, HID, PADDED), F32).ap()
    v_dram = nc.dram_tensor("v_dram", (BATCH, PADDED, HID), F32).ap()
    with Stage(nc, "wa") as st:
        woT = st.sb("woT", [P, HC, HID])
        bank = [st.ps(f"bank{i}") for i in range(8)]

        with Stage(nc, "wp") as p:
            wT = p.sb("wT", [P, HC, 3 * HID])
            bqk, bv_all, zeros = p.sb("bqk", [P, 4]), p.sb("bv_all", [P, HID]), p.sb("zeros", [P, BATCH, HID])
            xn, xnT = p.sb("xn", [P, 2, HID]), p.sb("xnT", [P, 2, HID])
            qk, v = p.sb("qk", [P, 4, 4, P]), p.sb("v", [P, 4, HID])
            names = "loaded zeroed padded step var_ready std_ready xn_ready xT_done xT_ready qk_done v_done qk_ready v_ready".split()
            loaded, zeroed, padded, step, var_ready, std_ready, xn_ready, xT_done, xT_ready, qk_done, v_done, qk_ready, v_ready = (
                p.sem(n) for n in names)
            stored = [p.sem(f"stored{n}") for n in range(4)]
            turned_copies(nc, R, "ww", [(A["L1_attn_b_Wqkv"], wT[:]), (A["L1_attn_b_Wout"], woT[:])], bank[6:8])
            with nc.Block() as block:
                @block.sync
                def _(sp):
                    sp.dma_start(bqk[:], A["L1_attn_b_bqkv"][0:2 * HID].rearrange("(c p) -> p c", p=P),
                                 allow_slow_non_contiguous=True).then_inc(loaded, 16)
                    sp.dma_start(bv_all[:], A["L1_attn_b_bqkv"][2 * HID:3 * HID].rearrange("(a d) -> a d", a=1).broadcast_to([P, HID])
                                 ).then_inc(loaded, 16)
                    sp.wait_ge(zeroed, 1)
                    for side in (0, PADDED - WIN // 2):
                        edge = slice(side, side + WIN // 2)
                        for c in range(HC):
                            sp.dma_start(kT_dram[:, c * P:(c + 1) * P, edge].rearrange("b p t -> p b t"), zeros[:, :, 0:WIN // 2]
                                         ).then_inc(padded, 16)
                        sp.dma_start(v_dram[:, edge, :].rearrange("b t d -> t b d"), zeros[0:WIN // 2]).then_inc(padded, 16)

                    def store(b, j, s):
                        n = b * TB + j
                        at = bass.ds(j * P + WIN // 2, P)
                        sp.wait_ge(qk_ready, n + 1)
                        sp.dma_start(qT_dram[bass.ds(n, 1)].rearrange("a (c p) t -> p (a c) t", p=P), qk[:, s, 0:2]).then_inc(stored[s], 16)
                        sp.dma_start(kT_dram[bass.ds(b, 1), :, at].rearrange("a (c p) t -> p (a c) t", p=P), qk[:, s, 2:4]).then_inc(stored[s], 16)
                        sp.wait_ge(v_ready, n + 1)
                        sp.dma_start(v_dram[bass.ds(b, 1), at, :].rearrange("a t d -> (a t) d"), v[:, s]).then_inc(stored[s], 16)

                    with sp.Fori(0, BATCH) as b:
                        for j in range(TB):
                            store(b, j, j % 4)
                    sp.wait_ge(padded, 96)
                    for n in range(4):
                        sp.wait_ge(stored[n], 48 * NT // 4)

                @block.tensor
                def _(pe):
                    def turn_x(i, s):
                        s %= 2
                        pe.wait_ge(xn_ready, i + 1)
                        if past(i, 2):
                            pe.wait_ge(xT_ready, i - 1)
                        for c in range(HC):
                            last = nc.tensor.transpose(bank[s][:, c * P:(c + 1) * P], xn[:, s, c * P:(c + 1) * P], R.ident[:])
                        last.then_inc(xT_done, 1)

                    def project(i, s):
                        s %= 2
                        pe.wait_ge(xT_ready, i + 1)
                        if past(i, 2):
                            pe.wait_ge(qk_ready, i - 1)
                            pe.wait_ge(v_ready, i - 1)
                        for e in range(4):
                            for c in range(HC):
                                last = nc.tensor.matmul(bank[2 + s][:, e * P:(e + 1) * P], wT[:, c, e * P:(e + 1) * P],
                                                        xnT[:, s, c * P:(c + 1) * P], start=(c == 0), stop=(c == HC - 1))
                        last.then_inc(qk_done, 1)
                        for c in range(HC):
                            last = nc.tensor.matmul(bank[4 + s][:, 0:HID], xnT[:, s, c * P:(c + 1) * P], wT[:, c, 2 * HID:3 * HID],
                                                    start=(c == 0), stop=(c == HC - 1))
                        last.then_inc(v_done, 1)

                    skewed(pe, NT, [(0, turn_x), (1, project)], unroll=4)

                @block.scalar
                def _(act):
                    std_of_var(nc, act, R, var_ready, std_ready)

                    def copy_xT(i, s):
                        s %= 2
                        act.wait_ge(xT_done, i + 1)
                        if past(i, 2):
                            act.wait_ge(v_done, i - 1)
                        nc.scalar.copy(xnT[:, s], bank[s][:, 0:HID]).then_inc(xT_ready, 1)

                    skewed(act, NT, [(0, copy_xT)], unroll=4)

                @block.vector
                def _(dve):
                    nc.vector.memset(zeros[:], 0.0).then_inc(zeroed, 1)
                    layernorm_scales(nc, dve, None, R, step, var_ready, std_ready)
                    dve.wait_ge(loaded, 32)

                    def normalize(i, s):
                        s %= 2
                        if past(i, 2):
                            dve.wait_ge(xT_done, i - 1)
                        nc.vector.tensor_scalar(xn[:, s], row_of(R.X, i), R.rstd[:, bass.ds(i, 1)], R.shift[:, bass.ds(i, 1)],
                                                ALU.mult, ALU.add).then_inc(xn_ready, 1)

                    def add_bias(i, s):
                        if past(i, 4):
                            dve.wait_ge(stored[s], 12 * (i - s))
                        dve.wait_ge(qk_done, i + 1)
                        nc.vector.tensor_tensor(qk[:, s], bank[2 + s % 2][:].rearrange("p (e t) -> p e t", e=4),
                                                bqk[:, :, None].broadcast_to([P, 4, P]), ALU.add).then_inc(qk_ready, 1)
                        dve.wait_ge(v_done, i + 1)
                        nc.vector.tensor_tensor(v[:, s], bank[4 + s % 2][:, 0:HID], bv_all[:], ALU.add).then_inc(v_ready, 1)

                    skewed(dve, NT, [(0, normalize), (1, add_bias)], unroll=4)

        with Stage(nc, "wq") as q:
            sb, sem = q.sb, q.sem
            KTw, Vw, QTw = sb("KTw", [P, 2, HC, SPAN]), sb("Vw", [P, 2, 2, HID]), sb("QTw", [P, 2, HC, P])
            QTs = sb("QTs", [P, 2, H, P])
            band, head, bo_all = sb("band", [P, SPAN]), sb("head", [P, PAIRS]), sb("bo_all", [P, HID])
            S, prob, probT = sb("S", [P, 2, 2, SPAN]), sb("prob", [P, 2, 2, SPAN]), sb("probT", [P, 2, 2, 2, P])
            top, shift, sums, share = sb("top", [P, 2, 2]), sb("shift", [P, 2, 2]), sb("sums", [P, 2, H]), sb("share", [P, H])
            OT2, O, OT, y = sb("OT2", [P, 4, P]), sb("O", [P, HID]), sb("OT", [P, HID]), sb("y", [P, 2, HID])
            bS, bT, bO, bU, bV = bank[0:2], bank[2:4], bank[4:6], bank[6], bank[7]
            names = """loaded S_done top_ready shift_ready prob_ready T_done T_ready PV_done Qs_ready OT2_ready back_done share_ready O_ready
                       turn_done OT_ready out_done y_ready x_ready""".split()
            s_ = {n: sem(n) for n in names}
            kv_in, q_in = [sem(f"kv_in{n}") for n in range(2)], [sem(f"q_in{n}") for n in range(2)]
            U = 2 * PAIRS
            with nc.Block() as block:
                @block.sync
                def _(sp):
                    sp.dma_start(band[:], C["band"]).then_inc(s_["loaded"], 16)
                    sp.dma_start(head[:], C["head16"]).then_inc(s_["loaded"], 16)
                    sp.dma_start(bo_all[:], A["L1_attn_b_bout"].rearrange("(a d) -> a d", a=1).broadcast_to([P, HID])).then_inc(s_["loaded"], 16)

                    def load(b, j, s, waits):
                        i = b * TB + j
                        if waits:
                            sp.wait_ge(s_["Qs_ready"], PAIRS * (i - 1))
                            sp.wait_ge(s_["PV_done"], PAIRS * (i - 1))
                        sp.dma_start(QTw[:, s], qT_dram[bass.ds(i, 1)].rearrange("a (c p) t -> p (a c) t", p=P)).then_inc(q_in[s], 16)
                        sp.dma_start(KTw[:, s], kT_dram[bass.ds(b, 1), :, bass.ds(j * P, SPAN)].rearrange("a (c p) t -> p (a c) t", p=P)
                                     ).then_inc(kv_in[s], 16)
                        sp.dma_start(Vw[:, s], v_dram[bass.ds(b, 1), bass.ds(j * P, SPAN), :].rearrange("a (k p) d -> p (a k) d", p=P)
                                     ).then_inc(kv_in[s], 16)

                    for j in range(TB):
                        load(0, j, j % 2, j >= 2)
                    with sp.Fori(1, BATCH) as b:
                        for j in range(TB):
                            load(b, j, j % 2, True)

                @block.gpsimd
                def _(pool):
                    pool.wait_ge(s_["loaded"], 48)

                    def spread(i, s):
                        pool.wait_ge(q_in[s], 8 * (i - s) + 16)
                        if past(i, 2):
                            pool.wait_ge(s_["S_done"], PAIRS * (i - 1))
                        for c in range(HC):
                            nc.gpsimd.tensor_tensor(QTs[:, s, PAIRS * c:PAIRS * (c + 1)], QTw[:, s, c:c + 1, :].broadcast_to([P, PAIRS, P]),
                                                    head[:, :, None].broadcast_to([P, PAIRS, P]), ALU.mult).then_inc(s_["Qs_ready"], PAIRS // 2)

                    def residual(i, s):
                        pool.wait_ge(s_["y_ready"], PAIRS * (i + 1))
                        nc.gpsimd.tensor_tensor(row_of(R.X, i), row_of(R.X, i), y[:, s], ALU.add).then_inc(s_["x_ready"], PAIRS)

                    skewed(pool, NT, [(0, spread), (2, residual)])

                @block.tensor
                def _(pe):
                    pe.wait_ge(s_["loaded"], 48)

                    def scores(n, s):
                        m, par = s % PAIRS, s // PAIRS
                        if m == 0:
                            pe.wait_ge(kv_in[par], (n - s) * 2 + 32)
                            pe.wait_ge(s_["Qs_ready"], n + PAIRS)
                        if past(n, 2):
                            pe.wait_ge(s_["top_ready"], n - 1)
                        for h in range(2):
                            last = nc.tensor.matmul(bS[s % 2][:, h * SPAN:(h + 1) * SPAN], QTs[:, par, 2 * m + h, :], KTw[:, par, m // 4, :],
                                                    start=True, stop=True)
                        last.then_inc(s_["S_done"], 1)

                    def turn(n, s):
                        pe.wait_ge(s_["prob_ready"], 2 * n + 2)
                        if past(n, 2):
                            pe.wait_ge(s_["T_ready"], n - 1)
                        for h in range(2):
                            for k in range(2):
                                last = nc.tensor.transpose(bT[s % 2][:, (2 * h + k) * P:(2 * h + k + 1) * P],
                                                           prob[:, s % 2, h, k * P:(k + 1) * P], R.ident[:])
                        last.then_inc(s_["T_done"], 1)

                    def weigh(n, s):
                        m, par = s % PAIRS, s // PAIRS
                        pe.wait_ge(s_["T_ready"], n + 1)
                        if m == 0 and past(n, U):
                            pe.wait_ge(s_["OT2_ready"], n - PAIRS)
                        rows = slice(32 * (m % 4), 32 * (m % 4) + 32)
                        for h in range(2):
                            for k in range(2):
                                cols = (2 * (m // 4) + h) * P
                                last = nc.tensor.matmul(bO[par][rows, cols:cols + P], Vw[:, par, k, 32 * m:32 * m + 32],
                                                        probT[:, s % 2, h, k, :], start=(k == 0), stop=(k == 1),
                                                        tile_position=(0, 32 * (m % 4)))
                        last.then_inc(s_["PV_done"], 1)

                    def last_of_tile(f):
                        def run(n, s):
                            if s % PAIRS == PAIRS - 1:
                                f(n + 1 - PAIRS, s // PAIRS)
                        return run

                    def back(i, par):
                        pe.wait_ge(s_["OT2_ready"], i + PAIRS)
                        if past(i, 1):
                            pe.wait_ge(s_["O_ready"], i)
                        for k in range(4):
                            last = nc.tensor.transpose(bU[:, k * P:(k + 1) * P], OT2[:, k, :], R.ident[:])
                        last.then_inc(s_["back_done"], PAIRS)

                    def turn_O(i, par):
                        pe.wait_ge(s_["O_ready"], i + PAIRS)
                        if past(i, 1):
                            pe.wait_ge(s_["y_ready"], i)
                        for c in range(HC):
                            last = nc.tensor.transpose(bV[:, c * P:(c + 1) * P], O[:, c * P:(c + 1) * P], R.ident[:])
                        last.then_inc(s_["turn_done"], PAIRS)

                    def mix(i, par):
                        pe.wait_ge(s_["OT_ready"], i + PAIRS)
                        for c in range(HC):
                            last = nc.tensor.matmul(bV[:, HID:2 * HID], OT[:, c * P:(c + 1) * P], woT[:, c, :], start=(c == 0), stop=(c == HC - 1))
                        last.then_inc(s_["out_done"], PAIRS)

                    skewed(pe, NU, [(3, weigh), (2, turn), (0, scores), (5, last_of_tile(back)), (6, last_of_tile(turn_O)),
                                    (7, last_of_tile(mix))], unroll=U)

                @block.scalar
                def _(act):
                    def exponent(n, s):
                        m, par = s % PAIRS, s // PAIRS
                        act.wait_ge(s_["shift_ready"], n + 1)
                        if past(n, 2):
                            act.wait_ge(s_["T_done"], n - 1)
                        if m == 0 and past(n, U):
                            act.wait_ge(s_["share_ready"], n - PAIRS)
                        for h in range(2):
                            nc.scalar.activation(prob[:, s % 2, h], S[:, s % 2, h], ACT.Exp, bias=shift[:, s % 2, h:h + 1], scale=D ** -0.5,
                                                 accum_out=sums[:, par, 2 * m + h:2 * m + h + 1]).then_inc(s_["prob_ready"], 1)

                    def copy_O(n, s):
                        if s % PAIRS == PAIRS - 1:
                            act.wait_ge(s_["PV_done"], n + 1)
                            if past(n, PAIRS):
                                act.wait_ge(s_["back_done"], n + 1 - PAIRS)
                            nc.scalar.copy(OT2[:].rearrange("p k t -> p (k t)"), bO[s // PAIRS][:]).then_inc(s_["OT2_ready"], PAIRS)

                    def copy_OT(n, s):
                        if s % PAIRS == PAIRS - 1:
                            act.wait_ge(s_["turn_done"], n + 1)
                            if past(n, PAIRS):
                                act.wait_ge(s_["out_done"], n + 1 - PAIRS)
                            nc.scalar.copy(OT[:], bV[:, 0:HID]).then_inc(s_["OT_ready"], PAIRS)

                    skewed(act, NU, [(1, exponent), (4, copy_O), (6, copy_OT)], unroll=U)

                @block.vector
                def _(dve):
                    dve.wait_ge(s_["loaded"], 48)

                    def mask(n, s):
                        dve.wait_ge(s_["S_done"], n + 1)
                        if past(n, 2):
                            dve.wait_ge(s_["prob_ready"], 2 * (n - 1))
                        nc.vector.memset(R.turnstile[:], 0.0)
                        for h in range(2):
                            ins = nc.vector.tensor_tensor_reduce(out=S[:, s % 2, h], in0=bS[s % 2][:, h * SPAN:(h + 1) * SPAN], in1=band[:],
                                                                 scale=1.0, scalar=-3e38, op0=ALU.add, op1=ALU.max,
                                                                 accum_out=top[:, s % 2, h:h + 1])
                        ins.then_inc(s_["top_ready"], 1)
                        dve.wait_ge(s_["top_ready"], n + 1)
                        nc.vector.tensor_scalar(shift[:, s % 2], top[:, s % 2], -(D ** -0.5), None, ALU.mult).then_inc(s_["shift_ready"], 1)

                    def copy_T(n, s):
                        dve.wait_ge(s_["T_done"], n + 1)
                        if past(n, 2):
                            dve.wait_ge(s_["PV_done"], n - 1)
                        nc.vector.tensor_copy(probT[:, s % 2].rearrange("p h k t -> p (h k t)"), bT[s % 2][:]).then_inc(s_["T_ready"], 1)

                    def normalize(n, s):
                        if s % PAIRS != PAIRS - 1:
                            return
                        par = s // PAIRS
                        dve.wait_ge(s_["prob_ready"], 2 * n + 2)
                        if past(n, PAIRS):
                            dve.wait_ge(s_["O_ready"], n + 1 - PAIRS)
                        nc.vector.reciprocal(share[:], sums[:, par]).then_inc(s_["share_ready"], PAIRS)
                        dve.wait_ge(s_["share_ready"], n + 1)
                        dve.wait_ge(s_["back_done"], n + 1)
                        if past(n, PAIRS):
                            dve.wait_ge(s_["turn_done"], n + 1 - PAIRS)
                        for h in range(2):
                            nc.vector.tensor_tensor(
                                O[:].rearrange("p (c m h d) -> p c m h d", c=2, m=4, h=2)[:, :, :, h, :],
                                bU[:].rearrange("p (c g m h d) -> p c g m h d", c=2, g=2, m=4, h=2)[:, :, h, :, h, :],
                                share[:].rearrange("p (c m h) -> p c m h", c=2, m=4)[:, :, :, h, None].broadcast_to([P, 2, 4, D]),
                                ALU.mult).then_inc(s_["O_ready"], PAIRS // 2)

                    def add_bias(n, s):
                        if s % PAIRS != PAIRS - 1:
                            return
                        par = s // PAIRS
                        dve.wait_ge(s_["out_done"], n + 1)
                        if past(n, U):
                            dve.wait_ge(s_["x_ready"], n + 1 - U)
                        nc.vector.tensor_tensor(y[:, par], bV[:, HID:2 * HID], bo_all[:], ALU.add).then_inc(s_["y_ready"], PAIRS)

                    def stats(n, s):
                        if s % PAIRS != PAIRS - 1:
                            return
                        i = (n - PAIRS + 1) // PAIRS
                        dve.wait_ge(s_["x_ready"], n + 1)
                        nc.vector.bn_stats(row_of(R.raw, i), row_of(R.X, i))

                    skewed(dve, NU, [(0, mask), (2, copy_T), (5, normalize), (7, add_bias), (9, stats)], unroll=U)


def local_attention(nc, R, A, C, sem_):
    def sem(name):
        return sem_(f"la_{name}")

    with ExitStack() as ctx:
        def sb(name, shape, dt=F32):
            return ctx.enter_context(nc.sbuf_tensor(f"la_{name}", shape, dt))

        def ps(name, shape, dt=F32):
            return ctx.enter_context(nc.psum_tensor(f"la_{name}", shape, dt))

        w = sb("w", [P, 3, HC, HID])
        wT = sb("wT", [P, 3, HC, HID])
        bqk = sb("bqk", [P, 4])
        bv_all = sb("bv_all", [P, HID])
        mask = sb("mask", [P, P])
        xn = sb("xn", [P, 2, HID])
        xnT = sb("xnT", [P, 2, HID])
        qkT = sb("qkT", [P, 2, 4, P])
        v = sb("v", [P, 4, HID])
        S = sb("S", [P, 2, P])
        prob = sb("prob", [P, 2, P])
        probT = sb("probT", [P, 2, P])
        top, total, share = sb("top", [P, 4]), sb("total", [P, 4]), sb("share", [P, 4])
        ps_xT = [ps(f"ps_xT{i}", [P, 2 * HID]) for i in range(2)]
        ps_qk = [ps(f"ps_qk{i}", [P, 4, P]) for i in range(2)]
        ps_v = ps("ps_v", [P, 2 * HID])
        ps_S = ps("ps_S", [P, 4, P])
        ps_pT = ps("ps_pT", [P, 4, P])
        ps_o = ps("ps_o", [P, 2 * HID])

        loaded, w_turned, w_ready = sem("loaded"), sem("w_turned"), sem("w_ready")
        step, var_ready, std_ready = sem("step"), sem("var_ready"), sem("std_ready")
        xn_ready, xT_done, xT_ready = sem("xn_ready"), sem("xT_done"), sem("xT_ready")
        qk_done, v_done, qk_ready, v_ready = sem("qk_done"), sem("v_done"), sem("qk_ready"), sem("v_ready")
        S_done, masked, top_ready, prob_ready = sem("S_done"), sem("masked"), sem("top_ready"), sem("prob_ready")
        pT_done, pT_ready, o_done = sem("pT_done"), sem("pT_ready"), sem("o_done")
        share_ready, x_ready, stats_done = sem("share_ready"), sem("x_ready"), sem("stats_done")

        with nc.Block() as block:
            @block.sync
            def _(sp):
                for n, name in enumerate("qkv"):
                    sp.dma_start(w[:, n], A[f"L0_attn_a_W{name}"].rearrange("(c p) d -> p c d", p=P)).then_inc(loaded, 16)
                for n, name in enumerate("qk"):
                    sp.dma_start(bqk[:, 2 * n:2 * n + 2], A[f"L0_attn_a_b{name}"].rearrange("(c p) -> p c", p=P),
                                 allow_slow_non_contiguous=True).then_inc(loaded, 16)
                sp.dma_start(bv_all[:], A["L0_attn_a_bv"].rearrange("(a d) -> a d", a=1).broadcast_to([P, HID])).then_inc(loaded, 16)
                sp.dma_start(mask[:], C["group_mask"]).then_inc(loaded, 16)

            @block.tensor
            def _(pe):
                pe.wait_ge(loaded, 7 * 16)
                for n in range(3):
                    if n == 2:
                        pe.wait_ge(w_ready, 1)
                    for c in range(HC):
                        for h in range(HC):
                            last = nc.tensor.transpose(ps_qk[n % 2][:, 2 * h + c, :], w[:, n, c, h * P:(h + 1) * P], R.ident[:])
                    last.then_inc(w_turned, 1)
                pe.wait_ge(w_ready, 3)

                def turn_x(i, s):
                    s %= 2
                    pe.wait_ge(xn_ready, i + 1)
                    if past(i, 2):
                        pe.wait_ge(xT_ready, i - 1)
                    for c in range(HC):
                        last = nc.tensor.transpose(ps_xT[s][:, c * P:(c + 1) * P], xn[:, s, c * P:(c + 1) * P], R.ident[:])
                    last.then_inc(xT_done, 1)

                def project(i, s):
                    s %= 2
                    pe.wait_ge(xT_ready, i + 1)
                    if past(i, 2):
                        pe.wait_ge(qk_ready, i - 1)
                    for n in range(2):
                        for e in range(HC):
                            for c in range(HC):
                                last = nc.tensor.matmul(ps_qk[s][:, 2 * n + e, :], wT[:, n, c, e * P:(e + 1) * P],
                                                        xnT[:, s, c * P:(c + 1) * P], start=(c == 0), stop=(c == HC - 1))
                    last.then_inc(qk_done, 1)
                    if past(i, 1):
                        pe.wait_ge(v_ready, i)
                    for c in range(HC):
                        last = nc.tensor.matmul(ps_v[:, 0:HID], xnT[:, s, c * P:(c + 1) * P], wT[:, 2, c, :],
                                                start=(c == 0), stop=(c == HC - 1))
                    last.then_inc(v_done, 1)

                def scores(i, s):
                    s %= 2
                    pe.wait_ge(qk_ready, i + 1)
                    if past(i, 1):
                        pe.wait_ge(masked, i)
                    for e in range(HC):
                        last = nc.tensor.matmul(ps_S[:, 0, :], qkT[:, s, e, :], qkT[:, s, 2 + e, :],
                                                start=(e == 0), stop=(e == HC - 1))
                    last.then_inc(S_done, 1)

                def turn_p(i, s):
                    pe.wait_ge(prob_ready, i + 1)
                    if past(i, 1):
                        pe.wait_ge(pT_ready, i)
                    nc.tensor.transpose(ps_pT[:, 0, :], prob[:, s % 2, :], R.ident[:]).then_inc(pT_done, 1)

                def weigh(i, s):
                    pe.wait_ge(pT_ready, i + 1)
                    pe.wait_ge(v_ready, i + 1)
                    if past(i, 1):
                        pe.wait_ge(x_ready, i)
                    nc.tensor.matmul(ps_o[:, 0:HID], probT[:, s % 2, :], v[:, s, :], start=True, stop=True).then_inc(o_done, 1)

                skewed(pe, NT, [(4, weigh), (3, turn_p), (2, scores), (0, turn_x), (1, project)], unroll=4)

            @block.scalar
            def _(act):
                std_of_var(nc, act, R, var_ready, std_ready)
                for n in range(3):
                    act.wait_ge(w_turned, n + 1)
                    nc.scalar.copy(wT[:, n].rearrange("p c d -> p (c d)"), ps_qk[n % 2][:].rearrange("p a b -> p (a b)")).then_inc(w_ready, 1)

                def copy_xT(i, s):
                    s %= 2
                    act.wait_ge(xT_done, i + 1)
                    if past(i, 2):
                        act.wait_ge(v_done, i - 1)
                    nc.scalar.copy(xnT[:, s], ps_xT[s][:, 0:HID]).then_inc(xT_ready, 1)

                def exponent(i, s):
                    s %= 2
                    act.wait_ge(top_ready, i + 1)
                    if past(i, 2):
                        act.wait_ge(pT_done, i - 1)
                        act.wait_ge(x_ready, i - 1)
                    nc.scalar.activation(prob[:, s], S[:, s], ACT.Exp, bias=top[:, s + 2:s + 3],
                                         accum_out=total[:, s:s + 1]).then_inc(prob_ready, 1)

                def copy_pT(i, s):
                    s %= 2
                    act.wait_ge(pT_done, i + 1)
                    if past(i, 2):
                        act.wait_ge(o_done, i - 1)
                    nc.scalar.copy(probT[:, s], ps_pT[:, 0]).then_inc(pT_ready, 1)

                skewed(act, NT, [(0, copy_xT), (3, copy_pT), (2, exponent)], unroll=4)

            @block.vector
            def _(dve):
                layernorm_scales(nc, dve, None, R, step, var_ready, std_ready)
                dve.wait_ge(loaded, 7 * 16)

                def normalize(i, s):
                    s %= 2
                    if past(i, 2):
                        dve.wait_ge(xT_done, i - 1)
                    nc.vector.tensor_scalar(xn[:, s], row_of(R.X, i), R.rstd[:, bass.ds(i, 1)], R.shift[:, bass.ds(i, 1)],
                                            ALU.mult, ALU.add).then_inc(xn_ready, 1)

                def copy_qk(i, s):
                    s %= 2
                    dve.wait_ge(qk_done, i + 1)
                    if past(i, 2):
                        dve.wait_ge(S_done, i - 1)
                    nc.vector.tensor_tensor(qkT[:, s], ps_qk[s][:], bqk[:, :, None].broadcast_to([P, 4, P]), ALU.add).then_inc(qk_ready, 1)

                def copy_v(i, s):
                    dve.wait_ge(v_done, i + 1)
                    if past(i, 4):
                        dve.wait_ge(o_done, i - 3)
                    nc.vector.tensor_tensor(v[:, s], ps_v[:, 0:HID], bv_all[:], ALU.add).then_inc(v_ready, 1)

                def mask_S(i, s):
                    s %= 2
                    dve.wait_ge(S_done, i + 1)
                    if past(i, 2):
                        dve.wait_ge(prob_ready, i - 1)
                    nc.vector.memset(R.turnstile[:], 0.0)
                    nc.vector.tensor_tensor_reduce(out=S[:, s], in0=ps_S[:, 0], in1=mask[:], scale=1.0, scalar=-3e38,
                                                   op0=ALU.add, op1=ALU.max, accum_out=top[:, s:s + 1]).then_inc(masked, 1)
                    dve.wait_ge(masked, i + 1)
                    nc.vector.tensor_scalar(top[:, s + 2:s + 3], top[:, s:s + 1], -1.0, None, ALU.mult).then_inc(top_ready, 1)

                def residual(i, s):
                    s %= 2
                    dve.wait_ge(prob_ready, i + 1)
                    nc.vector.reciprocal(share[:, s:s + 1], total[:, s:s + 1]).then_inc(share_ready, 1)
                    dve.wait_ge(o_done, i + 1)
                    dve.wait_ge(share_ready, i + 1)
                    nc.vector.scalar_tensor_tensor(out=row_of(R.X, i), in0=ps_o[:, 0:HID], scalar=share[:, s:s + 1],
                                                   in1=row_of(R.X, i), op0=ALU.mult, op1=ALU.add).then_inc(x_ready, 1)

                def stats(i, s):
                    dve.wait_ge(x_ready, i + 1)
                    nc.vector.bn_stats(row_of(R.raw, i), row_of(R.X, i))

                skewed(dve, NT, [(0, normalize), (2, mask_S), (1, copy_qk), (1, copy_v), (4, residual), (5, stats)], unroll=4)


class Resident:
    pass


def hybrid_kernel(nc, A, C, out):
    with ExitStack() as ctx:
        def sem(name):
            return ctx.enter_context(nc.semaphore(name))

        def sb(name, shape, dt=F32):
            return ctx.enter_context(nc.sbuf_tensor(name, shape, dt))

        R = Resident()
        R.fetched = [sem(f"fetched{n}") for n in range(4)]
        R.scattered = [sem(f"scattered{b}") for b in range(BATCH)]
        R.X = sb("X", [P, NT, HID])
        R.raw = sb("raw", [P, NT, 6])
        R.mean, R.var, R.rstd = sb("mean", [P, NT]), sb("var", [P, NT]), sb("rstd", [P, NT])
        R.shift, R.diff = sb("shift", [P, NT]), sb("diff", [P, NT])
        R.ident = sb("ident", [P, P])
        R.turnstile = sb("turnstile", [1, 1])
        made = sem("ident_made")
        with nc.Block() as block:
            @block.gpsimd
            def _(pool):
                nc.gpsimd.memset(R.ident[:], 0.0).then_inc(made, 1)
                pool.wait_ge(made, 1)
                nc.gpsimd.affine_select(out=R.ident[:], in_=R.ident[:], compare_op=ALU.not_equal, fill=1.0,
                                        base=0, pattern=[[-1, P]], channel_multiplier=1)
        R.xn_dram = nc.dram_tensor("xn_dram", (BATCH * SEQ, HID), F32).ap()
        R.sum_dram = nc.dram_tensor("sum_dram", (BATCH * SEQ, HID), F32).ap()
        R.gate_dram = nc.dram_tensor("gate_dram", (P, HID), F32).ap()
        reload_x(nc, R, "in", A["L0_attn_a_x"].rearrange("b s d -> (b s) d"))
        local_attention(nc, R, A, C, sem)
        top_k_experts(nc, R, "m2", A, C, 0)
        spectral_attention(nc, R, A, C)
        top_k_experts(nc, R, "m4", A, C, 1)
        second_order_attention(nc, R, A, C)
        tanh_ffn(nc, R, "t6", sem, A["L1_ffn_weight"], A["L1_ffn_aux_weight1"], A["L1_ffn_aux_weight2"], A["L1_ffn_bias"])
        window_attention(nc, R, A, C)
        tanh_ffn(nc, R, "t8", sem, A["L1_ffn_weight"], A["L1_ffn_aux_weight1"], A["L1_ffn_aux_weight2"], A["L1_ffn_bias"])
        store_x(nc, R, out, sem)


def shape_constants():
    token = np.arange(P)
    same = (token[:, None] // 64) == (token[None, :] // 64)
    n, f = np.arange(64), np.arange(33)
    angle = 2 * np.pi * (np.outer(n, f) % 64) / 64
    cos, sin = np.cos(angle), np.sin(angle)
    sin[:, [0, 32]] = 0.0
    forward = np.concatenate([cos, -sin], axis=1)
    dft = np.kron(np.eye(2), forward)
    twice = np.where((f == 0) | (f == 32), 1.0, 2.0)[:, None] / 64
    inv = [cos.T * twice, -sin.T * twice]
    inv_high = np.zeros((P, P))
    for r in range(2):
        for h in range(2):
            inv_high[64 * r + 29 * h:64 * r + 29 * (h + 1), 64 * h:64 * (h + 1)] = inv[r][4:]
    inv_low = np.zeros((P, TB, P))
    for r in range(2):
        for chunk in range(16):
            inv_low[64 * r + 4 * chunk:64 * r + 4 * chunk + 4, chunk // 2, 64 * (chunk % 2):64 * (chunk % 2) + 64] = inv[r][:4]
    low_pass = np.kron(np.eye(2), -(forward[:, :4] @ inv[0][:4] + forward[:, 33:37] @ inv[1][:4]))
    chunk = np.arange(64) // 4
    chunk_mask = np.tile(np.where(chunk[:, None] >= chunk[None, :], 0.0, -1e30), (2, 1))
    gamma, place = 0.99, np.arange(P)
    power = gamma ** (place[None, :] - place[:, None]).astype(np.float64)
    last = (np.arange(NT) % TB == TB - 1)[None, :]
    ahead = np.arange(2 * P)[None, :] - place[:, None]
    return {
        "band": np.where((ahead >= 0) & (ahead < P), 0.0, -1e30).astype(np.float32),
        "head16": (place[:, None] // 16 == np.arange(8)[None, :]).astype(np.float32),
        "upper": np.triu(power).astype(np.float32),
        "lower": np.triu(power, 1).astype(np.float32),
        "decay_t": np.tile(gamma ** (place + 1.0), (P, 1)).astype(np.float32),
        "to_end": np.where(last, 0.0, gamma ** (P - 1.0 - place)[:, None]).astype(np.float32),
        "decay": np.tile(np.where(last, 0.0, gamma ** P), (P, 1)).astype(np.float32),
        "head": (place[:, None] // 32 == np.arange(4)[None, :]).astype(np.float32),
        "dft": dft.astype(np.float32),
        "inv_high": inv_high.astype(np.float32),
        "inv_low": inv_low.astype(np.float32),
        "low_pass": low_pass.astype(np.float32),
        "chunk_mask": chunk_mask.astype(np.float32),
        "row_base": (np.arange(64) // 8 * SEQ).astype(np.float32)[:, None],
        "group_mask": np.where(same, 0.0, -1e30).astype(np.float32),
    }


_INS = ['L0_attn_a_x', 'L0_attn_a_Wq', 'L0_attn_a_bq', 'L0_attn_a_Wk', 'L0_attn_a_bk', 'L0_attn_a_Wv', 'L0_attn_a_bv',
        'L0_attn_b_q_w', 'L0_attn_b_k_w', 'L0_attn_b_v_w', 'L0_attn_b_o_w', 'L0_attn_b_dw_r', 'L0_attn_b_pw_r',
        'L0_attn_b_dw_i', 'L0_attn_b_pw_i', 'L0_attn_b_gate_w', 'L0_attn_b_alpha_raw', 'L0_ffn_Wg', 'L0_ffn_W1',
        'L0_ffn_b1', 'L0_ffn_W2', 'L0_ffn_b2', 'L1_attn_a_Wq', 'L1_attn_a_Wk', 'L1_attn_a_Wv', 'L1_attn_a_Wo',
        'L1_attn_b_Wqkv', 'L1_attn_b_bqkv', 'L1_attn_b_Wout', 'L1_attn_b_bout', 'L1_ffn_weight',
        'L1_ffn_aux_weight1', 'L1_ffn_aux_weight2', 'L1_ffn_bias']


def kernel(**inputs):
    import numpy as _np
    import concourse.bacc as _bacc
    from concourse import mybir as _mybir
    from concourse.bass_utils import run_bass_kernel_spmd as _run

    nc = _bacc.Bacc("TRN2", target_bir_lowering=False, num_devices=1)
    arrays, args = {}, {}
    for name in _INS:
        a = _np.ascontiguousarray(inputs[name])
        arrays[f"in_{name}_dram"] = a
        args[name] = nc.dram_tensor(f"in_{name}_dram", a.shape, _mybir.dt.from_np(a.dtype), kind="ExternalInput").ap()
    out = nc.dram_tensor("out_0_dram", (BATCH, SEQ, HID), _mybir.dt.float32, kind="ExternalOutput").ap()
    constants = {}
    for name, a in shape_constants().items():
        arrays[f"in_{name}_dram"] = a
        constants[name] = nc.dram_tensor(f"in_{name}_dram", a.shape, _mybir.dt.from_np(a.dtype), kind="ExternalInput").ap()
    hybrid_kernel(nc, args, constants, out)
    r = _run(nc, [arrays], core_ids=[0])
    return r.results[0]["out_0_dram"]
```

```python
from contextlib import ExitStack

import numpy as np

import concourse.bass as bass
from concourse import mybir

P = 128
F32 = mybir.dt.float32
BF16 = mybir.dt.bfloat16
F16 = mybir.dt.float16
F32R = mybir.dt.float32r
U32 = mybir.dt.uint32
I32 = mybir.dt.int32
ALU = mybir.AluOpType
ACT = mybir.ActivationFunctionType
AX_X = mybir.AxisListType.X

BATCH, SEQ, HID = 8, 1024, 256
HC = HID // P
TB = SEQ // P
NT = BATCH * TB
EPS = 1e-5


def past(index, least):
    return not isinstance(index, int) or index >= least


def skewed(eng, count, phases, unroll=2):
    latest = max(delay for delay, _ in phases)

    def step(at, slot):
        for delay, run in phases:
            index = at - delay
            if isinstance(at, int) and not 0 <= index < count:
                continue
            run(index, (slot - delay) % unroll)

    first = latest + unroll
    first += -first % unroll
    blocks = (count - first) // unroll
    if blocks < 2:
        first, blocks = 0, 0
    for at in range(first):
        step(at, at % unroll)
    if blocks:
        with eng.Fori(first, first + (blocks - 1) * unroll + 1, unroll) as at:
            for u in range(unroll):
                step(at + u, u)
    for at in range(first + blocks * unroll, count + latest):
        step(at, at % unroll)


class Chain:

    def __init__(self, eng, sem):
        self.eng, self.sem, self.n = eng, sem, 0

    def then(self, ins):
        ins.then_inc(self.sem, 1)
        self.n += 1
        self.eng.wait_ge(self.sem, self.n)


def layernorm_scales(nc, dve, act_side, R, step, var_ready, std_ready):
    raw, mean, var, rstd, shift, diff = R.raw, R.mean, R.var, R.rstd, R.shift, R.diff
    c = Chain(dve, step)
    c.then(nc.vector.tensor_tensor(mean[:], raw[:, :, 1], raw[:, :, 4], ALU.add))
    c.then(nc.vector.tensor_tensor(diff[:], raw[:, :, 1], raw[:, :, 4], ALU.subtract))
    c.then(nc.vector.tensor_tensor(var[:], raw[:, :, 2], raw[:, :, 5], ALU.add))
    c.then(nc.vector.tensor_tensor(diff[:], diff[:], diff[:], ALU.mult))
    c.then(nc.vector.tensor_scalar(diff[:], diff[:], 0.25, EPS, ALU.mult, ALU.add))
    c.then(nc.vector.scalar_tensor_tensor(out=var[:], in0=var[:], scalar=1.0 / HID, in1=diff[:],
                                          op0=ALU.mult, op1=ALU.add))
    nc.vector.tensor_scalar(mean[:], mean[:], -0.5, None, ALU.mult).then_inc(var_ready, 1)
    dve.wait_ge(std_ready, 1)
    c.then(nc.vector.reciprocal(rstd[:], var[:]))
    c.then(nc.vector.tensor_tensor(shift[:], mean[:], rstd[:], ALU.mult))


def std_of_var(nc, act, R, var_ready, std_ready):
    act.wait_ge(var_ready, 1)
    nc.scalar.activation(R.var[:], R.var[:], ACT.Sqrt).then_inc(std_ready, 1)


class Stage:

    def __init__(self, nc, tag):
        self.nc, self.tag, self.ctx, self.sems = nc, tag, ExitStack(), []

    def __enter__(self):
        return self

    def sb(self, name, shape, dt=F32):
        return self.ctx.enter_context(self.nc.sbuf_tensor(f"{self.tag}_{name}", shape, dt))

    def ps(self, name, shape=(P, 512), dt=F32):
        return self.ctx.enter_context(self.nc.psum_tensor(f"{self.tag}_{name}", list(shape), dt))

    def sem(self, name):
        self.sems.append(self.ctx.enter_context(self.nc.semaphore(f"{self.tag}_{name}")))
        return self.sems[-1]

    def __exit__(self, *error):
        if not error[0] and self.sems:
            with self.nc.Block() as block:
                @block.gpsimd
                def _(pool):
                    for s in self.sems:
                        pool.sem_clear(s)
        return self.ctx.__exit__(*error)


def reload_x(nc, R, tag, source):
    with Stage(nc, tag) as st:
        loaded = [st.sem(f"loaded{b}") for b in range(BATCH)]
        with nc.Block() as block:
            @block.sync
            def _(sp):
                for b in range(BATCH):
                    sp.dma_start(R.X[:, b * TB:(b + 1) * TB, :],
                                 source[b * SEQ:(b + 1) * SEQ, :].rearrange("(j p) d -> p j d", p=P)).then_inc(loaded[b], 16)

            @block.vector
            def _(dve):
                for b in range(BATCH):
                    dve.wait_ge(loaded[b], 16)
                    for j in range(TB):
                        nc.vector.bn_stats(R.raw[:, b * TB + j, :], R.X[:, b * TB + j, :])


def row_of(tensor, i):
    return tensor[:, bass.ds(i, 1), :].rearrange("p a b -> p (a b)")


def tanh_ffn(nc, R, tag, sem_, weight, aux1, aux2, bias, out=None):
    def sem(name):
        return sem_(f"{tag}_{name}")

    with ExitStack() as ctx:
        def sb(name, shape, dt=F32):
            return ctx.enter_context(nc.sbuf_tensor(f"{tag}_{name}", shape, dt))

        def ps(name, shape, dt=F32):
            return ctx.enter_context(nc.psum_tensor(f"{tag}_{name}", shape, dt))

        w = sb("w", [P, 3, HC, HID])
        wT = sb("wT", [P, HC, HID])
        w01T = sb("w01T", [P, HC, HID])
        wc = sb("wc", [P, HC, HID])
        bias_all = sb("bias_all", [P, HID])
        xn = sb("xn", [P, 4, HID])
        xnT = sb("xnT", [P, 4, HC, P])
        pre = sb("pre", [P, 4, HID])
        th = sb("th", [P, 4, HID])
        psT = [ps(f"psT{i}", [P, 512]) for i in range(2)]
        psY = [ps(f"psY{i}", [P, 512]) for i in range(4)]
        psW = ps("psW", [P, HC, HID])

        loaded, wstep, wcopied = sem("loaded"), sem("wstep"), sem("wcopied")
        step, var_ready, std_ready = sem("step"), sem("var_ready"), sem("std_ready")
        stored = sem("stored")
        xn_ready, psT_ready, xnT_ready, psY_ready = sem("xn_ready"), sem("psT_ready"), sem("xnT_ready"), sem("psY_ready")
        pre_ready, th_ready, x_ready, stats_done = sem("pre_ready"), sem("th_ready"), sem("x_ready"), sem("stats_done")

        with nc.Block() as block:
            @block.sync
            def _(sp):
                for n, src in enumerate((weight, aux1, aux2)):
                    sp.dma_start(w[:, n], src.rearrange("(c p) d -> p c d", p=P)).then_inc(loaded, 16)
                sp.dma_start(bias_all[:], bias.rearrange("(a d) -> a d", a=1).broadcast_to([P, HID])).then_inc(loaded, 16)
                if out is not None:
                    for b in range(BATCH):
                        sp.wait_ge(x_ready, TB * (b + 1))
                        sp.dma_start(out[b].rearrange("(j p) d -> p j d", p=P), R.X[:, b * TB:(b + 1) * TB, :]).then_inc(stored, 16)
                    sp.wait_ge(stored, 16 * BATCH)

            @block.tensor
            def _(pe):
                pe.wait_ge(loaded, 64)
                for c in range(HC):
                    for h in range(HC):
                        last = nc.tensor.transpose(psW[:, h, c * P:(c + 1) * P], w[:, 0, c, h * P:(h + 1) * P], R.ident[:])
                last.then_inc(wstep, 1)
                for m, (lhs, rhs) in enumerate(((1, wT), (2, w01T))):
                    pe.wait_ge(wcopied, m + 1)
                    for o in range(HC):
                        for c in range(HC):
                            if m == 0:
                                a, b = w[:, 1, c, o * P:(o + 1) * P], wT[:, c, :]
                            else:
                                a, b = w01T[:, c, o * P:(o + 1) * P], w[:, 2, c, :]
                            last = nc.tensor.matmul(psW[:, o, :], a, b, start=(c == 0), stop=(c == HC - 1))
                    last.then_inc(wstep, 1)
                pe.wait_ge(wcopied, 3)

                def transposes(i, s):
                    pe.wait_ge(xn_ready, i + 1)
                    if past(i, 2):
                        pe.wait_ge(xnT_ready, i - 1)
                    for c in range(HC):
                        last = nc.tensor.transpose(psT[s % 2][:, c * P:(c + 1) * P], xn[:, s, c * P:(c + 1) * P], R.ident[:])
                    last.then_inc(psT_ready, 1)

                def products(i, s):
                    pe.wait_ge(xnT_ready, i + 1)
                    if past(i, 4):
                        pe.wait_ge(pre_ready, i - 3)
                    for c in range(HC):
                        last = nc.tensor.matmul(psY[s][:, 0:HID], xnT[:, s, c, :], wc[:, c, :], start=(c == 0), stop=(c == HC - 1))
                    last.then_inc(psY_ready, 1)

                skewed(pe, NT, [(0, transposes), (2, products)], unroll=4)

            @block.scalar
            def _(act):
                std_of_var(nc, act, R, var_ready, std_ready)
                for m, dst in enumerate((wT, w01T, wc)):
                    act.wait_ge(wstep, m + 1)
                    nc.scalar.copy(dst[:], psW[:]).then_inc(wcopied, 1)

                def copy_xnT(i, s):
                    act.wait_ge(psT_ready, i + 1)
                    if past(i, 4):
                        act.wait_ge(psY_ready, i - 3)
                    nc.scalar.copy(xnT[:, s].rearrange("p c t -> p (c t)"), psT[s % 2][:, 0:HID]).then_inc(xnT_ready, 1)

                def tanh(i, s):
                    act.wait_ge(pre_ready, i + 1)
                    if past(i, 4):
                        act.wait_ge(x_ready, i - 3)
                    nc.scalar.activation(th[:, s], pre[:, s], ACT.Tanh).then_inc(th_ready, 1)

                skewed(act, NT, [(0, copy_xnT), (4, tanh)], unroll=4)

            @block.vector
            def _(dve):
                layernorm_scales(nc, dve, None, R, step, var_ready, std_ready)

                def normalize(i, s):
                    if past(i, 4):
                        dve.wait_ge(psT_ready, i - 3)
                    nc.vector.tensor_scalar(xn[:, s], row_of(R.X, i), R.rstd[:, bass.ds(i, 1)], R.shift[:, bass.ds(i, 1)],
                                            ALU.mult, ALU.add).then_inc(xn_ready, 1)

                def add_bias(i, s):
                    dve.wait_ge(psY_ready, i + 1)
                    if past(i, 4):
                        dve.wait_ge(th_ready, i - 3)
                    nc.vector.tensor_tensor(pre[:, s], psY[s][:, 0:HID], bias_all[:], ALU.add).then_inc(pre_ready, 1)

                def stats(i, s):
                    dve.wait_ge(x_ready, i + 1)
                    nc.vector.bn_stats(row_of(R.raw, i), row_of(R.X, i))

                skewed(dve, NT, [(0, normalize), (3, add_bias)] + ([(7, stats)] if out is None else []), unroll=4)

            @block.gpsimd
            def _(pool):
                def residual(i, s):
                    pool.wait_ge(th_ready, i + 1)
                    nc.gpsimd.tensor_tensor(row_of(R.X, i), row_of(R.X, i), th[:, s], ALU.add).then_inc(x_ready, 1)

                skewed(pool, NT, [(0, residual)], unroll=4)


def top_k_experts(nc, R, tag, A, C, before):
    E, F, K = 8, 1024, 128
    NF = F // P
    ROUNDS = K // 8
    PAIRS = E * BATCH // 2
    PE_ = BATCH // 2
    with Stage(nc, tag) as st:
        sb, ps, sem = st.sb, st.ps, st.sem
        QUARTERS, QF = 4, NF // 2
        w_raw = sb("w_raw", [P, QUARTERS, F])
        w_parts = sb("w_parts", [P, 2, 2, QUARTERS, F], F32R)
        b1_rows, b1 = sb("b1_rows", [E * NF, P]), sb("b1", [P, E * NF])
        b2_raw, b2 = sb("b2_raw", [P, HID]), sb("b2", [P, 2, HID])
        wgT = sb("wgT", [P, HC, E])
        gate, index = sb("gate", [P, E, BATCH]), sb("index", [P, E, BATCH], U32)
        zero = sb("zero", [P, 1], U32)
        ban = [ps(f"bank{i}") for i in range(8)]
        q_loaded = [sem(f"q_loaded{q}") for q in range(QUARTERS)]

        def load_quarter(sp, e, q):
            if q < 2:
                src = A["L0_ffn_W1"][bass.ds(e, 1), q * P:(q + 1) * P, :].rearrange("a p f -> p (a f)")
                dst = w_raw[:, q]
            else:
                rows = slice((q - 2) * QF * P, (q - 1) * QF * P)
                src = A["L0_ffn_W2"][bass.ds(e, 1), rows, :].rearrange("a (c p) d -> p (a c) d", p=P)
                dst = w_raw[:, q].rearrange("p (c d) -> p c d", d=HID)
            sp.dma_start(dst, src).then_inc(q_loaded[q], 16)
            if q == QUARTERS - 1:
                sp.dma_start(b2_raw[:], A["L0_ffn_b2"][bass.ds(e, 1), :].broadcast_to([P, HID])).then_inc(q_loaded[q], 16)

        gathered_from, summed = R.xn_dram, R.sum_dram

        with Stage(nc, tag + "r") as rt:
            xn, xnT = rt.sb("xn", [P, 8, HID]), rt.sb("xnT", [P, 2, HID])
            wg_rows = rt.sb("wg_rows", [E, HID])
            L, Lx, Lsum = rt.sb("L", [P, NT, E]), rt.sb("Lx", [P, NT, E]), rt.sb("Lsum", [P, NT])
            SC = rt.sb("SC", [BATCH * E, SEQ])
            top, where = rt.sb("top", [BATCH * E, K]), rt.sb("where", [BATCH * E, K], U32)
            wheref, rowbase = rt.sb("wheref", [BATCH * E, K]), rt.sb("rowbase", [BATCH * E, 1])
            loaded, x_out = rt.sem("loaded"), rt.sem("x_out")
            step, var_ready, std_ready = rt.sem("step"), rt.sem("var_ready"), rt.sem("std_ready")
            xn_ready, xT_done, xT_ready, L_done, L_ready = (rt.sem("xn_ready"), rt.sem("xT_done"), rt.sem("xT_ready"),
                                                           rt.sem("L_done"), rt.sem("L_ready"))
            shifted, exped, soft, turned, sc_ready = (rt.sem("shifted"), rt.sem("exped"), rt.sem("soft"), rt.sem("turned"),
                                                     rt.sem("sc_ready"))
            found, ends_turned, b1_turned, b1_ready = rt.sem("found"), rt.sem("ends_turned"), rt.sem("b1_turned"), rt.sem("b1_ready")
            wg_turned, wg_ready = rt.sem("wg_turned"), rt.sem("wg_ready")
            xn_to = gathered_from.rearrange("(i p) d -> i p d", p=P)
            half_out = [rt.sem(f"xn_out{n}") for n in range(2)]
            with nc.Block() as block:
                @block.sync
                def _(sp):
                    sp.dma_start(wg_rows[:], A["L0_ffn_Wg"]).then_inc(loaded, 16)
                    sp.dma_start(b1_rows[:], A["L0_ffn_b1"].rearrange("e (f p) -> (e f) p", p=P)).then_inc(loaded, 16)
                    sp.dma_start(rowbase[:], C["row_base"]).then_inc(loaded, 16)

                    def store_xn(g, s):
                        sp.wait_ge(xn_ready, 4 * (g + 1))
                        sp.dma_start(xn_to[bass.ds(4 * g, 4)].rearrange("a p d -> p a d"), xn[:, 4 * s:4 * s + 4]).then_inc(half_out[s], 16)

                    skewed(sp, NT // 4, [(0, store_xn)])
                    for b in range(BATCH):
                        sp.dma_start(summed[b * SEQ:(b + 1) * SEQ, :].rearrange("(j p) d -> p j d", p=P),
                                     R.X[:, b * TB:(b + 1) * TB, :]).then_inc(x_out, 16)
                    for q in range(QUARTERS):
                        load_quarter(sp, 0, q)
                    sp.wait_ge(x_out, 16 * BATCH)
                    for s in range(2):
                        sp.wait_ge(half_out[s], 16 * NT // 8)

                @block.tensor
                def _(pe):
                    pe.wait_ge(loaded, 48)
                    for c in range(HC):
                        last = nc.tensor.transpose(ban[6][:, c * E:(c + 1) * E], wg_rows[:, c * P:(c + 1) * P], R.ident[0:E, 0:E])
                    last.then_inc(wg_turned, 1)
                    nc.tensor.transpose(ban[7][:, 0:E * NF], b1_rows[:], R.ident[0:E * NF, 0:E * NF]).then_inc(b1_turned, 1)

                    def turn_x(i, s):
                        pe.wait_ge(xn_ready, i + 1)
                        if past(i, 2):
                            pe.wait_ge(xT_ready, i - 1)
                        for c in range(HC):
                            last = nc.tensor.transpose(ban[s % 2][:, c * P:(c + 1) * P], xn[:, s, c * P:(c + 1) * P], R.ident[:])
                        last.then_inc(xT_done, 1)

                    def logits(i, s):
                        pe.wait_ge(xT_ready, i + 1)
                        if past(i, 2):
                            pe.wait_ge(L_ready, i - 1)
                        for c in range(HC):
                            last = nc.tensor.matmul(ban[2 + s % 2][:, 0:E], xnT[:, s % 2, c * P:(c + 1) * P], wgT[:, c, :],
                                                    start=(c == 0), stop=(c == HC - 1))
                        last.then_inc(L_done, 1)

                    pe.wait_ge(wg_ready, 1)
                    skewed(pe, NT, [(0, turn_x), (2, logits)], unroll=8)
                    pe.wait_ge(soft, 1)
                    for j in range(TB):
                        if j >= 2:
                            pe.wait_ge(sc_ready, j - 1)
                        nc.tensor.transpose(ban[4 + j % 2][0:BATCH * E, 0:P], L[:, j * BATCH:(j + 1) * BATCH, :].rearrange("p b e -> p (b e)"), R.ident[:]).then_inc(turned, 1)
                    pe.wait_ge(found, 1)
                    nc.tensor.transpose(ban[6][:, 0:BATCH * E], top[:], R.ident[0:BATCH * E, 0:BATCH * E]).then_inc(ends_turned, 1)
                    pe.wait_ge(b1_ready, 1)
                    nc.tensor.transpose(ban[7][:, 0:BATCH * E], wheref[:], R.ident[0:BATCH * E, 0:BATCH * E]).then_inc(ends_turned, 1)

                @block.scalar
                def _(act):
                    std_of_var(nc, act, R, var_ready, std_ready)
                    act.wait_ge(wg_turned, 1)
                    nc.scalar.copy(wgT[:].rearrange("p c e -> p (c e)"), ban[6][:, 0:HC * E]).then_inc(wg_ready, 1)
                    act.wait_ge(b1_turned, 1)
                    nc.scalar.copy(b1[:], ban[7][:, 0:E * NF]).then_inc(b1_ready, 1)

                    def copy_xT(i, s):
                        act.wait_ge(xT_done, i + 1)
                        if past(i, 2):
                            act.wait_ge(L_done, i - 1)
                        nc.scalar.copy(xnT[:, s % 2], ban[s % 2][:, 0:HID]).then_inc(xT_ready, 1)

                    skewed(act, NT, [(0, copy_xT)], unroll=8)
                    act.wait_ge(shifted, 1)
                    nc.scalar.activation(Lx[:], Lx[:], ACT.Exp).then_inc(exped, 1)
                    for j in range(TB):
                        act.wait_ge(turned, j + 1)
                        nc.scalar.copy(SC[:, j * P:(j + 1) * P], ban[4 + j % 2][0:BATCH * E, 0:P]).then_inc(sc_ready, 1)

                @block.vector
                def _(dve):
                    layernorm_scales(nc, dve, None, R, step, var_ready, std_ready)

                    def normalize(i, s):
                        if past(i, 8):
                            dve.wait_ge(xT_done, i - 7)
                            if s % 4 == 0:
                                dve.wait_ge(half_out[s // 4], (i - s) * 2)
                        nc.vector.tensor_scalar(xn[:, s], row_of(R.X, i), R.rstd[:, bass.ds(i, 1)], R.shift[:, bass.ds(i, 1)],
                                                ALU.mult, ALU.add).then_inc(xn_ready, 1)

                    def copy_L(i, s):
                        dve.wait_ge(L_done, i + 1)
                        nc.vector.tensor_copy(row_of(L, i), ban[2 + s % 2][:, 0:E]).then_inc(L_ready, 1)

                    skewed(dve, NT, [(0, normalize), (4, copy_L)], unroll=8)
                    dve.wait_ge(L_ready, NT)
                    c = Chain(dve, rt.sem("softmax_step"))
                    c.then(nc.vector.tensor_reduce(Lsum[:], L[:], AX_X, ALU.max))
                    nc.vector.tensor_tensor(Lx[:], L[:], Lsum[:, :, None].broadcast_to([P, NT, E]), ALU.subtract).then_inc(shifted, 1)
                    dve.wait_ge(exped, 1)
                    c.then(nc.vector.tensor_reduce(Lsum[:], Lx[:], AX_X, ALU.add))
                    c.then(nc.vector.reciprocal(Lsum[:], Lsum[:]))
                    nc.vector.tensor_tensor(L[:].rearrange("p (j b) e -> p b j e", j=TB),
                                            Lx[:].rearrange("p (b j) e -> p b j e", j=TB),
                                            Lsum[:].rearrange("p (b j) -> p b j", j=TB)[:, :, :, None].broadcast_to([P, BATCH, TB, E]),
                                            ALU.mult).then_inc(soft, 1)
                    dve.wait_ge(sc_ready, TB)
                    for r in range(ROUNDS):
                        best = top[:, 8 * r:8 * r + 8]
                        c.then(nc.vector.max(out=best, in_=SC[:]))
                        c.then(nc.vector.max_index(out=where[:, 8 * r:8 * r + 8], in_max=best, in_values=SC[:]))
                        if r < ROUNDS - 1:
                            c.then(nc.vector.match_replace(out=SC[:], in_to_replace=best, in_values=SC[:], imm_value=-1.0))
                    c.then(nc.vector.tensor_copy(wheref[:], where[:]))
                    dve.wait_ge(loaded, 48)
                    nc.vector.tensor_scalar(wheref[:], wheref[:], rowbase[:, 0:1], None, ALU.add).then_inc(found, 1)
                    dve.wait_ge(ends_turned, 1)
                    nc.vector.tensor_copy(gate[:].rearrange("p e b -> p b e"), ban[6][:, 0:BATCH * E].rearrange("p (b e) -> p b e", e=E))
                    dve.wait_ge(ends_turned, 2)
                    nc.vector.tensor_copy(index[:].rearrange("p e b -> p b e"), ban[7][:, 0:BATCH * E].rearrange("p (b e) -> p b e", e=E))
                    nc.vector.memset(zero[:], 0)

        gate_g = gate[:].rearrange("p e b -> p (e b)")
        index_g = index[:].rearrange("p e b -> p (e b)")

        with Stage(nc, tag + "e") as ex:
            U = 2 * PE_
            rows = ex.sb("rows", [P, U, 2], U32)
            ex_in, exT = ex.sb("ex_in", [P, 2, 2, HID]), ex.sb("exT", [P, 2, 2, HC, 2 * P], F32R)
            h = ex.sb("h", [P, 4, 2 * P])
            hT = ex.sb("hT", [P, 2, 2, NF, 2 * P], F32R)
            pre, y = ex.sb("pre", [P, 2, HID]), ex.sb("y", [P, 2, 2, HID])
            turn = ex.sb("turn", [P, 2], U32)
            bias = ex.sb("bias", [P, 2, NF])
            bias_ready = ex.sem("bias_ready")
            row_back = [ex.sem(f"row_back{b}") for b in range(BATCH)]
            bx, bh, by = ban[0], ban[1:5], ban[6:8]
            fetched_before, scattered_before = before * PAIRS // 4 * 32, before * E * 16
            fetched, scattered = R.fetched, R.scattered
            rows_ready, x_turned, xT_ready, up_done, h_ready = (ex.sem("rows_ready"), ex.sem("x_turned"), ex.sem("xT_ready"),
                                                               ex.sem("up_done"), ex.sem("h_ready"))
            b2_ready, w_high, w_ready, x_high, h_low = ex.sem("b2_ready"), ex.sem("w_high"), ex.sem("w_ready"), ex.sem("x_high"), ex.sem("h_low")
            PARTS = ((0, 0), (0, 1), (1, 0))
            down_done, pre_ready, y_ready, turns = (ex.sem("down_done"), ex.sem("pre_ready"), ex.sem("y_ready"),
                                                     [ex.sem("turns0"), ex.sem("turns1")])

            with nc.Block() as block:
                @block.sync
                def _(sp):
                    with sp.Fori(1, E) as e:
                        for q in range(QUARTERS):
                            sp.wait_ge(w_ready, QUARTERS * (e - 1) + q + 1)
                            load_quarter(sp, e, q)
                    for b in range(BATCH):
                        sp.wait_ge(scattered[b], 16 * E + scattered_before)
                        sp.dma_start(R.X[:, b * TB:(b + 1) * TB, :],
                                     summed[b * SEQ:(b + 1) * SEQ, :].rearrange("(j p) d -> p j d", p=P)).then_inc(row_back[b], 16)

                @block.gpsimd
                def _(pool):
                    def fetch(t, s):
                        pair = rows[:, s, :]
                        if past(t, 2):
                            pool.wait_ge(x_turned, t - 1)
                        if past(t, U):
                            for u in range(2):
                                b = 2 * (s % PE_) + u
                                pool.wait_ge(scattered[b], 4 * (t - s % PE_) - 16 + scattered_before)
                        nc.gpsimd.tensor_tensor(pair, index_g[:, bass.ds(2 * t, 2)], zero[:].broadcast_to([P, 2]), ALU.add
                                                ).then_inc(rows_ready, 1)
                        pool.wait_ge(rows_ready, t + 1)
                        if past(t, 1):
                            pool.wait_ge(turns[0], t)
                        nc.gpsimd.tensor_tensor(turn[:, 0:1], zero[:], zero[:], ALU.add).then_inc(turns[0], 1)
                        for u in range(2):
                            nc.gpsimd.indirect_dma_start(out=ex_in[:, s % 2, u, :], out_offset=None, in_=gathered_from,
                                                         in_offset=bass.IndirectOffsetOnAxis(ap=rows[:, s, u:u + 1], axis=0)
                                                         ).then_inc(fetched[s % 4], 16)

                    def scatter(t, s):
                        pool.wait_ge(y_ready, 2 * t + 2)
                        if past(t, 1):
                            pool.wait_ge(turns[1], t)
                        nc.gpsimd.tensor_tensor(turn[:, 1:2], zero[:], zero[:], ALU.add).then_inc(turns[1], 1)
                        for u in range(2):
                            b = 2 * (s % PE_) + u
                            nc.gpsimd.indirect_dma_start(out=summed, out_offset=bass.IndirectOffsetOnAxis(ap=rows[:, s, u:u + 1], axis=0),
                                                         in_=y[:, s % 2, u, :], in_offset=None, compute_op=ALU.add
                                                         ).then_inc(scattered[b], 16)

                    skewed(pool, PAIRS, [(0, fetch), (3, scatter)], unroll=U)
                    for b in range(BATCH):
                        pool.wait_ge(scattered[b], 16 * E + scattered_before)

                @block.tensor
                def _(pe):
                    def turn_x(t, s):
                        pe.wait_ge(fetched[s % 4], 8 * (t - s % 4) + 32 + fetched_before)
                        if past(t, 1):
                            pe.wait_ge(xT_ready, t)
                        for c in range(HC):
                            for u in range(2):
                                last = nc.tensor.transpose(bx[:, (2 * c + u) * P:(2 * c + u + 1) * P],
                                                           ex_in[:, s % 2, u, c * P:(c + 1) * P], R.ident[:])
                        last.then_inc(x_turned, 1)

                    def up(t, s):
                        par = s // PE_
                        pe.wait_ge(xT_ready, t + 1)
                        if s % PE_ == 0:
                            pe.wait_ge(w_ready, t + 2)
                        for f in range(NF):
                            bank = bh[f % 4]
                            if f >= 4 or past(t, 1):
                                pe.wait_ge(h_ready, NF * t + f - 3)
                            steps = [(c, a, b) for c in range(HC) for a, b in PARTS]
                            for n, (c, a, b) in enumerate(steps):
                                last = nc.tensor.matmul(bank[:, 0:2 * P], w_parts[:, par, a, c, f * P:(f + 1) * P], exT[:, s % 2, b, c],
                                                        start=(n == 0), stop=(n == len(steps) - 1))
                            last.then_inc(up_done, 1)

                    def down(t, s):
                        par = s // PE_
                        if s % PE_ == 0:
                            pe.wait_ge(w_ready, t + QUARTERS)
                        pe.wait_ge(h_low, NF * t + NF)
                        for u in range(2):
                            if past(t, 1):
                                pe.wait_ge(pre_ready, 2 * t - 1 + u)
                            steps = [(f, a, b) for f in range(NF) for a, b in PARTS]
                            for n, (f, a, b) in enumerate(steps):
                                last = nc.tensor.matmul(by[u][:, 0:HID], hT[:, s % 2, a, f, u * P:(u + 1) * P],
                                                        w_parts[:, par, b, 2 + f // QF, f % QF * HID:(f % QF + 1) * HID],
                                                        start=(n == 0), stop=(n == len(steps) - 1))
                        last.then_inc(down_done, 1)

                    skewed(pe, PAIRS, [(0, turn_x), (1, up), (2, down)], unroll=U)

                @block.scalar
                def _(act):
                    def split_w(t, s):
                        q, par = s % QUARTERS, s // QUARTERS
                        loads = 2 if q == QUARTERS - 1 else 1
                        act.wait_ge(q_loaded[q], loads * (4 * (t - q) + 16))
                        if past(t, 2 * PE_):
                            if q < 2:
                                act.wait_ge(up_done, NF * (t - q - PE_))
                            else:
                                act.wait_ge(down_done, t - q - PE_)
                        nc.scalar.copy(w_parts[:, par, 0, q], w_raw[:, q]).then_inc(w_high, 1)

                    def gelu(t, s):
                        par = s // PE_
                        if s % PE_ == 0:
                            act.wait_ge(bias_ready, t + PE_)
                        for f in range(NF):
                            act.wait_ge(up_done, NF * t + f + 1)
                            if f == 0 and past(t, 2):
                                act.wait_ge(down_done, t - 1)
                            if f % 2 == 0 and (f >= 4 or past(t, 1)):
                                act.wait_ge(h_low, NF * t + f - 2)
                            for to in (hT[:, s % 2, 0, f], h[:, f % 4]):
                                last = nc.scalar.activation(to, bh[f % 4][:, 0:2 * P], ACT.Gelu_apprx_tanh,
                                                            bias=bias[:, par, f:f + 1])
                            last.then_inc(h_ready, 1)

                    skewed(act, PAIRS, [(0, split_w), (4, gelu)], unroll=U)

                @block.vector
                def _(dve):
                    def split_w(t, s):
                        q, par = s % QUARTERS, s // QUARTERS
                        dve.wait_ge(w_high, t + 1)
                        if q == QUARTERS - 1:
                            nc.vector.tensor_copy(b2[:, par], b2_raw[:]).then_inc(b2_ready, PE_)
                        nc.vector.tensor_tensor(w_parts[:, par, 1, q], w_raw[:, q], w_parts[:, par, 0, q].bitcast(F32), ALU.subtract
                                                ).then_inc(w_ready, 1)

                    def split_xT(t, s):
                        if s % PE_ == 0:
                            if past(t, U):
                                dve.wait_ge(h_ready, NF * (t - PE_))
                            nc.vector.tensor_scalar(bias[:, s // PE_], b1[:, bass.ds(t * (NF // PE_), NF)], 0.0, None, ALU.add
                                                    ).then_inc(bias_ready, PE_)
                        dve.wait_ge(x_turned, t + 1)
                        if past(t, 2):
                            dve.wait_ge(up_done, NF * (t - 1))
                        high, low = (exT[:, s % 2, part].rearrange("p c t -> p (c t)") for part in range(2))
                        nc.vector.tensor_copy(high, bx[:]).then_inc(x_high, 1)
                        dve.wait_ge(x_high, t + 1)
                        nc.vector.tensor_tensor(low, bx[:], high.bitcast(F32), ALU.subtract).then_inc(xT_ready, 1)

                    def split_h(t, s):
                        for f in range(0, NF, 2):
                            dve.wait_ge(h_ready, NF * t + f + 2)
                            nc.vector.tensor_tensor(hT[:, s % 2, 1, f:f + 2], h[:, f % 4:f % 4 + 2], hT[:, s % 2, 0, f:f + 2].bitcast(F32), ALU.subtract
                                                    ).then_inc(h_low, 2)

                    def add_b2(t, s):
                        for u in range(2):
                            if u == 0:
                                dve.wait_ge(down_done, t + 1)
                            if u == 0 and s % PE_ == 0:
                                dve.wait_ge(b2_ready, t + PE_)
                            if past(t, 1):
                                dve.wait_ge(y_ready, 2 * t - 1 + u)
                            nc.vector.tensor_tensor(pre[:, u], by[u][:, 0:HID], b2[:, s // PE_], ALU.add).then_inc(pre_ready, 1)

                    def weigh(t, s):
                        for u in range(2):
                            dve.wait_ge(pre_ready, 2 * t + u + 1)
                            if past(t, 2):
                                b = 2 * ((s - 2) % PE_) + u
                                dve.wait_ge(scattered[b], 4 * (t - 2 - (s - 2) % PE_) + 16 + scattered_before)
                            nc.vector.tensor_scalar(y[:, s % 2, u], pre[:, u], gate_g[:, bass.ds(2 * t + u, 1)], None, ALU.mult
                                                    ).then_inc(y_ready, 1)

                    def stats(t, s):
                        if isinstance(t, int) and t >= PAIRS - PE_:
                            for b in (2 * (s % PE_), 2 * (s % PE_) + 1):
                                dve.wait_ge(row_back[b], 16)
                                for j in range(TB):
                                    nc.vector.bn_stats(R.raw[:, b * TB + j, :], R.X[:, b * TB + j, :])

                    skewed(dve, PAIRS, [(3, split_xT), (4, split_h), (5, add_b2), (5, weigh), (0, split_w), (8, stats)], unroll=U)


def turned_copies(nc, R, tag, jobs, banks):
    blocks = []
    with Stage(nc, tag) as st:
        loaded, turned, copied = st.sem("loaded"), st.sem("turned"), st.sem("copied")
        for n, (src, dst) in enumerate(jobs):
            rows, cols = src.shape
            staged = st.sb(f"staged{n}", [P, rows // P, cols])
            flat = dst.rearrange("p c r -> p (c r)")
            places = [(c, r) for c in range(cols // P) for r in range(rows // P)]
            for k in range(0, len(places), 4):
                blocks.append(([staged[:, r, c * P:(c + 1) * P] for c, r in places[k:k + 4]], flat[:, k * P:(k + 4) * P]))
            jobs[n] = (src, staged)
        with nc.Block() as block:
            @block.sync
            def _(sp):
                for src, staged in jobs:
                    sp.dma_start(staged[:], src.rearrange("(r p) c -> p r c", p=P)).then_inc(loaded, 16)

            @block.tensor
            def _(pe):
                pe.wait_ge(loaded, 16 * len(jobs))
                for n, (parts, _) in enumerate(blocks):
                    if n >= 2:
                        pe.wait_ge(copied, n - 1)
                    for k, part in enumerate(parts):
                        last = nc.tensor.transpose(banks[n % 2][:, k * P:(k + 1) * P], part, R.ident[:])
                    last.then_inc(turned, 1)

            @block.scalar
            def _(act):
                for n, (_, to) in enumerate(blocks):
                    act.wait_ge(turned, n + 1)
                    nc.scalar.copy(to, banks[n % 2][:]).then_inc(copied, 1)


def spectral_attention(nc, R, A, C):
    CH = 64
    NF = CH // 2 + 1
    LOW = 4
    HIGH = NF - LOW
    NCH = BATCH * SEQ // CH
    CB = SEQ // CH
    TAPS = 7
    HEADS, KV, HD = 16, 4, 64
    PRS = HEADS // 2
    with Stage(nc, "sp") as st:
        sb, ps, sem = st.sb, st.ps, st.sem
        qwT, kwT, vwT = sb("qwT", [P, HC, HEADS * HD]), sb("kwT", [P, HC, HID]), sb("vwT", [P, HC, HID])
        gwT, owT = sb("gwT", [P, HC, HID]), sb("owT", [P, PRS, HID])
        pwT = [sb("pwT_r", [P, HC, HID]), sb("pwT_i", [P, HC, HID])]
        bank = [ps(f"bank{i}") for i in range(8)]
        turned_copies(nc, R, "spw", [(A["L0_attn_b_q_w"], qwT[:]), (A["L0_attn_b_k_w"], kwT[:]), (A["L0_attn_b_v_w"], vwT[:]),
                                     (A["L0_attn_b_gate_w"], gwT[:]), (A["L0_attn_b_o_w"], owT[:]),
                                     (A["L0_attn_b_pw_r"], pwT[0][:]), (A["L0_attn_b_pw_i"], pwT[1][:])], bank)
        XF = sb("XF", [P, HC, NCH, 2, NF])
        lowA = sb("lowA", [P, BATCH, HID])
        alpha = sb("alpha", [P, 1])
        dw = sb("dw", [P, HC, 2, TAPS])
        XF_tile = XF[:].rearrange("p c (t h) r f -> p c t (h r f)", h=2)
        W = 2 * 2 * NF

        with Stage(nc, "spf") as f:
            dft = f.sb("dft", [P, W])
            xn = f.sb("xn", [P, 4, HID])
            g = f.sb("g", [P, HID])
            loaded, xn_ready, f_done, f_ready, z_done, e_ready, g_ready, stored = (
                f.sem("loaded"), f.sem("xn_ready"), f.sem("f_done"), f.sem("f_ready"), f.sem("z_done"), f.sem("e_ready"),
                f.sem("g_ready"), f.sem("stored"))
            step, var_ready, std_ready = f.sem("step"), f.sem("var_ready"), f.sem("std_ready")
            with nc.Block() as block:
                @block.sync
                def _(sp):
                    sp.dma_start(dft[:], C["dft"]).then_inc(loaded, 16)
                    sp.dma_start(alpha[:], A["L0_attn_b_alpha_raw"].rearrange("(a b) -> a b", a=1).broadcast_to([P, 1])).then_inc(loaded, 16)
                    for r, name in enumerate(("dw_r", "dw_i")):
                        sp.dma_start(dw[:, :, r, :], A[f"L0_attn_b_{name}"].rearrange("(c p) a k -> p c (a k)", p=P)).then_inc(loaded, 16)
                    sp.wait_ge(g_ready, 1)
                    sp.dma_start(R.gate_dram, g[:]).then_inc(stored, 16)
                    sp.wait_ge(stored, 16)

                @block.tensor
                def _(pe):
                    pe.wait_ge(loaded, 64)

                    def transform(i, s):
                        pe.wait_ge(xn_ready, i + 1)
                        if past(i, 4):
                            pe.wait_ge(f_ready, i - 3)
                        for c in range(HC):
                            last = nc.tensor.matmul(bank[s][:, c * W:(c + 1) * W], xn[:, s, c * P:(c + 1) * P], dft[:],
                                                    start=True, stop=True)
                        last.then_inc(f_done, 1)

                    skewed(pe, NT, [(0, transform)], unroll=4)
                    pe.wait_ge(f_ready, NT)
                    for c in range(HC):
                        last = nc.tensor.matmul(bank[2][:, 0:HID], XF[:, c, :, 0, 0], gwT[:, c, :], start=(c == 0), stop=(c == HC - 1))
                    last.then_inc(z_done, 1)

                @block.scalar
                def _(act):
                    std_of_var(nc, act, R, var_ready, std_ready)
                    act.wait_ge(loaded, 64)
                    nc.scalar.activation(alpha[:], alpha[:], ACT.Exp, scale=-1.0).then_inc(e_ready, 1)
                    act.wait_ge(z_done, 1)
                    nc.scalar.activation(g[:], bank[2][:, 0:HID], ACT.Exp, scale=-1.0 / CH).then_inc(e_ready, 1)

                @block.vector
                def _(dve):
                    layernorm_scales(nc, dve, None, R, step, var_ready, std_ready)

                    def normalize(i, s):
                        if past(i, 4):
                            dve.wait_ge(f_done, i - 3)
                        nc.vector.tensor_scalar(xn[:, s], row_of(R.X, i), R.rstd[:, bass.ds(i, 1)], R.shift[:, bass.ds(i, 1)],
                                                ALU.mult, ALU.add).then_inc(xn_ready, 1)

                    def copy_f(i, s):
                        dve.wait_ge(f_done, i + 1)
                        nc.vector.tensor_scalar(XF_tile[:, :, bass.ds(i, 1), :].rearrange("p c a w -> p (c a) w"),
                                                bank[s][:, 0:HC * W].rearrange("p (c w) -> p c w", c=HC), 0.0, None, ALU.add
                                                ).then_inc(f_ready, 1)

                    skewed(dve, NT, [(0, normalize), (3, copy_f)], unroll=4)
                    c = Chain(dve, f.sem("gate_step"))
                    dve.wait_ge(e_ready, 1)
                    c.then(nc.vector.tensor_scalar(alpha[:], alpha[:], 1.0, None, ALU.add))
                    c.then(nc.vector.reciprocal(alpha[:], alpha[:]))
                    dve.wait_ge(e_ready, 2)
                    c.then(nc.vector.tensor_scalar(g[:], g[:], 1.0, None, ALU.add))
                    nc.vector.reciprocal(g[:], g[:]).then_inc(g_ready, 1)

        T = CB * LOW
        with Stage(nc, "spa") as a:
            kwd = a.sb("kwd", [P, HC, KV, 2, HD])
            XL = a.sb("XL", [P, 2, HC, 2, T])
            Qd = a.sb("Qd", [P, 2, PRS, 2, T])
            kT = a.sb("kT", [P, KV, 2, T])
            v = a.sb("v", [P, 4, HID])
            mask = a.sb("mask", [P, T])
            probs, tops, sums = (a.sb("probs", [P, 2, 2 * PRS, T]), a.sb("tops", [P, 2 * PRS]),
                                   a.sb("sums", [P, 2 * PRS]))
            pT, oT = a.sb("pT", [P, PRS, P]), a.sb("oT", [P, PRS, P])
            names = "loaded kwd_ready zeroed XL_ready q_done k_done v_done q_ready kv_ready S_done S_read shifted exped prob_ready pT_done pT_ready o_done o_ready A_done A_ready soft".split()
            (loaded, kwd_ready, zeroed, XL_ready, q_done, k_done, v_done, q_ready, kv_ready, S_done, S_read, shifted, exped,
             prob_ready, pT_done, pT_ready, o_done, o_ready, A_done, A_ready, soft) = (a.sem(n) for n in names)
            XF_row = XF[:].rearrange("p c (b n) r f -> p c b n r f", b=BATCH)
            with nc.Block() as block:
                @block.sync
                def _(sp):
                    sp.dma_start(mask[:], C["chunk_mask"]).then_inc(loaded, 16)

                @block.tensor
                def _(pe):
                    pe.wait_ge(kwd_ready, 2)

                    def project(b, s):
                        pe.wait_ge(XL_ready, b + 1)
                        if past(b, 1):
                            pe.wait_ge(q_ready, 4 * b)
                            pe.wait_ge(kv_ready, 2 * b)
                        for m in range(PRS):
                            for c in range(HC):
                                last = nc.tensor.matmul(bank[m // 4][:, m % 4 * P:(m % 4 + 1) * P], qwT[:, c, m * P:(m + 1) * P],
                                                        XL[:, s, c].rearrange("p r t -> p (r t)"), start=(c == 0), stop=(c == HC - 1))
                            if m % 4 == 3:
                                last.then_inc(q_done, 1)
                        for m in range(KV):
                            for c in range(HC):
                                last = nc.tensor.matmul(bank[2][:, m * P:(m + 1) * P], kwd[:, c, m].rearrange("p u d -> p (u d)"),
                                                        XL[:, s, c].rearrange("p r t -> p (r t)"), start=(c == 0), stop=(c == HC - 1))
                        last.then_inc(k_done, 1)
                        if past(b, 1):
                            if b >= 3:
                                pe.wait_ge(A_ready, b - 2)
                        for c in range(HC):
                            last = nc.tensor.matmul(bank[3][:, 0:HID], XL[:, s, c].rearrange("p r t -> p (r t)"), vwT[:, c, :],
                                                    start=(c == 0), stop=(c == HC - 1))
                        last.then_inc(v_done, 1)

                    def scores(b, s):
                        pe.wait_ge(q_ready, 4 * b + 4)
                        pe.wait_ge(kv_ready, 2 * b + 2)
                        if past(b, 1):
                            pe.wait_ge(S_read, 2 * b)
                        for m in range(PRS):
                            for r in range(2):
                                last = nc.tensor.matmul(bank[4 + m // 4][:, (m % 4 * 2 + r) * T:(m % 4 * 2 + r + 1) * T],
                                                        Qd[:, r, m].rearrange("p h q -> p (h q)"), kT[:, m // 2, r], start=True, stop=True)
                            if m % 4 == 3:
                                last.then_inc(S_done, 1)

                    def weigh(b, s):
                        pe.wait_ge(prob_ready, b + 1)
                        if past(b, 1):
                            pe.wait_ge(o_ready, 2 * b)
                        for m in range(PRS):
                            last = nc.tensor.transpose(bank[6 + m // 4][:, m % 4 * P:(m % 4 + 1) * P],
                                                       probs[:, s, 2 * m:2 * m + 2].rearrange("p r k -> p (r k)"), R.ident[:])
                            if m % 4 == 3:
                                last.then_inc(pT_done, 1)
                        pe.wait_ge(pT_ready, 2 * b + 2)
                        for r in range(2):
                            for m in range(PRS):
                                for h in range(2):
                                    last = nc.tensor.matmul(bank[6 + r][h * HD:(h + 1) * HD, m * T:(m + 1) * T],
                                                            v[r * T:(r + 1) * T, b % 4, (m // 2) * HD:(m // 2 + 1) * HD],
                                                            pT[r * T:(r + 1) * T, m, h * T:(h + 1) * T], start=True, stop=True)
                            last.then_inc(o_done, 1)
                        pe.wait_ge(o_ready, 2 * b + 2)
                        pe.wait_ge(kv_ready, 2 * min(b + 3, BATCH))
                        for m in range(PRS):
                            last = nc.tensor.matmul(bank[3][:, HID:2 * HID], oT[:, m, :], owT[:, m, :], start=(m == 0), stop=(m == PRS - 1))
                        last.then_inc(A_done, 1)

                    for b in range(-2, BATCH):
                        if 0 <= b + 1 < BATCH:
                            scores(b + 1, (b + 1) % 2)
                        if b + 2 < BATCH:
                            project(b + 2, b % 2)
                        if b >= 0:
                            weigh(b, b % 2)

                @block.scalar
                def _(act):
                    for u in range(2):
                        nc.scalar.copy(kwd[:, :, :, u, :], kwT[:].rearrange("p c (k d) -> p c k d", d=HD)).then_inc(kwd_ready, 1)

                    def copies(b):
                        for n in range(2):
                            act.wait_ge(q_done, 2 * b + n + 1)
                            if b == 0 and n == 0:
                                act.wait_ge(zeroed, 1)
                            if b >= 1 and n == 0:
                                act.wait_ge(S_done, 2 * b)
                            for h in range(2):
                                half = slice(h * HD, (h + 1) * HD)
                                nc.scalar.copy(Qd[half, :, 4 * n:4 * n + 4, h, :].rearrange("p r m q -> p m r q"),
                                               bank[n][half, :].rearrange("p (m r q) -> p m r q", m=4, r=2)).then_inc(q_ready, 1)
                        act.wait_ge(k_done, b + 1)
                        nc.scalar.copy(kT[:].rearrange("p k r t -> p (k r t)"), bank[2][:]).then_inc(kv_ready, 1)
                        act.wait_ge(v_done, b + 1)
                        if b >= 4:
                            act.wait_ge(o_done, 2 * (b - 3))
                        nc.scalar.copy(v[:, b % 4], bank[3][:, 0:HID]).then_inc(kv_ready, 1)

                    copies(0)
                    copies(1)
                    for b in range(BATCH):
                        act.wait_ge(shifted, b + 1)
                        nc.scalar.activation(probs[:, b % 2], probs[:, b % 2], ACT.Exp).then_inc(exped, 1)
                        if b + 2 < BATCH:
                            copies(b + 2)
                        for n in range(2):
                            act.wait_ge(pT_done, 2 * b + n + 1)
                            nc.scalar.copy(pT[:, 4 * n:4 * n + 4].rearrange("p m t -> p (m t)"), bank[6 + n][:]).then_inc(pT_ready, 1)
                        for n in range(2):
                            act.wait_ge(o_done, 2 * b + n + 1)
                            if b and n == 0:
                                act.wait_ge(A_done, b)
                            nc.scalar.copy(oT[:, :, n * T:(n + 1) * T], bank[6 + n][:].rearrange("p (m t) -> p m t", t=T)).then_inc(o_ready, 1)
                        act.wait_ge(A_done, b + 1)
                        nc.scalar.copy(lowA[:, b], bank[3][:, HID:2 * HID]).then_inc(A_ready, 1)

                @block.vector
                def _(dve):
                    nc.vector.memset(Qd[:], 0.0).then_inc(zeroed, 1)
                    c = Chain(dve, soft)

                    def low_part(b):
                        if b >= 2:
                            dve.wait_ge(v_done, b - 1)
                        for half in range(HC):
                            ins = nc.vector.tensor_copy(XL[:, b % 2, half].rearrange("p r (n f) -> p r n f", f=LOW),
                                                        XF_row[:, half, b, :, :, 0:LOW].rearrange("p n r f -> p r n f"))
                        ins.then_inc(XL_ready, 1)

                    low_part(0)
                    low_part(1)
                    for b in range(BATCH):
                        S = prob = probs[:, b % 2]
                        if b + 2 < BATCH:
                            low_part(b + 2)
                        if b >= 2:
                            dve.wait_ge(pT_done, 2 * (b - 1))
                        if b == 0:
                            dve.wait_ge(loaded, 16)
                        for n in range(2):
                            dve.wait_ge(S_done, 2 * b + n + 1)
                            c.then(nc.vector.scalar_tensor_tensor(
                                out=S[:, 8 * n:8 * n + 8], in0=bank[4 + n][:].rearrange("p (m t) -> p m t", t=T), scalar=HD ** -0.5,
                                in1=mask[:, None, :].broadcast_to([P, PRS, T]), op0=ALU.mult, op1=ALU.add))
                            nc.vector.memset(R.turnstile[:], 0.0).then_inc(S_read, 1)
                        c.then(nc.vector.tensor_reduce(tops[:], S, AX_X, ALU.max))
                        nc.vector.tensor_tensor(S, S, tops[:, :, None].broadcast_to([P, 2 * PRS, T]), ALU.subtract).then_inc(shifted, 1)
                        dve.wait_ge(exped, b + 1)
                        c.then(nc.vector.tensor_reduce(sums[:], prob, AX_X, ALU.add))
                        c.then(nc.vector.reciprocal(sums[:], sums[:]))
                        nc.vector.tensor_tensor(prob, prob, sums[:, :, None].broadcast_to([P, 2 * PRS, T]), ALU.mult
                                                ).then_inc(prob_ready, 1)

        G = 4
        GC = 2 * G
        STEPS = NT // G
        with Stage(nc, "spc") as k:
            inv_high, inv_low, low_pass = k.sb("inv_high", [P, P]), k.sb("inv_low", [P, TB, P]), k.sb("low_pass", [P, P])
            acc = k.sb("acc", [P, HC, 2, GC, HIGH])
            gel = k.sb("gel", [P, 2, HC, 2, GC, HIGH])
            H = k.sb("H", [P, 2, HID])
            xn = k.sb("xn", [P, 4, HID])
            gx = k.sb("gx", [P, 4, HID])
            high, low = k.sb("high", [P, 2, HID]), k.sb("low", [P, 2, HID])
            names = "loaded zeroed acc_ready gel_ready xn_ready H_done H_ready Y_done terms_ready high_in x_ready taps".split()
            loaded, zeroed, acc_ready, gel_ready, xn_ready, H_done, H_ready, Y_done, terms_ready, high_in, x_ready, taps = (
                k.sem(n) for n in names)
            gx_in = [k.sem(f"gx_in{n}") for n in range(4)]
            XF_step = XF[:].rearrange("p c (k n) r f -> p c k n r f", n=GC)
            NTAP = HC * TAPS * 2
            with nc.Block() as block:
                @block.sync
                def _(sp):
                    for to, name in ((inv_high[:], "inv_high"), (inv_low[:], "inv_low"), (low_pass[:], "low_pass")):
                        sp.dma_start(to, C[name]).then_inc(loaded, 16)

                    def gates(i, s):
                        if past(i, 4):
                            sp.wait_ge(terms_ready, 2 * (i - 3))
                        for h in range(2):
                            sp.dma_start(gx[h * CH:(h + 1) * CH, s], R.gate_dram[bass.ds(2 * i + h, 1)].broadcast_to([CH, HID])
                                         ).then_inc(gx_in[s], 16)

                    skewed(sp, NT, [(0, gates)], unroll=4)

                @block.tensor
                def _(pe):
                    pe.wait_ge(loaded, 48)

                    def tile_H(t, j, s):
                        n = G * t + j
                        if not isinstance(t, int) or n >= 2:
                            pe.wait_ge(H_ready, 2 * (n - 1))
                        for r in range(2):
                            for c in range(HC):
                                last = nc.tensor.matmul(bank[n_slot(j)][r * CH:r * CH + 2 * HIGH, 0:HID],
                                                        gel[:, s, c, r, 2 * j:2 * j + 2].rearrange("p n f -> p (n f)"), pwT[r][:, c, :],
                                                        start=(c == 0), stop=(c == HC - 1))
                        last.then_inc(H_done, 1)

                    def tile_Y(t, j, place, row):
                        n = G * t + j
                        pe.wait_ge(H_ready, 2 * (n + 1))
                        pe.wait_ge(xn_ready, n + 1)
                        if not isinstance(t, int) or n >= 2:
                            pe.wait_ge(terms_ready, 2 * (n - 1))
                        nc.tensor.matmul(bank[2 + j % 2][:, 0:HID], inv_high[:], H[:, j % 2], start=True, stop=True)
                        nc.tensor.matmul(bank[4 + j % 2][:, 0:HID], low_pass[:], xn[:, j % 4], start=True, stop=False)
                        nc.tensor.matmul(bank[4 + j % 2][:, 0:HID], inv_low[:, place, :], row, start=False, stop=True).then_inc(Y_done, 1)

                    def n_slot(j):
                        return j % 2

                    lowA_flat = lowA[:].rearrange("p b d -> p (b d)")

                    def tiles(t, s):
                        pe.wait_ge(gel_ready, 4 * (t + 1))
                        row = lowA[:, t // 2, :] if isinstance(t, int) else lowA_flat[:, bass.ds((t - s) * (HID // 2), HID)]
                        for j in range(G + 1):
                            if j < G:
                                tile_H(t, j, s)
                            if j > 0:
                                tile_Y(t, j - 1, G * s + j - 1, row)

                    skewed(pe, STEPS, [(1, tiles)])

                @block.scalar
                def _(act):
                    def gelus(t, s, c):
                        for r in range(2):
                            act.wait_ge(acc_ready, 4 * t + 2 * c + r + 1)
                            if past(t, 2) and c == 0 and r == 0:
                                act.wait_ge(H_done, G * (t - 1))
                            nc.scalar.activation(gel[:, s, c, r], acc[:, c, r], ACT.Gelu).then_inc(gel_ready, 1)

                    def copies(t, j):
                        n = G * t + j
                        act.wait_ge(H_done, n + 1)
                        if not isinstance(t, int) or n >= 2:
                            act.wait_ge(Y_done, n - 1)
                        for r in range(2):
                            rows = slice(r * CH, r * CH + 2 * HIGH)
                            nc.scalar.copy(H[rows, j % 2], bank[j % 2][rows, 0:HID]).then_inc(H_ready, 1)

                    def first_copies(t, s):
                        for j in range(G - 1):
                            copies(t, j)

                    def last_copies(t, s):
                        copies(t, G - 1)

                    act.wait_ge(zeroed, 1)
                    skewed(act, STEPS, [(1, first_copies), (0, lambda t, s: gelus(t, s, 0)), (1, last_copies),
                                        (0, lambda t, s: gelus(t, s, 1))])

                @block.vector
                def _(dve):
                    nc.vector.memset(H[:], 0.0).then_inc(zeroed, 1)

                    def tile_norm(n, j):
                        if past(n, 4):
                            dve.wait_ge(terms_ready, 2 * (n - 3))
                        nc.vector.tensor_scalar(xn[:, j % 4], row_of(R.X, n), R.rstd[:, bass.ds(n, 1)], R.shift[:, bass.ds(n, 1)],
                                                ALU.mult, ALU.add).then_inc(xn_ready, 1)

                    def tile_terms(n, j):
                        dve.wait_ge(Y_done, n + 1)
                        dve.wait_ge(gx_in[j], (n - j) * 8 + 32)
                        if past(n, 2):
                            dve.wait_ge(x_ready, 2 * (n - 1))
                        nc.vector.tensor_tensor(high[:, j % 2], bank[2 + j % 2][:, 0:HID], gx[:, j], ALU.mult).then_inc(terms_ready, 1)
                        nc.vector.scalar_tensor_tensor(out=low[:, j % 2], in0=bank[4 + j % 2][:, 0:HID], scalar=alpha[:, 0:1],
                                                       in1=xn[:, j], op0=ALU.mult, op1=ALU.add).then_inc(terms_ready, 1)

                    def tile_stats(n):
                        dve.wait_ge(x_ready, 2 * (n + 1))
                        nc.vector.bn_stats(row_of(R.raw, n), row_of(R.X, n))

                    def taps_of(t, c, r, tap, order):
                        back = TAPS - 1 - tap
                        at = NTAP * t + order
                        src = XF_step[:, c, bass.ds(t, 1), :, r, LOW:NF - back].rearrange("p a n f -> p (a n) f")
                        if tap == TAPS - 1:
                            if past(t, 1):
                                dve.wait_ge(gel_ready, 4 * (t - 1) + 2 * c + r + 1)
                            ins = nc.vector.tensor_scalar(acc[:, c, r], src, dw[:, c, r, tap:tap + 1], None, ALU.mult)
                        else:
                            dve.wait_ge(taps, at - 1)
                            part = acc[:, c, r, :, back:HIGH]
                            ins = nc.vector.scalar_tensor_tensor(out=part, in0=src, scalar=dw[:, c, r, tap:tap + 1], in1=part,
                                                                 op0=ALU.mult, op1=ALU.add)
                        ins.then_inc(taps, 1)
                        if tap == 0:
                            dve.wait_ge(taps, at + 1)
                            nc.vector.memset(R.turnstile[:], 0.0).then_inc(acc_ready, 1)

                    ORDER = [(c, r, tap) for c in range(HC) for tap in range(TAPS - 1, -1, -1) for r in range(2)]
                    PART = len(ORDER) // G

                    def convolve(j):
                        def run(t, s):
                            for order in range(PART * j, PART * (j + 1)):
                                taps_of(t, *ORDER[order], order)
                        return run

                    def norm(j):
                        return lambda t, s: tile_norm(G * t + j, j)

                    def terms(j):
                        return lambda t, s: tile_terms(G * t + j, j)

                    def finish(t, s):
                        for j in range(G):
                            tile_stats(G * t + j)

                    phases = [(1, norm(0)), (0, convolve(0))]
                    for j in range(1, G):
                        phases += [(1, norm(j)), (0, convolve(j)), (1, terms(j - 1))]
                    skewed(dve, STEPS, phases + [(1, terms(G - 1)), (2, finish)])

                @block.gpsimd
                def _(pool):
                    def residual(n, j):
                        pool.wait_ge(terms_ready, 2 * n + 2)
                        nc.gpsimd.tensor_tensor(high[:, j % 2], high[:, j % 2], low[:, j % 2], ALU.add).then_inc(high_in, 1)
                        pool.wait_ge(high_in, n + 1)
                        nc.gpsimd.tensor_tensor(row_of(R.X, n), row_of(R.X, n), high[:, j % 2], ALU.add).then_inc(x_ready, 2)

                    skewed(pool, NT, [(0, residual)], unroll=4)


def second_order_attention(nc, R, A, C):
    H, DK = 16, 32
    HG = 4
    UT = H // HG
    NU = NT * UT
    with Stage(nc, "so") as st:
        sb, ps, sem = st.sb, st.ps, st.sem
        w = sb("w", [P, 3, HC, H * DK])
        wo = sb("wo", [P, UT, HID])
        upper, lower = sb("upper", [P, P]), sb("lower", [P, P])
        decay_t = sb("decay_t", [P, P])
        to_end, decay = sb("to_end", [P, NT]), sb("decay", [P, NT])
        head = sb("head", [P, HG])
        xn, xnT = sb("xn", [P, HID]), sb("xnT", [P, HID])
        QT, KT = sb("QT", [P, 2, UT, P]), sb("KT", [P, 2, UT, P])
        QTg, KTg = sb("QTg", [P, 2, UT, P]), sb("KTg", [P, 2, UT, P])
        QTp, KTp = sb("QTp", [P, 2, 2, UT, P], F32R), sb("KTp", [P, 2, 2, UT, P], F32R)
        QTs = sb("QTs", [P, 2, 2, UT, HG, P], F32R)
        PARTS = ((0, 0), (0, 1), (1, 0))
        V, K = sb("V", [P, 2, UT, P]), sb("K", [P, 2, UT, P])
        Ke, Qe = sb("Ke", [P, 2, UT, P]), sb("Qe", [P, 2, UT, P])
        M, AT, BT = sb("M", [P, 2, HG, P]), sb("AT", [P, 4, HG, P]), sb("BT", [P, HG, P])
        PT, Us, Ug = sb("PT", [P, 2, HG, P]), sb("Us", [P, 2, 2, HG, P], F32R), sb("Ug", [P, 4, P])
        WT, W, OT = sb("WT", [P, 2, P]), sb("W", [P, 2, P]), sb("OT", [P, 2, UT, P])
        state = sb("state", [P, UT, 3, P])
        b0, b1, bM, bB, bP, bU, bW, bS = (ps(f"bank{i}") for i in range(8))
        names = """loaded zeroed step var_ready std_ready xn_ready xT_done xT_ready QT_done KT_done QT_ready KT_ready V_done K_done
                   V_ready K_ready Q_done Qe_ready Ke_ready Qs_ready Qg_ready Kg_ready M_done M_ready AT_ready B_done BT_ready
                   U_done U_ready P_done PT_ready WT_done WT_ready W_done W_ready O_done O_ready S_done S_ready out_done
                   x_ready U_high QT_low KT_low Qs_high """.split()
        s_ = {n: sem(n) for n in names}

        with nc.Block() as block:
            @block.sync
            def _(sp):
                for n, name in enumerate("qkv"):
                    sp.dma_start(w[:, n], A[f"L1_attn_a_W{name}"].rearrange("(c p) d -> p c d", p=P)).then_inc(s_["loaded"], 16)
                sp.dma_start(wo[:], A["L1_attn_a_Wo"].rearrange("(u p) d -> p u d", p=P)).then_inc(s_["loaded"], 16)
                for to, name in ((upper, "upper"), (lower, "lower"), (decay_t, "decay_t"), (to_end, "to_end"), (decay, "decay"), (head, "head")):
                    sp.dma_start(to[:], C[name]).then_inc(s_["loaded"], 16)

            @block.tensor
            def _(pe):
                def T(n, s):
                    return n - s % UT

                def tile_part(n, s):
                    u, par, t4 = s % UT, s // UT, T(n, s)
                    if u == 0:
                        pe.wait_ge(s_["xn_ready"], t4 + 4)
                        if past(n, 4):
                            pe.wait_ge(s_["K_ready"], t4)
                        for c in range(HC):
                            last = pe_t(b0[:, c * P:(c + 1) * P], xn[:, c * P:(c + 1) * P])
                        last.then_inc(s_["xT_done"], 4)
                    elif u == 1:
                        pe.wait_ge(s_["xT_ready"], t4 + 4)
                        if past(n, 4):
                            pe.wait_ge(s_["Qe_ready"], t4)
                        for k in range(UT):
                            for c in range(HC):
                                last = nc.tensor.matmul(b1[:, k * P:(k + 1) * P], w[:, 0, c, k * P:(k + 1) * P], xnT[:, c * P:(c + 1) * P],
                                                        start=(c == 0), stop=(c == HC - 1))
                        last.then_inc(s_["QT_done"], 4)
                        if past(n, 12):
                            pe.wait_ge(s_["x_ready"], t4 - 8)
                        for k in range(UT):
                            for c in range(HC):
                                last = nc.tensor.matmul(b0[:, k * P:(k + 1) * P], w[:, 1, c, k * P:(k + 1) * P], xnT[:, c * P:(c + 1) * P],
                                                        start=(c == 0), stop=(c == HC - 1))
                        last.then_inc(s_["KT_done"], 4)
                    elif u == 2:
                        pe.wait_ge(s_["QT_ready"], t4 + 4)
                        for c in range(HC):
                            last = nc.tensor.matmul(b1[:], xnT[:, c * P:(c + 1) * P], w[:, 2, c, :], start=(c == 0), stop=(c == HC - 1))
                        last.then_inc(s_["V_done"], 4)
                        pe.wait_ge(s_["KT_ready"], t4 + 4)
                        for k in range(UT):
                            last = pe_t(b0[:, k * P:(k + 1) * P], KT[:, par, k])
                        last.then_inc(s_["K_done"], 4)
                    else:
                        pe.wait_ge(s_["V_ready"], t4 + 4)
                        for k in range(UT):
                            last = pe_t(b1[:, k * P:(k + 1) * P], QT[:, par, k])
                        last.then_inc(s_["Q_done"], 4)

                def pe_t(out, in_):
                    return nc.tensor.transpose(out, in_, R.ident[:])

                def keys_queries(n, s):
                    u, par = s % UT, s // UT
                    if u == 0:
                        pe.wait_ge(s_["KT_low"], n + 4)
                        pe.wait_ge(s_["Qs_high"], n + 4)
                        pe.wait_ge(s_["Qs_ready"], n + 4)
                    if past(n, 1):
                        pe.wait_ge(s_["M_ready"], n)
                    for k, (a, b) in enumerate(PARTS):
                        last = nc.tensor.matmul(bM[:], KTp[:, par, a, u], QTs[:, par, b, u].rearrange("p h t -> p (h t)"),
                                                start=(k == 0), stop=(k == len(PARTS) - 1))
                    last.then_inc(s_["M_done"], 1)

                def turn_and_U(n, s):
                    u, par = s % UT, s // UT
                    pe.wait_ge(s_["M_ready"], n + 1)
                    if past(n, 1):
                        pe.wait_ge(s_["BT_ready"], n)
                    for h in range(HG):
                        last = pe_t(bB[:, h * P:(h + 1) * P], M[:, s % 2, h])
                    last.then_inc(s_["B_done"], 1)
                    if u == 0:
                        pe.wait_ge(s_["Qg_ready"], n + 4)
                    pe.wait_ge(s_["AT_ready"], n + 1)
                    if past(n, 4):
                        pe.wait_ge(s_["S_ready"], 4 * (n - 3))
                    if past(n, 1):
                        pe.wait_ge(s_["U_ready"], n)
                    for h in range(HG):
                        nc.tensor.matmul(bU[h * DK:(h + 1) * DK, 0:P], K[:, par, u, h * DK:(h + 1) * DK], AT[:, s % 4, h],
                                         start=True, stop=False, tile_position=(0, h * DK))
                    nc.tensor.matmul(bU[:, 0:P], state[:, u, 0], QTg[:, par, u], start=False, stop=True).then_inc(s_["U_done"], 1)

                def products_of_U(n, s):
                    u, par = s % UT, s // UT
                    pe.wait_ge(s_["U_ready"], n + 1)
                    if past(n, 1):
                        pe.wait_ge(s_["PT_ready"], n)
                    for k, (a, b) in enumerate(PARTS):
                        last = nc.tensor.matmul(bP[:], QTp[:, par, a, u], Us[:, s % 2, b].rearrange("p h t -> p (h t)"),
                                                start=(k == 0), stop=(k == len(PARTS) - 1))
                    last.then_inc(s_["P_done"], 1)

                def values(n, s):
                    u, par = s % UT, s // UT
                    pe.wait_ge(s_["BT_ready"], n + 1)
                    if u == 0:
                        pe.wait_ge(s_["Kg_ready"], n + 4)
                    if past(n, 1):
                        pe.wait_ge(s_["W_ready"], n)
                    for h in range(HG):
                        nc.tensor.matmul(bW[h * DK:(h + 1) * DK, 0:P], V[:, par, u, h * DK:(h + 1) * DK], BT[:, h],
                                         start=True, stop=False, tile_position=(0, h * DK))
                    nc.tensor.matmul(bW[:, 0:P], state[:, u, 2], KTg[:, par, u], start=False, stop=True).then_inc(s_["WT_done"], 1)

                def turn_W(n, s):
                    pe.wait_ge(s_["WT_ready"], n + 1)
                    pe_t(bW[:, P:2 * P], WT[:, s % 2]).then_inc(s_["W_done"], 1)

                def outputs(n, s):
                    u, par = s % UT, s // UT
                    pe.wait_ge(s_["PT_ready"], n + 1)
                    pe.wait_ge(s_["W_ready"], n + 1)
                    if past(n, 1):
                        pe.wait_ge(s_["O_ready"], n)
                    for h in range(HG):
                        out = bS[h * DK:(h + 1) * DK, 3 * P:4 * P]
                        nc.tensor.matmul(out, V[:, par, u, h * DK:(h + 1) * DK], PT[:, s % 2, h],
                                         start=True, stop=False, tile_position=(0, h * DK))
                        nc.tensor.matmul(out, W[:, s % 2, h * DK:(h + 1) * DK], AT[:, s % 4, h],
                                         start=False, stop=False, tile_position=(0, h * DK))
                    nc.tensor.matmul(bS[:, 3 * P:4 * P], state[:, u, 2], Ug[:, s % 4], start=False, stop=False)
                    nc.tensor.matmul(bS[:, 3 * P:4 * P], state[:, u, 1], QTg[:, par, u], start=False, stop=True).then_inc(s_["O_done"], 1)
                    pe.wait_ge(s_["Ke_ready"], T(n, s) + 4)
                    pe.wait_ge(s_["Qe_ready"], T(n, s) + 4)
                    nc.tensor.matmul(bS[:, 0:P], Ke[:, par, u], K[:, par, u], start=True, stop=True)
                    nc.tensor.matmul(bS[:, P:2 * P], Ke[:, par, u], W[:, s % 2], start=True, stop=True)
                    nc.tensor.matmul(bS[:, 2 * P:3 * P], Qe[:, par, u], V[:, par, u], start=True, stop=True).then_inc(s_["S_done"], 1)

                def mix(n, s):
                    if s % UT != UT - 1:
                        return
                    pe.wait_ge(s_["O_ready"], n + 1)
                    if not isinstance(n, int) or n + 9 < NU:
                        pe.wait_ge(s_["xT_ready"], n + 13)
                    else:
                        pe.wait_ge(s_["K_ready"], NU)
                        pe.wait_ge(s_["x_ready"], n - 3)
                    for u in range(UT):
                        last = nc.tensor.matmul(b0[:, 0:HID], OT[:, s // UT, u], wo[:, u], start=(u == 0), stop=(u == UT - 1))
                    last.then_inc(s_["out_done"], 4)

                pe.wait_ge(s_["loaded"], 160)
                pe.wait_ge(s_["zeroed"], 3)
                skewed(pe, NU, [(7, turn_W), (5, turn_and_U), (4, keys_queries), (6, values), (6, products_of_U), (0, tile_part), (7, outputs), (9, mix)],
                       unroll=2 * UT)

            @block.scalar
            def _(act):
                std_of_var(nc, act, R, s_["var_ready"], s_["std_ready"])

                def flat(ap):
                    return ap.rearrange("p u t -> p (u t)")

                def copy_out(n, s):
                    act.wait_ge(s_["S_ready"], 4 * n + 4)
                    if past(n, 8):
                        act.wait_ge(s_["out_done"], n - s % UT - 4)
                    nc.scalar.copy(OT[:, s // UT, s % UT], bS[:, 3 * P:4 * P]).then_inc(s_["O_ready"], 1)

                def negate_W(n, s):
                    act.wait_ge(s_["W_done"], n + 1)
                    if past(n, 2):
                        act.wait_ge(s_["S_done"], n - 1)
                    nc.scalar.mul(W[:, s % 2], bW[:, P:2 * P], -1.0).then_inc(s_["W_ready"], 1)

                def copy_WT(n, s):
                    act.wait_ge(s_["WT_done"], n + 1)
                    nc.scalar.copy(WT[:, s % 2], bW[:, 0:P]).then_inc(s_["WT_ready"], 1)

                def copy_M(n, s):
                    act.wait_ge(s_["M_done"], n + 1)
                    if past(n, 2):
                        act.wait_ge(s_["B_done"], n - 1)
                        act.wait_ge(s_["AT_ready"], n - 1)
                    nc.scalar.copy(flat(M[:, s % 2]), bM[:]).then_inc(s_["M_ready"], 1)

                def tile_part(n, s):
                    u, par, t4 = s % UT, s // UT, n - s % UT
                    if u == 0:
                        act.wait_ge(s_["xT_done"], t4 + 4)
                        if past(n, 4):
                            act.wait_ge(s_["V_done"], t4)
                        nc.scalar.copy(xnT[:], b0[:, 0:HID]).then_inc(s_["xT_ready"], 4)
                    elif u == 1:
                        act.wait_ge(s_["QT_done"], t4 + 4)
                        if past(n, 8):
                            act.wait_ge(s_["Qg_ready"], t4 - 4)
                            act.wait_ge(s_["Kg_ready"], t4 - 4)
                            act.wait_ge(s_["Qs_ready"], t4 - 4)
                            act.wait_ge(s_["P_done"], t4 - 4)
                        nc.scalar.copy(flat(QTp[:, par, 0]), b1[:])
                        nc.scalar.copy(flat(QT[:, par]), b1[:]).then_inc(s_["QT_ready"], 4)
                        act.wait_ge(s_["KT_done"], t4 + 4)
                        nc.scalar.copy(flat(KTp[:, par, 0]), b0[:])
                        nc.scalar.copy(flat(KT[:, par]), b0[:]).then_inc(s_["KT_ready"], 4)
                    elif u == 2:
                        act.wait_ge(s_["QT_ready"], t4 + 4)
                        if past(n, 8):
                            act.wait_ge(s_["M_done"], t4 - 4)
                        for h in range(HG):
                            rows = slice(h * DK, (h + 1) * DK)
                            last = nc.scalar.copy(QTs[rows, par, 0, :, h, :], QTp[rows, par, 0].bitcast(F32))
                        last.then_inc(s_["Qs_high"], 4)
                        if past(n, 8):
                            act.wait_ge(s_["S_done"], t4 - 4)
                            act.wait_ge(s_["Ke_ready"], t4 - 4)
                        act.wait_ge(s_["V_done"], t4 + 4)
                        nc.scalar.copy(flat(V[:, par]), b1[:]).then_inc(s_["V_ready"], 4)
                        act.wait_ge(s_["K_done"], t4 + 4)
                        nc.scalar.copy(flat(K[:, par]), b0[:]).then_inc(s_["K_ready"], 4)

                def spread_U(n, s):
                    act.wait_ge(s_["U_done"], n + 1)
                    if past(n, 2):
                        act.wait_ge(s_["P_done"], n - 1)
                    for h in range(HG):
                        rows = slice(h * DK, (h + 1) * DK)
                        last = nc.scalar.copy(Us[rows, s % 2, 0, h], bU[rows, 0:P])
                    last.then_inc(s_["U_high"], 1)

                act.wait_ge(s_["loaded"], 160)
                act.wait_ge(s_["zeroed"], 3)
                skewed(act, NU, [(8, copy_out), (7, negate_W), (4, copy_M), (5, spread_U), (6, copy_WT), (0, tile_part)], unroll=2 * UT)

            @block.vector
            def _(dve):
                nc.vector.memset(QTs[:].bitcast(F32), 0.0).then_inc(s_["zeroed"], 1)
                nc.vector.memset(Us[:].bitcast(F32), 0.0).then_inc(s_["zeroed"], 1)
                nc.vector.memset(state[:], 0.0).then_inc(s_["zeroed"], 1)
                layernorm_scales(nc, dve, None, R, s_["step"], s_["var_ready"], s_["std_ready"])
                dve.wait_ge(s_["loaded"], 160)

                def spread4(ap):
                    return ap[:, None, :].broadcast_to([P, HG, P])

                def normalize(n, s):
                    if s % UT:
                        return
                    tile = n // UT
                    if past(n, 4):
                        dve.wait_ge(s_["xT_done"], n)
                    nc.vector.tensor_scalar(xn[:], row_of(R.X, tile), R.rstd[:, bass.ds(tile, 1)], R.shift[:, bass.ds(tile, 1)],
                                            ALU.mult, ALU.add).then_inc(s_["xn_ready"], 4)

                def update(n, s):
                    tile = (n - s % UT) // UT
                    dve.wait_ge(s_["S_done"], n + 1)
                    for h in range(HG):
                        rows, cols = slice(h * DK, (h + 1) * DK), slice(h * DK, (h + 1) * DK)
                        old = state[rows, s % UT, :, cols]
                        new = bS[rows, 0:3 * P].rearrange("p (m t) -> p m t", m=3)[:, :, cols]
                        nc.vector.scalar_tensor_tensor(out=old, in0=old, scalar=decay[rows, bass.ds(tile, 1)], in1=new,
                                                       op0=ALU.mult, op1=ALU.add).then_inc(s_["S_ready"], 1)

                def mask_P(n, s):
                    dve.wait_ge(s_["P_done"], n + 1)
                    if past(n, 2):
                        dve.wait_ge(s_["O_done"], n - 1)
                    nc.vector.tensor_tensor(PT[:, s % 2], bP[:].rearrange("p (h t) -> p h t", h=HG), spread4(upper[:]), ALU.mult
                                            ).then_inc(s_["PT_ready"], 1)

                def mask_B(n, s):
                    dve.wait_ge(s_["B_done"], n + 1)
                    if past(n, 1):
                        dve.wait_ge(s_["WT_done"], n)
                    nc.vector.tensor_tensor(BT[:], bB[:].rearrange("p (h t) -> p h t", h=HG), spread4(lower[:]), ALU.mult
                                            ).then_inc(s_["BT_ready"], 1)

                def spread_U(n, s):
                    dve.wait_ge(s_["U_high"], n + 1)
                    if past(n, 4):
                        dve.wait_ge(s_["O_done"], n - 3)
                    for h in range(HG):
                        rows = slice(h * DK, (h + 1) * DK)
                        nc.vector.tensor_tensor(Us[rows, s % 2, 1, h], bU[rows, 0:P], Us[rows, s % 2, 0, h].bitcast(F32), ALU.subtract)
                    nc.vector.tensor_tensor(Ug[:, s % 4], bU[:, 0:P], decay_t[:], ALU.mult).then_inc(s_["U_ready"], 1)

                def tile_part(n, s):
                    u, par, t4 = s % UT, s // UT, n - s % UT
                    if u == 1:
                        dve.wait_ge(s_["QT_ready"], t4 + 4)
                        nc.vector.tensor_tensor(QTp[:, par, 1], QT[:, par], QTp[:, par, 0].bitcast(F32), ALU.subtract).then_inc(s_["QT_low"], 4)
                        if past(n, 8):
                            dve.wait_ge(s_["M_done"], t4 - 4)
                        dve.wait_ge(s_["QT_low"], t4 + 4)
                        for h in range(HG):
                            rows = slice(h * DK, (h + 1) * DK)
                            nc.vector.tensor_copy(QTs[rows, par, 1, :, h, :], QTp[rows, par, 1].bitcast(F32)).then_inc(s_["Qs_ready"], 1)
                    elif u == 2:
                        dve.wait_ge(s_["KT_ready"], t4 + 4)
                        nc.vector.tensor_tensor(KTp[:, par, 1], KT[:, par], KTp[:, par, 0].bitcast(F32), ALU.subtract).then_inc(s_["KT_low"], 4)
                        dve.wait_ge(s_["K_ready"], t4 + 4)
                        if past(n, 8):
                            dve.wait_ge(s_["S_done"], t4 - 4)
                        nc.vector.tensor_scalar(Ke[:, par], K[:, par], to_end[:, bass.ds(t4 // UT, 1)], None, ALU.mult).then_inc(s_["Ke_ready"], 4)
                    elif u == 3:
                        dve.wait_ge(s_["Q_done"], t4 + 4)
                        if past(n, 8):
                            dve.wait_ge(s_["S_done"], t4 - 4)
                        nc.vector.tensor_scalar(Qe[:, par].rearrange("p u t -> p (u t)"), b1[:], to_end[:, bass.ds(t4 // UT, 1)], None,
                                                ALU.mult).then_inc(s_["Qe_ready"], 4)

                def residual(n, s):
                    if s % UT != UT - 1:
                        return
                    tile = (n - s % UT) // UT
                    dve.wait_ge(s_["out_done"], n + 1)
                    nc.vector.tensor_tensor(row_of(R.X, tile), row_of(R.X, tile), b0[:, 0:HID], ALU.add).then_inc(s_["x_ready"], 4)

                def stats(n, s):
                    if s % UT != UT - 1:
                        return
                    tile = (n - s % UT) // UT
                    dve.wait_ge(s_["x_ready"], n + 1)
                    nc.vector.bn_stats(row_of(R.raw, tile), row_of(R.X, tile))

                skewed(dve, NU, [(0, normalize), (8, update), (5, mask_B), (5, spread_U), (6, mask_P), (1, tile_part), (9, residual), (10, stats)],
                       unroll=2 * UT)

            @block.gpsimd
            def _(pool):
                pool.wait_ge(s_["loaded"], 160)

                def mask_M(n, s):
                    pool.wait_ge(s_["M_ready"], n + 1)
                    if past(n, 4):
                        pool.wait_ge(s_["O_done"], n - 3)
                    nc.gpsimd.tensor_tensor(AT[:, s % 4], M[:, s % 2], upper[:, None, :].broadcast_to([P, HG, P]), ALU.mult
                                            ).then_inc(s_["AT_ready"], 1)

                def tile_part(n, s):
                    if s % UT != 1:
                        return
                    par, t4 = s // UT, n - 1
                    pool.wait_ge(s_["QT_ready"], t4 + 4)
                    if past(n, 8):
                        pool.wait_ge(s_["O_done"], t4 - 4)
                    for to, of, done in ((QTg, QT, "Qg_ready"), (KTg, KT, "Kg_ready")):
                        if of is KT:
                            pool.wait_ge(s_["KT_ready"], t4 + 4)
                        nc.gpsimd.tensor_tensor(to[:, par], of[:, par], decay_t[:, None, :].broadcast_to([P, UT, P]), ALU.mult
                                                ).then_inc(s_[done], 4)

                skewed(pool, NU, [(4, mask_M), (1, tile_part)], unroll=2 * UT)


def window_attention(nc, R, A, C):
    H, D, WIN = 16, 16, 128
    SPAN = 2 * WIN
    PADDED = SEQ + WIN
    PAIRS = H // 2
    NU = NT * PAIRS
    qT_dram = nc.dram_tensor("qT_dram", (BATCH * TB, HID, P), F32).ap()
    kT_dram = nc.dram_tensor("kT_dram", (BATCH, HID, PADDED), F32).ap()
    v_dram = nc.dram_tensor("v_dram", (BATCH, PADDED, HID), F32).ap()
    with Stage(nc, "wa") as st:
        woT = st.sb("woT", [P, HC, HID])
        bank = [st.ps(f"bank{i}") for i in range(8)]

        with Stage(nc, "wp") as p:
            wT = p.sb("wT", [P, HC, 3 * HID])
            bqk, bv_all, zeros = p.sb("bqk", [P, 4]), p.sb("bv_all", [P, HID]), p.sb("zeros", [P, BATCH, HID])
            xn, xnT = p.sb("xn", [P, 2, HID]), p.sb("xnT", [P, 2, HID])
            qk, v = p.sb("qk", [P, 4, 4, P]), p.sb("v", [P, 4, HID])
            names = "loaded zeroed padded step var_ready std_ready xn_ready xT_done xT_ready qk_done v_done qk_ready v_ready".split()
            loaded, zeroed, padded, step, var_ready, std_ready, xn_ready, xT_done, xT_ready, qk_done, v_done, qk_ready, v_ready = (
                p.sem(n) for n in names)
            stored = [p.sem(f"stored{n}") for n in range(4)]
            turned_copies(nc, R, "ww", [(A["L1_attn_b_Wqkv"], wT[:]), (A["L1_attn_b_Wout"], woT[:])], bank[6:8])
            with nc.Block() as block:
                @block.sync
                def _(sp):
                    sp.dma_start(bqk[:], A["L1_attn_b_bqkv"][0:2 * HID].rearrange("(c p) -> p c", p=P),
                                 allow_slow_non_contiguous=True).then_inc(loaded, 16)
                    sp.dma_start(bv_all[:], A["L1_attn_b_bqkv"][2 * HID:3 * HID].rearrange("(a d) -> a d", a=1).broadcast_to([P, HID])
                                 ).then_inc(loaded, 16)
                    sp.wait_ge(zeroed, 1)
                    for side in (0, PADDED - WIN // 2):
                        edge = slice(side, side + WIN // 2)
                        for c in range(HC):
                            sp.dma_start(kT_dram[:, c * P:(c + 1) * P, edge].rearrange("b p t -> p b t"), zeros[:, :, 0:WIN // 2]
                                         ).then_inc(padded, 16)
                        sp.dma_start(v_dram[:, edge, :].rearrange("b t d -> t b d"), zeros[0:WIN // 2]).then_inc(padded, 16)

                    def store(b, j, s):
                        n = b * TB + j
                        at = bass.ds(j * P + WIN // 2, P)
                        sp.wait_ge(qk_ready, n + 1)
                        sp.dma_start(qT_dram[bass.ds(n, 1)].rearrange("a (c p) t -> p (a c) t", p=P), qk[:, s, 0:2]).then_inc(stored[s], 16)
                        sp.dma_start(kT_dram[bass.ds(b, 1), :, at].rearrange("a (c p) t -> p (a c) t", p=P), qk[:, s, 2:4]).then_inc(stored[s], 16)
                        sp.wait_ge(v_ready, n + 1)
                        sp.dma_start(v_dram[bass.ds(b, 1), at, :].rearrange("a t d -> (a t) d"), v[:, s]).then_inc(stored[s], 16)

                    with sp.Fori(0, BATCH) as b:
                        for j in range(TB):
                            store(b, j, j % 4)
                    sp.wait_ge(padded, 96)
                    for n in range(4):
                        sp.wait_ge(stored[n], 48 * NT // 4)

                @block.tensor
                def _(pe):
                    def turn_x(i, s):
                        s %= 2
                        pe.wait_ge(xn_ready, i + 1)
                        if past(i, 2):
                            pe.wait_ge(xT_ready, i - 1)
                        for c in range(HC):
                            last = nc.tensor.transpose(bank[s][:, c * P:(c + 1) * P], xn[:, s, c * P:(c + 1) * P], R.ident[:])
                        last.then_inc(xT_done, 1)

                    def project(i, s):
                        s %= 2
                        pe.wait_ge(xT_ready, i + 1)
                        if past(i, 2):
                            pe.wait_ge(qk_ready, i - 1)
                            pe.wait_ge(v_ready, i - 1)
                        for e in range(4):
                            for c in range(HC):
                                last = nc.tensor.matmul(bank[2 + s][:, e * P:(e + 1) * P], wT[:, c, e * P:(e + 1) * P],
                                                        xnT[:, s, c * P:(c + 1) * P], start=(c == 0), stop=(c == HC - 1))
                        last.then_inc(qk_done, 1)
                        for c in range(HC):
                            last = nc.tensor.matmul(bank[4 + s][:, 0:HID], xnT[:, s, c * P:(c + 1) * P], wT[:, c, 2 * HID:3 * HID],
                                                    start=(c == 0), stop=(c == HC - 1))
                        last.then_inc(v_done, 1)

                    skewed(pe, NT, [(0, turn_x), (2, project)], unroll=4)

                @block.scalar
                def _(act):
                    std_of_var(nc, act, R, var_ready, std_ready)

                    def copy_xT(i, s):
                        s %= 2
                        act.wait_ge(xT_done, i + 1)
                        if past(i, 2):
                            act.wait_ge(v_done, i - 1)
                        nc.scalar.copy(xnT[:, s], bank[s][:, 0:HID]).then_inc(xT_ready, 1)

                    skewed(act, NT, [(0, copy_xT)], unroll=4)

                @block.vector
                def _(dve):
                    nc.vector.memset(zeros[:], 0.0).then_inc(zeroed, 1)
                    layernorm_scales(nc, dve, None, R, step, var_ready, std_ready)
                    dve.wait_ge(loaded, 32)

                    def normalize(i, s):
                        s %= 2
                        if past(i, 2):
                            dve.wait_ge(xT_done, i - 1)
                        nc.vector.tensor_scalar(xn[:, s], row_of(R.X, i), R.rstd[:, bass.ds(i, 1)], R.shift[:, bass.ds(i, 1)],
                                                ALU.mult, ALU.add).then_inc(xn_ready, 1)

                    def add_bias(i, s):
                        if past(i, 4):
                            dve.wait_ge(stored[s], 12 * (i - s))
                        dve.wait_ge(qk_done, i + 1)
                        nc.vector.tensor_tensor(qk[:, s], bank[2 + s % 2][:].rearrange("p (e t) -> p e t", e=4),
                                                bqk[:, :, None].broadcast_to([P, 4, P]), ALU.add).then_inc(qk_ready, 1)
                        dve.wait_ge(v_done, i + 1)
                        nc.vector.tensor_tensor(v[:, s], bank[4 + s % 2][:, 0:HID], bv_all[:], ALU.add).then_inc(v_ready, 1)

                    skewed(dve, NT, [(0, normalize), (3, add_bias)], unroll=4)

        with Stage(nc, "wq") as q:
            sb, sem = q.sb, q.sem
            KTw, Vw, QTw = sb("KTw", [P, 2, HC, SPAN]), sb("Vw", [P, 2, 2, HID]), sb("QTw", [P, 2, HC, P])
            QTs = sb("QTs", [P, 2, H, P])
            band, head, bo_all = sb("band", [P, SPAN]), sb("head", [P, PAIRS]), sb("bo_all", [P, HID])
            S, prob, probT = sb("S", [P, 4, 2, SPAN]), sb("prob", [P, 4, 2, SPAN]), sb("probT", [P, 4, 2, 2, P])
            top, shift, sums, share = sb("top", [P, 4, 2]), sb("shift", [P, 4, 2]), sb("sums", [P, 2, H]), sb("share", [P, 2, H])
            OT2, O, OT, y = sb("OT2", [P, 4, P]), sb("O", [P, HID]), sb("OT", [P, HID]), sb("y", [P, 2, HID])
            bS, bT, bO, bU, bV = bank[0:2], bank[2:4], bank[4:6], bank[6], bank[7]
            names = """loaded S_done top_ready shift_ready prob_ready T_done T_copied T3_copied PV_done Qs_ready OT2_ready back_done share_ready O_ready
                       turn_done OT_ready out_done y_ready x_ready""".split()
            s_ = {n: sem(n) for n in names}
            k_in, v_in, q_in = ([sem(f"{what}_in{n}") for n in range(2)] for what in "kvq")
            U = 2 * PAIRS

            def wait_for_copy(eng, n, s):
                if s % 4 == 3:
                    eng.wait_ge(s_["T3_copied"], n + 1)
                else:
                    eng.wait_ge(s_["T_copied"], n + 1 + (s % 4 == 2))

            with nc.Block() as block:
                @block.sync
                def _(sp):
                    sp.dma_start(band[:], C["band"]).then_inc(s_["loaded"], 16)
                    sp.dma_start(head[:], C["head16"]).then_inc(s_["loaded"], 16)
                    sp.dma_start(bo_all[:], A["L1_attn_b_bout"].rearrange("(a d) -> a d", a=1).broadcast_to([P, HID])).then_inc(s_["loaded"], 16)

                    def load(b, j, s, waits):
                        i = b * TB + j
                        if waits:
                            sp.wait_ge(s_["Qs_ready"], PAIRS * (i - 1))
                            sp.wait_ge(s_["S_done"], PAIRS * (i - 1))
                        sp.dma_start(QTw[:, s], qT_dram[bass.ds(i, 1)].rearrange("a (c p) t -> p (a c) t", p=P)).then_inc(q_in[s], 16)
                        sp.dma_start(KTw[:, s], kT_dram[bass.ds(b, 1), :, bass.ds(j * P, SPAN)].rearrange("a (c p) t -> p (a c) t", p=P)
                                     ).then_inc(k_in[s], 16)
                        if waits:
                            sp.wait_ge(s_["PV_done"], PAIRS * (i - 1))
                        sp.dma_start(Vw[:, s], v_dram[bass.ds(b, 1), bass.ds(j * P, SPAN), :].rearrange("a (k p) d -> p (a k) d", p=P)
                                     ).then_inc(v_in[s], 16)

                    for j in range(TB):
                        load(0, j, j % 2, j >= 2)
                    with sp.Fori(1, BATCH) as b:
                        for j in range(TB):
                            load(b, j, j % 2, True)

                @block.gpsimd
                def _(pool):
                    pool.wait_ge(s_["loaded"], 48)

                    def spread(i, s):
                        pool.wait_ge(q_in[s], 8 * (i - s) + 16)
                        if past(i, 2):
                            pool.wait_ge(s_["S_done"], PAIRS * (i - 1))
                        for c in range(HC):
                            nc.gpsimd.tensor_tensor(QTs[:, s, PAIRS * c:PAIRS * (c + 1)], QTw[:, s, c:c + 1, :].broadcast_to([P, PAIRS, P]),
                                                    head[:, :, None].broadcast_to([P, PAIRS, P]), ALU.mult).then_inc(s_["Qs_ready"], PAIRS // 2)

                    def residual(i, s):
                        pool.wait_ge(s_["y_ready"], PAIRS * (i + 1))
                        nc.gpsimd.tensor_tensor(row_of(R.X, i), row_of(R.X, i), y[:, s], ALU.add).then_inc(s_["x_ready"], PAIRS)

                    skewed(pool, NT, [(0, spread), (2, residual)])

                @block.tensor
                def _(pe):
                    pe.wait_ge(s_["loaded"], 48)

                    def scores(n, s):
                        m, par = s % PAIRS, s // PAIRS
                        if m == 0:
                            pe.wait_ge(k_in[par], (n - s) + 16)
                            pe.wait_ge(s_["Qs_ready"], n + PAIRS)
                        if past(n, 2):
                            pe.wait_ge(s_["top_ready"], n - 1)
                        for h in range(2):
                            last = nc.tensor.matmul(bS[s % 2][:, h * SPAN:(h + 1) * SPAN], QTs[:, par, 2 * m + h, :], KTw[:, par, m // 4, :],
                                                    start=True, stop=True)
                        last.then_inc(s_["S_done"], 1)

                    def turn(n, s):
                        pe.wait_ge(s_["prob_ready"], 2 * n + 2)
                        if past(n, 2):
                            wait_for_copy(pe, n - 2, s - 2)
                        for h in range(2):
                            for k in range(2):
                                last = nc.tensor.transpose(bT[s % 2][:, (2 * h + k) * P:(2 * h + k + 1) * P],
                                                           prob[:, s % 4, h, k * P:(k + 1) * P], R.ident[:])
                        last.then_inc(s_["T_done"], 1)

                    def weigh(n, s):
                        m, par = s % PAIRS, s // PAIRS
                        wait_for_copy(pe, n, s)
                        if m == 0:
                            pe.wait_ge(v_in[par], (n - s) + 16)
                            if past(n, U):
                                pe.wait_ge(s_["OT2_ready"], n - PAIRS)
                        rows = slice(32 * (m % 4), 32 * (m % 4) + 32)
                        for h in range(2):
                            for k in range(2):
                                cols = (2 * (m // 4) + h) * P
                                last = nc.tensor.matmul(bO[par][rows, cols:cols + P], Vw[:, par, k, 32 * m:32 * m + 32],
                                                        probT[:, s % 4, h, k, :], start=(k == 0), stop=(k == 1),
                                                        tile_position=(0, 32 * (m % 4)))
                        last.then_inc(s_["PV_done"], 1)

                    def last_of_tile(f):
                        def run(n, s):
                            if s % PAIRS == PAIRS - 1:
                                f(n + 1 - PAIRS, s // PAIRS)
                        return run

                    def back(i, par):
                        pe.wait_ge(s_["OT2_ready"], i + PAIRS)
                        if past(i, 1):
                            pe.wait_ge(s_["O_ready"], i)
                        for k in range(4):
                            last = nc.tensor.transpose(bU[:, k * P:(k + 1) * P], OT2[:, k, :], R.ident[:])
                        last.then_inc(s_["back_done"], PAIRS)

                    def turn_O(i, par):
                        pe.wait_ge(s_["O_ready"], i + PAIRS)
                        if past(i, 1):
                            pe.wait_ge(s_["y_ready"], i)
                        for c in range(HC):
                            last = nc.tensor.transpose(bV[:, c * P:(c + 1) * P], O[:, c * P:(c + 1) * P], R.ident[:])
                        last.then_inc(s_["turn_done"], PAIRS)

                    def mix(i, par):
                        pe.wait_ge(s_["OT_ready"], i + PAIRS)
                        for c in range(HC):
                            last = nc.tensor.matmul(bV[:, HID:2 * HID], OT[:, c * P:(c + 1) * P], woT[:, c, :], start=(c == 0), stop=(c == HC - 1))
                        last.then_inc(s_["out_done"], PAIRS)

                    skewed(pe, NU, [(0, scores), (6, weigh), (3, turn), (8, last_of_tile(back)), (10, last_of_tile(turn_O)),
                                    (12, last_of_tile(mix))], unroll=U)

                @block.scalar
                def _(act):
                    def exponent(n, s):
                        m, par = s % PAIRS, s // PAIRS
                        act.wait_ge(s_["shift_ready"], n + 1)
                        if past(n, 4):
                            act.wait_ge(s_["T_done"], n - 3)
                        if m == 0 and past(n, U):
                            act.wait_ge(s_["share_ready"], n - PAIRS)
                        for h in range(2):
                            nc.scalar.activation(prob[:, s % 4, h], S[:, s % 4, h], ACT.Exp, bias=shift[:, s % 4, h:h + 1], scale=D ** -0.5,
                                                 accum_out=sums[:, par, 2 * m + h:2 * m + h + 1]).then_inc(s_["prob_ready"], 1)

                    def copy_T(n, s):
                        if s % 4 != 3:
                            return
                        act.wait_ge(s_["T_done"], n + 1)
                        if past(n, 4):
                            act.wait_ge(s_["PV_done"], n - 3)
                        nc.scalar.copy(probT[:, 3].rearrange("p h k t -> p (h k t)"), bT[1][:]).then_inc(s_["T3_copied"], 4)

                    def copy_O(n, s):
                        if s % PAIRS == PAIRS - 1:
                            act.wait_ge(s_["PV_done"], n + 1)
                            if past(n, PAIRS):
                                act.wait_ge(s_["back_done"], n + 1 - PAIRS)
                            nc.scalar.copy(OT2[:].rearrange("p k t -> p (k t)"), bO[s // PAIRS][:]).then_inc(s_["OT2_ready"], PAIRS)

                    def copy_OT(n, s):
                        if s % PAIRS == PAIRS - 1:
                            act.wait_ge(s_["turn_done"], n + 1)
                            if past(n, PAIRS):
                                act.wait_ge(s_["out_done"], n + 1 - PAIRS)
                            nc.scalar.copy(OT[:], bV[:, 0:HID]).then_inc(s_["OT_ready"], PAIRS)

                    skewed(act, NU, [(4, copy_T), (7, copy_O), (11, copy_OT), (0, exponent)], unroll=U)

                @block.vector
                def _(dve):
                    dve.wait_ge(s_["loaded"], 48)

                    def mask(n, s):
                        dve.wait_ge(s_["S_done"], n + 1)
                        if past(n, 4):
                            dve.wait_ge(s_["prob_ready"], 2 * (n - 3))
                        nc.vector.memset(R.turnstile[:], 0.0)
                        for h in range(2):
                            ins = nc.vector.tensor_tensor_reduce(out=S[:, s % 4, h], in0=bS[s % 2][:, h * SPAN:(h + 1) * SPAN], in1=band[:],
                                                                 scale=1.0, scalar=-3e38, op0=ALU.add, op1=ALU.max,
                                                                 accum_out=top[:, s % 4, h:h + 1])
                        ins.then_inc(s_["top_ready"], 1)
                        dve.wait_ge(s_["top_ready"], n + 1)
                        nc.vector.tensor_scalar(shift[:, s % 4], top[:, s % 4], -(D ** -0.5), None, ALU.mult).then_inc(s_["shift_ready"], 1)

                    def copy_T(n, s):
                        if s % 4 == 3:
                            return
                        dve.wait_ge(s_["T_done"], n + 1)
                        if past(n, 4):
                            dve.wait_ge(s_["PV_done"], n - 3)
                        nc.vector.tensor_copy(probT[:, s % 4].rearrange("p h k t -> p (h k t)"), bT[s % 2][:]
                                              ).then_inc(s_["T_copied"], 2 if s % 4 == 2 else 1)

                    def shares(n, s):
                        if s % PAIRS != PAIRS - 1:
                            return
                        dve.wait_ge(s_["prob_ready"], 2 * n + 2)
                        if past(n, U):
                            dve.wait_ge(s_["O_ready"], n + 1 - U)
                        nc.vector.reciprocal(share[:, s // PAIRS], sums[:, s // PAIRS]).then_inc(s_["share_ready"], PAIRS)

                    def normalize(n, s):
                        if s % PAIRS != PAIRS - 1:
                            return
                        par = s // PAIRS
                        dve.wait_ge(s_["share_ready"], n + 1)
                        dve.wait_ge(s_["back_done"], n + 1)
                        if past(n, PAIRS):
                            dve.wait_ge(s_["turn_done"], n + 1 - PAIRS)
                        for h in range(2):
                            nc.vector.tensor_tensor(
                                O[:].rearrange("p (c m h d) -> p c m h d", c=2, m=4, h=2)[:, :, :, h, :],
                                bU[:].rearrange("p (c g m h d) -> p c g m h d", c=2, g=2, m=4, h=2)[:, :, h, :, h, :],
                                share[:, par].rearrange("p (c m h) -> p c m h", c=2, m=4)[:, :, :, h, None].broadcast_to([P, 2, 4, D]),
                                ALU.mult).then_inc(s_["O_ready"], PAIRS // 2)

                    def add_bias(n, s):
                        if s % PAIRS != PAIRS - 1:
                            return
                        par = s // PAIRS
                        dve.wait_ge(s_["out_done"], n + 1)
                        if past(n, U):
                            dve.wait_ge(s_["x_ready"], n + 1 - U)
                        nc.vector.tensor_tensor(y[:, par], bV[:, HID:2 * HID], bo_all[:], ALU.add).then_inc(s_["y_ready"], PAIRS)

                    def stats(n, s):
                        if s % PAIRS != PAIRS - 1:
                            return
                        i = (n - PAIRS + 1) // PAIRS
                        dve.wait_ge(s_["x_ready"], n + 1)
                        nc.vector.bn_stats(row_of(R.raw, i), row_of(R.X, i))

                    skewed(dve, NU, [(4, copy_T), (9, normalize), (13, add_bias), (0, mask), (3, shares), (15, stats)], unroll=U)


def local_attention(nc, R, A, C, sem_):
    def sem(name):
        return sem_(f"la_{name}")

    with ExitStack() as ctx:
        def sb(name, shape, dt=F32):
            return ctx.enter_context(nc.sbuf_tensor(f"la_{name}", shape, dt))

        def ps(name, shape, dt=F32):
            return ctx.enter_context(nc.psum_tensor(f"la_{name}", shape, dt))

        w = sb("w", [P, 3, HC, HID])
        wT = sb("wT", [P, 3, HC, HID])
        bqk = sb("bqk", [P, 4])
        bv_all = sb("bv_all", [P, HID])
        mask = sb("mask", [P, P])
        xn = sb("xn", [P, 2, HID])
        xnT = sb("xnT", [P, 2, HID])
        qkT = sb("qkT", [P, 2, 4, P])
        v = sb("v", [P, 4, HID])
        S = sb("S", [P, 4, P])
        prob = sb("prob", [P, 4, P])
        probT = sb("probT", [P, 4, P])
        top, total, share = sb("top", [P, 8]), sb("total", [P, 4]), sb("share", [P, 4])
        ps_xT = ps("ps_xT", [P, 2 * HID])
        ps_qk = [ps(f"ps_qk{i}", [P, 4, P]) for i in range(2)]
        ps_v = ps("ps_v", [P, 2 * HID])
        ps_S = ps("ps_S", [P, 4, P])
        ps_pT = ps("ps_pT", [P, 4, P])
        ps_o = [ps(f"ps_o{i}", [P, 2 * HID]) for i in range(2)]

        loaded, w_turned, w_ready = sem("loaded"), sem("w_turned"), sem("w_ready")
        step, var_ready, std_ready = sem("step"), sem("var_ready"), sem("std_ready")
        xn_ready, xT_done, xT_ready = sem("xn_ready"), sem("xT_done"), sem("xT_ready")
        qk_done, v_done, qk_ready, v_ready = sem("qk_done"), sem("v_done"), sem("qk_ready"), sem("v_ready")
        S_done, masked, top_ready, prob_ready = sem("S_done"), sem("masked"), sem("top_ready"), sem("prob_ready")
        pT_done, pT_ready, o_done = sem("pT_done"), sem("pT_ready"), sem("o_done")
        share_ready, x_ready, stats_done = sem("share_ready"), sem("x_ready"), sem("stats_done")

        with nc.Block() as block:
            @block.sync
            def _(sp):
                for n, name in enumerate("qkv"):
                    sp.dma_start(w[:, n], A[f"L0_attn_a_W{name}"].rearrange("(c p) d -> p c d", p=P)).then_inc(loaded, 16)
                for n, name in enumerate("qk"):
                    sp.dma_start(bqk[:, 2 * n:2 * n + 2], A[f"L0_attn_a_b{name}"].rearrange("(c p) -> p c", p=P),
                                 allow_slow_non_contiguous=True).then_inc(loaded, 16)
                sp.dma_start(bv_all[:], A["L0_attn_a_bv"].rearrange("(a d) -> a d", a=1).broadcast_to([P, HID])).then_inc(loaded, 16)
                sp.dma_start(mask[:], C["group_mask"]).then_inc(loaded, 16)

            @block.tensor
            def _(pe):
                pe.wait_ge(loaded, 7 * 16)
                for n in range(3):
                    if n == 2:
                        pe.wait_ge(w_ready, 1)
                    for c in range(HC):
                        for h in range(HC):
                            last = nc.tensor.transpose(ps_qk[n % 2][:, 2 * h + c, :], w[:, n, c, h * P:(h + 1) * P], R.ident[:])
                    last.then_inc(w_turned, 1)
                pe.wait_ge(w_ready, 3)

                def turn_x(i, s):
                    s %= 2
                    pe.wait_ge(xn_ready, i + 1)
                    if past(i, 1):
                        pe.wait_ge(xT_ready, i)
                    for c in range(HC):
                        last = nc.tensor.transpose(ps_xT[:, c * P:(c + 1) * P], xn[:, s, c * P:(c + 1) * P], R.ident[:])
                    last.then_inc(xT_done, 1)

                def project(i, s):
                    s %= 2
                    pe.wait_ge(xT_ready, i + 1)
                    if past(i, 2):
                        pe.wait_ge(qk_ready, i - 1)
                    for n in range(2):
                        for e in range(HC):
                            for c in range(HC):
                                last = nc.tensor.matmul(ps_qk[s][:, 2 * n + e, :], wT[:, n, c, e * P:(e + 1) * P],
                                                        xnT[:, s, c * P:(c + 1) * P], start=(c == 0), stop=(c == HC - 1))
                    last.then_inc(qk_done, 1)
                    if past(i, 1):
                        pe.wait_ge(v_ready, i)
                    for c in range(HC):
                        last = nc.tensor.matmul(ps_v[:, 0:HID], xnT[:, s, c * P:(c + 1) * P], wT[:, 2, c, :],
                                                start=(c == 0), stop=(c == HC - 1))
                    last.then_inc(v_done, 1)

                def scores(i, s):
                    s %= 2
                    pe.wait_ge(qk_ready, i + 1)
                    if past(i, 1):
                        pe.wait_ge(masked, i)
                    for e in range(HC):
                        last = nc.tensor.matmul(ps_S[:, 0, :], qkT[:, s, e, :], qkT[:, s, 2 + e, :],
                                                start=(e == 0), stop=(e == HC - 1))
                    last.then_inc(S_done, 1)

                def turn_p(i, s):
                    pe.wait_ge(prob_ready, i + 1)
                    if past(i, 1):
                        pe.wait_ge(pT_ready, i)
                    nc.tensor.transpose(ps_pT[:, 0, :], prob[:, s, :], R.ident[:]).then_inc(pT_done, 1)

                def weigh(i, s):
                    pe.wait_ge(pT_ready, i + 1)
                    pe.wait_ge(v_ready, i + 1)
                    if past(i, 2):
                        pe.wait_ge(x_ready, i - 1)
                    nc.tensor.matmul(ps_o[s % 2][:, 0:HID], probT[:, s, :], v[:, s, :], start=True, stop=True).then_inc(o_done, 1)

                skewed(pe, NT, [(5, weigh), (4, turn_p), (3, scores), (0, turn_x), (1, project)], unroll=4)

            @block.scalar
            def _(act):
                std_of_var(nc, act, R, var_ready, std_ready)
                for n in range(3):
                    act.wait_ge(w_turned, n + 1)
                    nc.scalar.copy(wT[:, n].rearrange("p c d -> p (c d)"), ps_qk[n % 2][:].rearrange("p a b -> p (a b)")).then_inc(w_ready, 1)

                def copy_xT(i, s):
                    s %= 2
                    act.wait_ge(xT_done, i + 1)
                    if past(i, 2):
                        act.wait_ge(v_done, i - 1)
                    nc.scalar.copy(xnT[:, s], ps_xT[:, 0:HID]).then_inc(xT_ready, 1)

                def exponent(i, s):
                    act.wait_ge(top_ready, i + 1)
                    if past(i, 4):
                        act.wait_ge(pT_done, i - 3)
                        act.wait_ge(x_ready, i - 3)
                    nc.scalar.activation(prob[:, s], S[:, s], ACT.Exp, bias=top[:, s + 4:s + 5],
                                         accum_out=total[:, s:s + 1]).then_inc(prob_ready, 1)

                def copy_pT(i, s):
                    act.wait_ge(pT_done, i + 1)
                    if past(i, 4):
                        act.wait_ge(o_done, i - 3)
                    nc.scalar.copy(probT[:, s], ps_pT[:, 0]).then_inc(pT_ready, 1)

                skewed(act, NT, [(0, copy_xT), (4, copy_pT), (3, exponent)], unroll=4)

            @block.vector
            def _(dve):
                layernorm_scales(nc, dve, None, R, step, var_ready, std_ready)
                dve.wait_ge(loaded, 7 * 16)

                def normalize(i, s):
                    s %= 2
                    if past(i, 2):
                        dve.wait_ge(xT_done, i - 1)
                    nc.vector.tensor_scalar(xn[:, s], row_of(R.X, i), R.rstd[:, bass.ds(i, 1)], R.shift[:, bass.ds(i, 1)],
                                            ALU.mult, ALU.add).then_inc(xn_ready, 1)

                def copy_qk(i, s):
                    s %= 2
                    dve.wait_ge(qk_done, i + 1)
                    if past(i, 2):
                        dve.wait_ge(S_done, i - 1)
                    nc.vector.tensor_tensor(qkT[:, s], ps_qk[s][:], bqk[:, :, None].broadcast_to([P, 4, P]), ALU.add).then_inc(qk_ready, 1)

                def copy_v(i, s):
                    dve.wait_ge(v_done, i + 1)
                    if past(i, 4):
                        dve.wait_ge(o_done, i - 3)
                    nc.vector.tensor_tensor(v[:, s], ps_v[:, 0:HID], bv_all[:], ALU.add).then_inc(v_ready, 1)

                def mask_S(i, s):
                    dve.wait_ge(S_done, i + 1)
                    if past(i, 4):
                        dve.wait_ge(prob_ready, i - 3)
                    nc.vector.memset(R.turnstile[:], 0.0)
                    nc.vector.tensor_tensor_reduce(out=S[:, s], in0=ps_S[:, 0], in1=mask[:], scale=1.0, scalar=-3e38,
                                                   op0=ALU.add, op1=ALU.max, accum_out=top[:, s:s + 1]).then_inc(masked, 1)
                    dve.wait_ge(masked, i + 1)
                    nc.vector.tensor_scalar(top[:, s + 4:s + 5], top[:, s:s + 1], -1.0, None, ALU.mult).then_inc(top_ready, 1)

                def residual(i, s):
                    dve.wait_ge(prob_ready, i + 1)
                    nc.vector.reciprocal(share[:, s:s + 1], total[:, s:s + 1]).then_inc(share_ready, 1)
                    dve.wait_ge(o_done, i + 1)
                    dve.wait_ge(share_ready, i + 1)
                    nc.vector.scalar_tensor_tensor(out=row_of(R.X, i), in0=ps_o[s % 2][:, 0:HID], scalar=share[:, s:s + 1],
                                                   in1=row_of(R.X, i), op0=ALU.mult, op1=ALU.add).then_inc(x_ready, 1)

                def stats(i, s):
                    dve.wait_ge(x_ready, i + 1)
                    nc.vector.bn_stats(row_of(R.raw, i), row_of(R.X, i))

                skewed(dve, NT, [(0, normalize), (5, residual), (3, mask_S), (1, copy_qk), (1, copy_v), (7, stats)], unroll=4)


class Resident:
    pass


def hybrid_kernel(nc, A, C, out):
    with ExitStack() as ctx:
        def sem(name):
            return ctx.enter_context(nc.semaphore(name))

        def sb(name, shape, dt=F32):
            return ctx.enter_context(nc.sbuf_tensor(name, shape, dt))

        R = Resident()
        R.fetched = [sem(f"fetched{n}") for n in range(4)]
        R.scattered = [sem(f"scattered{b}") for b in range(BATCH)]
        R.X = sb("X", [P, NT, HID])
        R.raw = sb("raw", [P, NT, 6])
        R.mean, R.var, R.rstd = sb("mean", [P, NT]), sb("var", [P, NT]), sb("rstd", [P, NT])
        R.shift, R.diff = sb("shift", [P, NT]), sb("diff", [P, NT])
        R.ident = sb("ident", [P, P])
        R.turnstile = sb("turnstile", [1, 1])
        made = sem("ident_made")
        with nc.Block() as block:
            @block.gpsimd
            def _(pool):
                nc.gpsimd.memset(R.ident[:], 0.0).then_inc(made, 1)
                pool.wait_ge(made, 1)
                nc.gpsimd.affine_select(out=R.ident[:], in_=R.ident[:], compare_op=ALU.not_equal, fill=1.0,
                                        base=0, pattern=[[-1, P]], channel_multiplier=1)
        R.xn_dram = nc.dram_tensor("xn_dram", (BATCH * SEQ, HID), F32).ap()
        R.sum_dram = nc.dram_tensor("sum_dram", (BATCH * SEQ, HID), F32).ap()
        R.gate_dram = nc.dram_tensor("gate_dram", (P, HID), F32).ap()
        reload_x(nc, R, "in", A["L0_attn_a_x"].rearrange("b s d -> (b s) d"))
        local_attention(nc, R, A, C, sem)
        top_k_experts(nc, R, "m2", A, C, 0)
        spectral_attention(nc, R, A, C)
        top_k_experts(nc, R, "m4", A, C, 1)
        second_order_attention(nc, R, A, C)
        tanh_ffn(nc, R, "t6", sem, A["L1_ffn_weight"], A["L1_ffn_aux_weight1"], A["L1_ffn_aux_weight2"], A["L1_ffn_bias"])
        window_attention(nc, R, A, C)
        tanh_ffn(nc, R, "t8", sem, A["L1_ffn_weight"], A["L1_ffn_aux_weight1"], A["L1_ffn_aux_weight2"], A["L1_ffn_bias"], out)


def shape_constants():
    token = np.arange(P)
    same = (token[:, None] // 64) == (token[None, :] // 64)
    n, f = np.arange(64), np.arange(33)
    angle = 2 * np.pi * (np.outer(n, f) % 64) / 64
    cos, sin = np.cos(angle), np.sin(angle)
    sin[:, [0, 32]] = 0.0
    forward = np.concatenate([cos, -sin], axis=1)
    dft = np.kron(np.eye(2), forward)
    twice = np.where((f == 0) | (f == 32), 1.0, 2.0)[:, None] / 64
    inv = [cos.T * twice, -sin.T * twice]
    inv_high = np.zeros((P, P))
    for r in range(2):
        for h in range(2):
            inv_high[64 * r + 29 * h:64 * r + 29 * (h + 1), 64 * h:64 * (h + 1)] = inv[r][4:]
    inv_low = np.zeros((P, TB, P))
    for r in range(2):
        for chunk in range(16):
            inv_low[64 * r + 4 * chunk:64 * r + 4 * chunk + 4, chunk // 2, 64 * (chunk % 2):64 * (chunk % 2) + 64] = inv[r][:4]
    low_pass = np.kron(np.eye(2), -(forward[:, :4] @ inv[0][:4] + forward[:, 33:37] @ inv[1][:4]))
    chunk = np.arange(64) // 4
    chunk_mask = np.tile(np.where(chunk[:, None] >= chunk[None, :], 0.0, -1e30), (2, 1))
    gamma, place = 0.99, np.arange(P)
    power = gamma ** (place[None, :] - place[:, None]).astype(np.float64)
    last = (np.arange(NT) % TB == TB - 1)[None, :]
    ahead = np.arange(2 * P)[None, :] - place[:, None]
    return {
        "band": np.where((ahead >= 0) & (ahead < P), 0.0, -1e30).astype(np.float32),
        "head16": (place[:, None] // 16 == np.arange(8)[None, :]).astype(np.float32),
        "upper": np.triu(power).astype(np.float32),
        "lower": np.triu(power, 1).astype(np.float32),
        "decay_t": np.tile(gamma ** (place + 1.0), (P, 1)).astype(np.float32),
        "to_end": np.where(last, 0.0, gamma ** (P - 1.0 - place)[:, None]).astype(np.float32),
        "decay": np.tile(np.where(last, 0.0, gamma ** P), (P, 1)).astype(np.float32),
        "head": (place[:, None] // 32 == np.arange(4)[None, :]).astype(np.float32),
        "dft": dft.astype(np.float32),
        "inv_high": inv_high.astype(np.float32),
        "inv_low": inv_low.astype(np.float32),
        "low_pass": low_pass.astype(np.float32),
        "chunk_mask": chunk_mask.astype(np.float32),
        "row_base": (np.arange(64) // 8 * SEQ).astype(np.float32)[:, None],
        "group_mask": np.where(same, 0.0, -1e30).astype(np.float32),
    }


_INS = ['L0_attn_a_x', 'L0_attn_a_Wq', 'L0_attn_a_bq', 'L0_attn_a_Wk', 'L0_attn_a_bk', 'L0_attn_a_Wv', 'L0_attn_a_bv',
        'L0_attn_b_q_w', 'L0_attn_b_k_w', 'L0_attn_b_v_w', 'L0_attn_b_o_w', 'L0_attn_b_dw_r', 'L0_attn_b_pw_r',
        'L0_attn_b_dw_i', 'L0_attn_b_pw_i', 'L0_attn_b_gate_w', 'L0_attn_b_alpha_raw', 'L0_ffn_Wg', 'L0_ffn_W1',
        'L0_ffn_b1', 'L0_ffn_W2', 'L0_ffn_b2', 'L1_attn_a_Wq', 'L1_attn_a_Wk', 'L1_attn_a_Wv', 'L1_attn_a_Wo',
        'L1_attn_b_Wqkv', 'L1_attn_b_bqkv', 'L1_attn_b_Wout', 'L1_attn_b_bout', 'L1_ffn_weight',
        'L1_ffn_aux_weight1', 'L1_ffn_aux_weight2', 'L1_ffn_bias']


def kernel(**inputs):
    import numpy as _np
    import concourse.bacc as _bacc
    from concourse import mybir as _mybir
    from concourse.bass_utils import run_bass_kernel_spmd as _run

    nc = _bacc.Bacc("TRN2", target_bir_lowering=False, num_devices=1)
    arrays, args = {}, {}
    for name in _INS:
        a = _np.ascontiguousarray(inputs[name])
        arrays[f"in_{name}_dram"] = a
        args[name] = nc.dram_tensor(f"in_{name}_dram", a.shape, _mybir.dt.from_np(a.dtype), kind="ExternalInput").ap()
    out = nc.dram_tensor("out_0_dram", (BATCH, SEQ, HID), _mybir.dt.float32, kind="ExternalOutput").ap()
    constants = {}
    for name, a in shape_constants().items():
        arrays[f"in_{name}_dram"] = a
        constants[name] = nc.dram_tensor(f"in_{name}_dram", a.shape, _mybir.dt.from_np(a.dtype), kind="ExternalInput").ap()
    hybrid_kernel(nc, args, constants, out)
    r = _run(nc, [arrays], core_ids=[0])
    return r.results[0]["out_0_dram"]
```
